# Optimizing a Trainium2 kernel written in Bass

```python
import numpy as np
import jax
import jax.numpy as jnp

def _softmax(x, axis=-1):
    return jax.nn.softmax(x, axis=axis)

def _gelu(x):
    return jax.nn.gelu(x, approximate=True)

def _silu(x):
    return jax.nn.silu(x)

def _sigmoid(x):
    return jax.nn.sigmoid(x)

def _layernorm(x, axis=-1, eps=1e-05):
    m = jnp.mean(x, axis=axis, keepdims=True)
    v = jnp.var(x, axis=axis, keepdims=True)
    return (x - m) / jnp.sqrt(v + eps)

def _scatter_add(tgt, idx, src, axis=0):
    return tgt.at[idx].add(src)

def _segment_sum(src, seg, n):
    return jax.ops.segment_sum(src, seg, n)
kernel_name = 'mk_xattn_ffn_d2_seqx_r8_6373bc'

def setup_inputs(seed: int=0):
    np.random.seed(seed)
    _w = jnp.asarray

    def _rec_inputs():
        import jax
        import jax.numpy as jnp
        _rk = jax.random.key(seed)
        x = 7.22e-05 + 1 * jax.random.normal(jax.random.fold_in(_rk, 1), (64, 64, 128), jnp.float32)
        _lenS = 64 - jax.random.randint(jax.random.fold_in(_rk, 7), (64,), 0, max(1, 64 // 4) + 1, jnp.int32)
        _lenS2 = 64 - jax.random.randint(jax.random.fold_in(_rk, 8), (64,), 0, max(1, 64 // 4) + 1, jnp.int32)
        _ctx_1024P = jax.random.normal(jax.random.fold_in(_rk, 11), (64, 16, 128), jnp.float32)
        _ctx_1024c = jax.random.dirichlet(jax.random.fold_in(_rk, 511), 0.3 * jnp.ones((16,), jnp.float32), (64, 64))
        _ctx_1024t = jnp.einsum('bsk,bkd->bsd', _ctx_1024c, _ctx_1024P)
        _ctx_1024t = _ctx_1024t * jax.lax.rsqrt(jnp.mean(jnp.square(_ctx_1024t)) + 1e-12) * 0.953939
        ctx_1024 = 4.13588e-05 + 0.999923 * (_ctx_1024t + 0.3 * jax.random.normal(jax.random.fold_in(_rk, 611), (64, 64, 128), jnp.float32))
        _validS = jnp.arange(64)[None, :] < _lenS[:, None]
        _validS2 = jnp.arange(64)[None, :] < _lenS2[:, None]
        _causal = jnp.tril(jnp.ones((64, 64), dtype=bool))
        mask_BxS2_ff0 = jnp.where(jnp.ones((64, 64), dtype=bool), 0.0, -1000000000.0).astype(jnp.float32)
        return (x, ctx_1024, mask_BxS2_ff0)
    x, ctx_1024, mask_BxS2_ff0 = _rec_inputs()

    def _L0_xattn_setup():
        import jax, jax.numpy as jnp
        import numpy as np
        B, S, D, H = (4, 256, 128, 16)
        DK = D // H
        WINDOW = 32
        GLOBAL = 16
        NEG_INF = float(np.finfo(np.float32).min)

        def local_window_mask(seq_len, window, global_tokens):
            i = jnp.arange(seq_len)[:, None]
            j = jnp.arange(seq_len)[None, :]
            is_global = (i < global_tokens) | (j < global_tokens)
            out_of_window = jnp.abs(i - j) > window
            return jnp.where(out_of_window & ~is_global, NEG_INF, 0.0).astype(jnp.float32)
        key = jax.random.key(seed)
        ks = jax.random.split(key, 8)
        std = 1.0 / np.sqrt(D)
        return {'q': jax.random.normal(ks[0], (B, S, D), jnp.float32), 'k': jax.random.normal(ks[1], (B, S, D), jnp.float32), 'v': jax.random.normal(ks[2], (B, S, D), jnp.float32), 'attn_mask': jnp.zeros((B, S), jnp.float32), 'wq': jax.random.normal(ks[3], (D, D), jnp.float32) * std, 'bq': jnp.zeros((D,), jnp.float32), 'wk': jax.random.normal(ks[4], (D, D), jnp.float32) * std, 'bk': jnp.zeros((D,), jnp.float32), 'wv': jax.random.normal(ks[5], (D, D), jnp.float32) * std, 'bv': jnp.zeros((D,), jnp.float32), 'wo': jax.random.normal(ks[6], (D, D), jnp.float32) * std, 'bo': jnp.zeros((D,), jnp.float32)}
    _L0_xattn_all = _L0_xattn_setup()
    _L0_xattn_in = {k: v for k, v in _L0_xattn_all.items() if k in ('wq', 'bq', 'wk', 'bk', 'wv', 'bv', 'wo', 'bo')}
    del _L0_xattn_all

    def _L0_ffn_setup():
        import jax, jax.numpy as jnp
        import numpy as np
        from jax import lax
        DIM = 128
        INTER = 64
        N_EXPERTS = 16
        TOPK = 4
        ROUTE_SCALE = 2.5
        VOCAB = 4000

        def _silu_and_mul(gu):
            gate, up = jnp.split(gu, 2, axis=-1)
            return jax.nn.silu(gate) * up
        key = jax.random.key(seed)
        ks = jax.random.split(key, 8)
        x = jax.random.normal(ks[0], (2, 64, DIM), dtype=jnp.float32)
        input_ids = jax.random.randint(ks[1], (2, 64), 0, VOCAB)
        s = 0.02
        gate_w = jax.random.normal(ks[2], (N_EXPERTS, DIM), dtype=jnp.float32) * s
        gate_b = jax.random.normal(ks[3], (N_EXPERTS,), dtype=jnp.float32) * s
        w13 = jax.random.normal(ks[4], (N_EXPERTS, 2 * INTER, DIM), dtype=jnp.float32) * s
        w2 = jax.random.normal(ks[5], (N_EXPERTS, DIM, INTER), dtype=jnp.float32) * s
        w13_s = jax.random.normal(ks[6], (2 * INTER, DIM), dtype=jnp.float32) * s
        w2_s = jax.random.normal(ks[7], (DIM, INTER), dtype=jnp.float32) * s
        return {'x': x, 'input_ids': input_ids, 'gate_w': gate_w, 'gate_b': gate_b, 'w13': w13, 'w2': w2, 'w13_s': w13_s, 'w2_s': w2_s}
    _L0_ffn_all = _L0_ffn_setup()
    _L0_ffn_in = {k: v for k, v in _L0_ffn_all.items() if k in ('input_ids', 'gate_w', 'gate_b', 'w13', 'w2', 'w13_s', 'w2_s')}
    del _L0_ffn_all

    def _L1_xattn_setup():
        import jax, jax.numpy as jnp
        import numpy as np
        import math
        D = 128
        H = 8
        HD = D // H
        TEMP = math.sqrt(D)
        EPS = 1e-05

        def _layernorm(x, g, b):
            mu = jnp.mean(x, axis=-1, keepdims=True)
            var = jnp.var(x, axis=-1, keepdims=True)
            return (x - mu) * jax.lax.rsqrt(var + EPS) * g + b
        key = jax.random.key(seed)
        ks = jax.random.split(key, 8)
        B, Lq, Lk = (4, 256, 256)
        Q = jax.random.normal(ks[0], (B, Lq, D), dtype=jnp.float32)
        K = jax.random.normal(ks[1], (B, Lk, D), dtype=jnp.float32)
        V = jax.random.normal(ks[2], (B, Lk, D), dtype=jnp.float32)
        Wq = jax.random.normal(ks[3], (D, D), dtype=jnp.float32) * 0.02
        Wk = jax.random.normal(ks[4], (D, D), dtype=jnp.float32) * 0.02
        Wv = jax.random.normal(ks[5], (D, D), dtype=jnp.float32) * 0.02
        Wo = jax.random.normal(ks[6], (D, D), dtype=jnp.float32) * 0.02
        pre_g = jnp.ones((D,), jnp.float32)
        pre_b = jnp.zeros((D,), jnp.float32)
        ln_g = jnp.ones((D,), jnp.float32)
        ln_b = jnp.zeros((D,), jnp.float32)
        return {'Q': Q, 'K': K, 'V': V, 'Wq': Wq, 'Wk': Wk, 'Wv': Wv, 'Wo': Wo, 'pre_g': pre_g, 'pre_b': pre_b, 'ln_g': ln_g, 'ln_b': ln_b}
    _L1_xattn_all = _L1_xattn_setup()
    _L1_xattn_in = {k: v for k, v in _L1_xattn_all.items() if k in ('Wq', 'Wk', 'Wv', 'Wo', 'pre_g', 'pre_b', 'ln_g', 'ln_b')}
    del _L1_xattn_all

    def _L1_ffn_setup():
        import jax, jax.numpy as jnp
        import numpy as np
        DIM, E, K, H = (128, 8, 2, 512)
        key = jax.random.key(seed)
        ks = jax.random.split(key, 5)
        s_in = 1.0 / np.sqrt(DIM)
        s_h = 1.0 / np.sqrt(H)
        return {'x': jax.random.normal(ks[0], (4, 256, DIM), dtype=jnp.float32), 'Wr': jax.random.normal(ks[1], (DIM, E), dtype=jnp.float32) * s_in, 'W1': jax.random.normal(ks[2], (E, DIM, H), dtype=jnp.float32) * s_in, 'b1': jnp.zeros((E, H), dtype=jnp.float32), 'W2': jax.random.normal(ks[3], (E, H, DIM), dtype=jnp.float32) * s_h, 'b2': jnp.zeros((E, DIM), dtype=jnp.float32)}
    _L1_ffn_all = _L1_ffn_setup()
    _L1_ffn_in = {k: v for k, v in _L1_ffn_all.items() if k in ('Wr', 'W1', 'b1', 'W2', 'b2')}
    del _L1_ffn_all
    return {'x': x, 'ctx_1024': ctx_1024, 'mask_BxS2_ff0': mask_BxS2_ff0, 'L0_xattn_wq': _L0_xattn_in['wq'], 'L0_xattn_bq': _L0_xattn_in['bq'], 'L0_xattn_wk': _L0_xattn_in['wk'], 'L0_xattn_bk': _L0_xattn_in['bk'], 'L0_xattn_wv': _L0_xattn_in['wv'], 'L0_xattn_bv': _L0_xattn_in['bv'], 'L0_xattn_wo': _L0_xattn_in['wo'], 'L0_xattn_bo': _L0_xattn_in['bo'], 'L0_ffn_input_ids': _L0_ffn_in['input_ids'], 'L0_ffn_gate_w': _L0_ffn_in['gate_w'], 'L0_ffn_gate_b': _L0_ffn_in['gate_b'], 'L0_ffn_w13': _L0_ffn_in['w13'], 'L0_ffn_w2': _L0_ffn_in['w2'], 'L0_ffn_w13_s': _L0_ffn_in['w13_s'], 'L0_ffn_w2_s': _L0_ffn_in['w2_s'], 'L1_xattn_Wq': _L1_xattn_in['Wq'], 'L1_xattn_Wk': _L1_xattn_in['Wk'], 'L1_xattn_Wv': _L1_xattn_in['Wv'], 'L1_xattn_Wo': _L1_xattn_in['Wo'], 'L1_xattn_pre_g': _L1_xattn_in['pre_g'], 'L1_xattn_pre_b': _L1_xattn_in['pre_b'], 'L1_xattn_ln_g': _L1_xattn_in['ln_g'], 'L1_xattn_ln_b': _L1_xattn_in['ln_b'], 'L1_ffn_Wr': _L1_ffn_in['Wr'], 'L1_ffn_W1': _L1_ffn_in['W1'], 'L1_ffn_b1': _L1_ffn_in['b1'], 'L1_ffn_W2': _L1_ffn_in['W2'], 'L1_ffn_b2': _L1_ffn_in['b2']}

def reference(x, ctx_1024, mask_BxS2_ff0, L0_xattn_wq, L0_xattn_bq, L0_xattn_wk, L0_xattn_bk, L0_xattn_wv, L0_xattn_bv, L0_xattn_wo, L0_xattn_bo, L0_ffn_input_ids, L0_ffn_gate_w, L0_ffn_gate_b, L0_ffn_w13, L0_ffn_w2, L0_ffn_w13_s, L0_ffn_w2_s, L1_xattn_Wq, L1_xattn_Wk, L1_xattn_Wv, L1_xattn_Wo, L1_xattn_pre_g, L1_xattn_pre_b, L1_xattn_ln_g, L1_xattn_ln_b, L1_ffn_Wr, L1_ffn_W1, L1_ffn_b1, L1_ffn_W2, L1_ffn_b2):
    import jax
    import jax.numpy as jnp

    def _L0_xattn_ref(q, k, v, attn_mask, wq, bq, wk, bk, wv, bv, wo, bo):
        import jax, jax.numpy as jnp
        import numpy as np
        B, S, D, H = (4, 256, 128, 16)
        DK = D // H
        WINDOW = 32
        GLOBAL = 16
        NEG_INF = float(np.finfo(np.float32).min)

        def local_window_mask(seq_len, window, global_tokens):
            i = jnp.arange(seq_len)[:, None]
            j = jnp.arange(seq_len)[None, :]
            is_global = (i < global_tokens) | (j < global_tokens)
            out_of_window = jnp.abs(i - j) > window
            return jnp.where(out_of_window & ~is_global, NEG_INF, 0.0).astype(jnp.float32)
        b, s, d = q.shape
        Q = (q @ wq + bq).reshape(b, s, H, DK).transpose(0, 2, 1, 3)
        K = (k @ wk + bk).reshape(b, s, H, DK).transpose(0, 2, 1, 3)
        V = (v @ wv + bv).reshape(b, s, H, DK).transpose(0, 2, 1, 3)
        scale = 1.0 / np.sqrt(DK)
        scores = jnp.einsum('bhqd,bhkd->bhqk', Q, K) * scale
        scores = scores + attn_mask[:, None, None, :]
        scores = scores + local_window_mask(s, WINDOW, GLOBAL)[None, None, :, :]
        probs = jax.nn.softmax(scores, axis=-1)
        out = jnp.einsum('bhqk,bhkd->bhqd', probs, V)
        out = out.transpose(0, 2, 1, 3).reshape(b, s, d)
        return out @ wo + bo

    def _L0_ffn_ref(x, input_ids, gate_w, gate_b, w13, w2, w13_s, w2_s):
        import jax, jax.numpy as jnp
        import numpy as np
        from jax import lax
        DIM = 128
        INTER = 64
        N_EXPERTS = 16
        TOPK = 4
        ROUTE_SCALE = 2.5
        VOCAB = 4000

        def _silu_and_mul(gu):
            gate, up = jnp.split(gu, 2, axis=-1)
            return jax.nn.silu(gate) * up
        B, S, D = x.shape
        xt = x.reshape(-1, D)
        T = xt.shape[0]
        scores = jax.nn.sigmoid(xt.astype(jnp.float32) @ gate_w.T)
        biased = scores + gate_b
        _, idx = lax.top_k(biased, TOPK)
        w = jnp.take_along_axis(scores, idx, axis=-1)
        w = w / jnp.sum(w, axis=-1, keepdims=True)
        w = w * ROUTE_SCALE
        comb = jnp.zeros((T, N_EXPERTS), jnp.float32)
        comb = comb.at[jnp.arange(T)[:, None], idx].add(w)
        comb = comb.astype(x.dtype)

        def expert_body(y, args):
            w13_e, w2_e, c_e = args
            h = _silu_and_mul(xt @ w13_e.T)
            return (y + c_e[:, None] * (h @ w2_e.T), None)
        y, _ = lax.scan(expert_body, jnp.zeros_like(xt), (w13, w2, comb.T))
        y = y + _silu_and_mul(xt @ w13_s.T) @ w2_s.T
        return y.astype(x.dtype).reshape(B, S, D)

    def _L1_xattn_ref(Q, K, V, Wq, Wk, Wv, Wo, pre_g, pre_b, ln_g, ln_b):
        import jax, jax.numpy as jnp
        import numpy as np
        import math
        D = 128
        H = 8
        HD = D // H
        TEMP = math.sqrt(D)
        EPS = 1e-05

        def _layernorm(x, g, b):
            mu = jnp.mean(x, axis=-1, keepdims=True)
            var = jnp.var(x, axis=-1, keepdims=True)
            return (x - mu) * jax.lax.rsqrt(var + EPS) * g + b
        B, Lq, _ = Q.shape
        Lk = K.shape[1]
        Qn = _layernorm(Q, pre_g, pre_b)
        Kn = _layernorm(K, pre_g, pre_b)
        q = (Qn @ Wq).reshape(B, Lq, H, HD)
        k = (Kn @ Wk).reshape(B, Lk, H, HD)
        v = (V @ Wv).reshape(B, Lk, H, HD)
        scores = jnp.einsum('bqhd,bkhd->bhqk', q, k) / TEMP
        scores = jnp.clip(scores, -10000.0, 10000.0)
        A = jax.nn.softmax(scores, axis=-1)
        O = jnp.einsum('bhqk,bkhd->bqhd', A, v).reshape(B, Lq, D)
        O = _layernorm(O, ln_g, ln_b)
        O = O + jax.nn.gelu(O @ Wo, approximate=False)
        return O

    def _L1_ffn_ref(x, Wr, W1, b1, W2, b2):
        import jax, jax.numpy as jnp
        import numpy as np
        DIM, E, K, H = (128, 8, 2, 512)
        batch, seq, dim = x.shape
        x_flat = x.reshape(-1, dim)
        logits = x_flat @ Wr
        w, ind = jax.lax.top_k(logits, K)
        w = jax.nn.softmax(w, axis=-1)
        combine = jnp.einsum('tke,tk->te', jax.nn.one_hot(ind, E, dtype=x.dtype), w)

        def body(acc, params):
            W1e, b1e, W2e, b2e, ce = params
            h = jax.nn.gelu(x_flat @ W1e + b1e, approximate=False)
            y = h @ W2e + b2e
            return (acc + ce[:, None] * y, None)
        out0 = jnp.zeros_like(x_flat)
        out, _ = jax.lax.scan(body, out0, (W1, b1, W2, b2, combine.T))
        return out.reshape(batch, seq, dim)
    x = x + _L0_xattn_ref(_layernorm(x, axis=-1), ctx_1024, ctx_1024, mask_BxS2_ff0, L0_xattn_wq, L0_xattn_bq, L0_xattn_wk, L0_xattn_bk, L0_xattn_wv, L0_xattn_bv, L0_xattn_wo, L0_xattn_bo)
    x = x + _L0_ffn_ref(_layernorm(x, axis=-1), L0_ffn_input_ids, L0_ffn_gate_w, L0_ffn_gate_b, L0_ffn_w13, L0_ffn_w2, L0_ffn_w13_s, L0_ffn_w2_s)
    x = x + _L1_xattn_ref(_layernorm(x, axis=-1), ctx_1024, ctx_1024, L1_xattn_Wq, L1_xattn_Wk, L1_xattn_Wv, L1_xattn_Wo, L1_xattn_pre_g, L1_xattn_pre_b, L1_xattn_ln_g, L1_xattn_ln_b)
    x = x + _L1_ffn_ref(_layernorm(x, axis=-1), L1_ffn_Wr, L1_ffn_W1, L1_ffn_b1, L1_ffn_W2, L1_ffn_b2)
    return x

_drawn_inputs = setup_inputs


def setup_inputs(seed=0):
    import zlib

    import numpy as np

    out = dict(_drawn_inputs(seed))
    spreads = {'L0_xattn_bq': (0.0, 0.1),
     'L0_xattn_bk': (0.0, 2.0),
     'L0_xattn_bv': (0.0, 0.1),
     'L0_xattn_bo': (0.0, 0.1),
     'L1_xattn_pre_g': (1.0, 0.6),
     'L1_xattn_pre_b': (0.0, 0.8),
     'L1_xattn_ln_g': (1.0, 0.2),
     'L1_xattn_ln_b': (0.0, 0.1),
     'L1_ffn_b1': (0.0, 0.315),
     'L1_ffn_b2': (0.0, 0.1)}
    factors = {'L0_ffn_gate_w': 4.897,
     'L0_ffn_gate_b': 6.193,
     'L0_ffn_w13': 4.904,
     'L0_ffn_w2': 4.615,
     'L0_ffn_w13_s': 5.518,
     'L0_ffn_w2_s': 4.751,
     'L1_xattn_Wq': 4.061,
     'L1_xattn_Wk': 3.68}
    for name, (base, spread) in spreads.items():
        noise = np.random.default_rng([zlib.crc32(name.encode()), seed]).standard_normal(out[name].shape)
        drawn = base * np.exp(spread * noise) if base else spread * noise
        out[name] = jnp.asarray(drawn.astype(out[name].dtype))
    for name, factor in factors.items():
        out[name] = (out[name] * factor).astype(out[name].dtype)
    return out
```

```python
from contextlib import ExitStack

import concourse.bass as bass
from concourse import mybir
import numpy as np

F32 = mybir.dt.float32
BF16 = mybir.dt.bfloat16
I32 = mybir.dt.int32
U32 = mybir.dt.uint32
ALU = mybir.AluOpType
ACT = mybir.ActivationFunctionType
AX = mybir.AxisListType

P = 128
D = 128
B, S = 64, 64
TOK = B * S
NT = TOK // P
GT = 4
NG = NT // GT
GTOK = GT * P
EPS = 1e-5
NEWTON = 3
ROOT_STEPS = 3 + 3 * NEWTON

H0, H1 = 16, 8
WINDOW, GLOBAL = 32, 16
RANKS = S - WINDOW - 1 - GLOBAL
NEG = -3.3895313892515355e38
MROW = 32
MROWS = MROW + 3

E0, K0, INTER = 16, 4, 64
ROUTE_SCALE = 2.5
PAIRS = E0 // 2
ITEMS = PAIRS + 1

E1, HID = 8, 512
CH = HID // P
ST = 256
NST = TOK * 2 // ST + E1 - 1
NSLOT = NST * ST
WPACK = HID + HID + CH + D


def constants():
    p = np.arange(P)
    dk0, dk1 = D // H0, D // H1
    head0 = (p[:, None] % 32) // dk0 == np.arange(32 // dk0)[None, :]
    head1 = (p[:, None] % 32) // dk1 == np.arange(32 // dk1)[None, :]
    s = np.arange(S)
    u = np.zeros((MROWS, S), np.float32)
    v = np.zeros((MROW, S), np.float32)
    for r in range(RANKS):
        u[r] = s >= GLOBAL + WINDOW + 1 + r
        v[r] = NEG * (s == GLOBAL + r)
        u[RANKS + r] = s == GLOBAL + r
        v[RANKS + r] = NEG * (s >= GLOBAL + WINDOW + 1 + r)
    u[MROW:] = 1.0
    sel3 = np.zeros((3, E0, PAIRS, 2, INTER), np.float32)
    for e in range(E0):
        sel3[:, e, e // 2, e % 2] = 1.0
    reset0 = np.ones((P, NT, E0), np.float32)
    reset0[:, :, 0] = 0.0
    reset1 = np.ones((P, NT, E1), np.float32)
    reset1[:, :, 0] = 0.0
    reset_t = np.ones((P, E1, NT), np.float32)
    reset_t[:, :, 0] = 0.0
    return {
        "c_ident": np.eye(P, dtype=np.float32),
        "c_head0": head0.astype(np.float32) * np.float32(dk0 ** -0.5),
        "c_head1": head1.astype(np.float32) * np.float32(D ** -0.5),
        "c_win_u": np.concatenate([u, u], 1),
        "c_win_v": v,
        "c_sel3": sel3.reshape(3 * E0, PAIRS * P),
        "c_before": (p[:, None] < p[None, :]).astype(np.float32),
        "c_reset0": reset0.reshape(P, NT * E0),
        "c_reset1": reset1.reshape(P, NT * E1),
        "c_reset_t": reset_t.reshape(P, E1 * NT),
        "c_steps": np.broadcast_to(ST * np.arange(TOK // ST, dtype=np.float32), (P, TOK // ST)).copy(),
        "c_tile": np.arange(NST, dtype=np.float32)[None, :].copy(),
    }


class Att:

    def __init__(self, layer):
        self.layer = layer
        self.heads = H0 if layer == 0 else H1
        self.hl = self.heads // 4
        self.dk = D // self.heads
        self.units = 8 if layer == 0 else 4

    def slot(self, u, c):
        return (u // 2, 2 * c) if self.layer == 0 else (2 * (u // 2) + c, 0)


def need(eng, sem, value):
    if isinstance(value, int) and value <= 0:
        return
    eng.wait_ge(sem, value)


def bodies(eng, body, count):
    body(-1, 1, False, False, True)
    body(0, 0, False, True, True)
    with eng.Fori(0, (count - 2) // 2) as i:
        body(2 * i + 1, 1, True, True, True)
        body(2 * i + 2, 0, True, True, True)
    for g in range(1 + 2 * ((count - 2) // 2), count - 1):
        body(g, g % 2, True, True, True)
    body(count - 1, (count - 1) % 2, True, True, False)
    body(count, count % 2, True, False, False)


def sixteens(k, parity):
    return 8 * (k + 2 - parity)


def span(start, size):
    return slice(start, start + size) if isinstance(start, int) else bass.ds(start, size)


def program(nc, d, out, stop=9):
    with ExitStack() as ctx:
        def sb(name, shape, dt=F32):
            return ctx.enter_context(nc.sbuf_tensor(name, shape, dt))

        def sem(name):
            return ctx.enter_context(nc.semaphore(name))

        PS = ctx.enter_context(nc.psum_tensor("PS", [P, 8, 512], F32))
        X = sb("X", [P, NT, D])
        CN = sb("CN", [P, NT, D])
        XNT = sb("XNT", [P, TOK])
        X2T = sb("X2T", [P, TOK])
        KNT = sb("KNT", [P, TOK])
        ctg = sb("ctg", [P, GTOK])
        rows48 = sb("rows48", [3 * E0, TOK], BF16)
        mask_rows = rows48[0:MROWS, :]
        combT = rows48
        Qz = sb("Qz", [P, 2, 8, 4, S])
        KTb = sb("KTb", [P, 2, GTOK])
        Vz = [sb(f"Vz{l}", [P, 2, GT, hl * (P + D // (4 * hl))]) for l, hl in enumerate((4, 2))]
        Pr = sb("Pr", [P, 4, 512])
        PT = sb("PT", [P, 2, 512])
        OTs = sb("OTs", [P, GTOK])
        mx = sb("mx", [P, 2, 8])
        sums = sb("sums", [P, 2, 8])
        rsum = sb("rsum", [P, 2, 8])
        xn = sb("xn", [P, GT, D])
        xm = sb("xm", [P, GT, D])
        xnT = sb("xnT", [P, GTOK])
        stats = sb("stats", [P, GT, 6])
        mv = sb("mv", [P, GT, 2])
        rstd = sb("rstd", [P, GT])
        var_eps = sb("var_eps", [P, GT])
        root_t = sb("root_t", [P, GT])
        LG = sb("LG", [P, NT, E0])
        w_att = [sb(f"w_att{l}", [P, 4, D]) for l in range(2)]
        cols = sb("cols", [P, 8])
        bq_h = sb("bq_h", [P, 4])
        bo_row = sb("bo_row", [1, D])
        ones_row = sb("ones_row", [1, P])
        ident = sb("ident", [P, P])
        identb = sb("identb", [P, P], BF16)
        head0 = sb("head0", [P, 4])
        head1 = sb("head1", [P, 2])
        win_u = sb("win_u", [MROWS, P])
        win_ub = sb("win_ub", [MROWS, P], BF16)
        win_v = sb("win_v", [MROW, S])
        mask_in = sb("mask_in", [B, S])
        mask_left = sb("mask_left", [B, S])
        mask_part = sb("mask_part", [B, 3, S], BF16)
        gw = sb("gw", [P, E0])
        gb = sb("gb", [P, E0])
        BQ, BK, BV, PG, PB = range(5)
        w_gate = sb("w_gate", [P, ITEMS * P - INTER])
        w_up = sb("w_up", [P, ITEMS * P - INTER])
        w_down = sb("w_down", [P, ITEMS, D])
        sel3 = sb("sel3", [3 * E0, PAIRS * P], BF16)
        comb3 = sb("comb3", [P, NT, 3 * E0], BF16)
        reset0 = sb("reset0", [P, NT * E0])
        top8 = sb("top8", [P, NT, 8])
        left = sb("left", [P, NT])
        on = sb("on", [P, 2, GT, D])
        onT = sb("onT", [P, GTOK])
        ln_gb = sb("ln_gb", [P, 2, D])
        wr = sb("wr", [P, E1])
        reset1 = sb("reset1", [P, NT * E1])
        reset_t = sb("reset_t", [P, NT * E1])
        steps = sb("steps", [P, TOK // ST])
        tile_no = sb("tile_no", [1, NST])
        before = sb("before", [P, P])
        beforeb = sb("beforeb", [P, P], BF16)
        onesb = sb("onesb", [P, P], BF16)
        zero = sb("zero", [P, D])
        chosenb = sb("chosenb", [P, E1, NT], BF16)
        count = sb("count", [P, 4, E1])
        expert = sb("expert", [1, NST], I32)
        slot = sb("slot", [P, 2, NT], U32)
        slot_f = sb("slot_f", [P, 2, NT])
        weight = sb("weight", [P, 2, NT])
        OA = X2T[:, :].rearrange("p (t d) -> p t d", t=NT)
        XE = CN
        got = [XNT[:, :].rearrange("p (t d) -> p t d", t=NT), X2T[:, :].rearrange("p (t d) -> p t d", t=NT)]
        q_flat = Qz[:, :, :, :, :].rearrange("p a b c d -> p (a b c d)")
        silu = q_flat[:, 0:2 * GTOK].rearrange("p (a s) -> p a s", a=2)
        hid = q_flat[:, 2 * GTOK:4 * GTOK].rearrange("p (a s) -> p a s", a=2)
        gated = q_flat[:, 4 * GTOK:6 * GTOK].rearrange("p (a s) -> p a s", a=2)
        W1N, W2N = HID + CH, HID + D
        w1 = q_flat[:, 0:2 * W1N].rearrange("p (a n) -> p a n", a=2)
        w2 = q_flat[:, 2 * W1N:2 * (W1N + W2N)].rearrange("p (a n) -> p a n", a=2)
        v_flat = Vz[0][:, :, :, :].rearrange("p a b c -> p (a b c)")
        hx = v_flat[:, 0:2 * CH * ST].rearrange("p (a c s) -> p a c s", a=2, c=CH)
        o = 2 * CH * ST
        xs = v_flat[:, o:o + 2 * ST].rearrange("p (a h d) -> p a h d", a=2, d=D)
        xsT = v_flat[:, o + 2 * ST:o + 4 * ST].rearrange("p (a s) -> p a s", a=2)
        ys = v_flat[:, o + 4 * ST:o + 6 * ST].rearrange("p (a h d) -> p a h d", a=2, d=D)
        XS = nc.dram_tensor("sorted_tokens", (NSLOT, D), F32, kind="Internal").ap()
        YS = nc.dram_tensor("sorted_results", (NSLOT, D), F32, kind="Internal").ap()

        x_in, cn_in, w_in, ct_in, mask_in_s, mask_spread = map(sem, ("x_in", "cn_in", "w_in", "ct_in", "mask_in_s", "mask_spread"))
        const_ready, vz_zero, mask_cut, mask_fill = map(sem, ("const_ready", "vz_zero", "mask_cut", "mask_fill"))
        bqh_ready, mask_clamped = map(sem, ("bqh_ready", "mask_clamped"))

        stood = {}

        def stand(eng):
            name = type(eng).__name__
            if name not in stood:
                stood[name] = sem(f"stood_{len(stood)}")
            eng.sem_inc(stood[name], 1)

        class Norm:
            def __init__(self, name):
                self.stats, self.aggr, self.rstd, self.done = (sem(f"{name}_{x}") for x in ("stats", "aggr", "rstd", "done"))

        def norm_stats(dve, ln, g, src):
            stand(dve)
            for j in range(GT):
                nc.vector.bn_stats(stats[:, j, :], src[j]).then_inc(ln.stats, 1)
            dve.wait_ge(ln.stats, g * GT + GT)
            stand(dve)
            for j in range(GT):
                nc.vector.bn_aggr(mv[:, j, :], stats[:, j, :]).then_inc(ln.aggr, 1)

            dve.wait_ge(ln.aggr, g * GT + GT)
            step = [0]

            def chain(instruction):
                step[0] += 1
                instruction.then_inc(ln.rstd, 1)
                dve.wait_ge(ln.rstd, g * ROOT_STEPS + step[0])

            chain(nc.vector.tensor_scalar(var_eps[:, :], mv[:, :, 1], EPS, None, ALU.add))
            chain(nc.vector.tensor_scalar(rstd[:, :].bitcast(I32), var_eps[:, :].bitcast(I32), 1, None, ALU.logical_shift_right))
            chain(nc.vector.tensor_scalar(rstd[:, :].bitcast(I32), rstd[:, :].bitcast(I32), -1.0, float(0x5f3759df), ALU.mult, ALU.add))
            for _ in range(NEWTON):
                chain(nc.vector.tensor_tensor(root_t[:, :], rstd[:, :], rstd[:, :], ALU.mult))
                chain(nc.vector.scalar_tensor_tensor(out=root_t[:, :], in0=root_t[:, :], scalar=-0.5, in1=var_eps[:, :],
                                                     op0=ALU.mult, op1=ALU.mult))
                chain(nc.vector.scalar_tensor_tensor(out=rstd[:, :], in0=root_t[:, :], scalar=1.5, in1=rstd[:, :],
                                                     op0=ALU.add, op1=ALU.mult))
            assert step[0] == ROOT_STEPS

        def norm_apply(dve, ln, g, src, dst):
            for j in range(GT):
                nc.vector.tensor_scalar(dst[j], src[j], mv[:, j, 0:1], rstd[:, j:j + 1],
                                        ALU.subtract, ALU.mult).then_inc(ln.done, 1)

        def tiles4(t, g):
            return [t[:, g * GT + j, :] for j in range(GT)]

        def local4(t):
            return [t[:, j, :] for j in range(GT)]

        ln1 = Norm("ln1")
        ln1_T, ln1_kept = sem("ln1_T"), sem("ln1_kept")

        class AttSems:
            def __init__(self, l):
                self.k_ready, self.q_ready, self.v_ready, self.k_kept, self.q_kept = (
                    sem(f"{n}{l}") for n in ("k_ready", "q_ready", "v_ready", "k_kept", "q_kept"))
                self.v_kept, self.ct_in, self.scores, self.maxed, self.clipped = (
                    sem(f"{n}{l}") for n in ("v_kept", "ct_in", "scores", "maxed", "clipped"))
                self.shifted, self.exped, self.summed, self.recip, self.normed = (
                    sem(f"{n}{l}") for n in ("shifted", "exped", "summed", "recip", "normed"))
                self.pt_ready, self.pt_kept, self.pv, self.o_kept = (
                    sem(f"{n}{l}") for n in ("pt_ready", "pt_kept", "pv", "o_kept"))

        att_sems = [AttSems(0), AttSems(1)]
        a0, a1 = att_sems
        proj_ready, x1_ready, x2T_ready, x2T_kept, x2T_spread, lg_ready, lg_kept = map(
            sem, ("proj_ready", "x1_ready", "x2T_ready", "x2T_kept", "x2T_spread", "lg_ready", "lg_kept"))
        ln2 = Norm("ln2")
        oT_ready, oN_kept = sem("oT_ready"), sem("oN_kept")
        out_done = sem("out_done")
        sig_done, gate_step, comb_ready, combT_ready, combT_kept = map(sem, ("sig_done", "gate_step", "comb_ready", "combT_ready", "combT_kept"))
        a_ready, b_ready, silu_done, gated_done, hid_done, down_done, y_ready, x2_ready = map(
            sem, ("a_ready", "b_ready", "silu_done", "gated_done", "hid_done", "down_done", "y_ready", "x2_ready"))
        ln3, ln3b, ln_ctx = Norm("ln3"), Norm("ln3b"), Norm("ln_ctx")
        qT_ready, qT_kept, kT_ready, kT_kept = map(sem, ("qT_ready", "qT_kept", "kT_ready", "kT_kept"))
        ln_o, ln4 = Norm("ln_o"), Norm("ln4")
        scaled, on_ready, onT_ready, onT_kept, wo_ready, gelu_o, x_on, x3_ready = map(
            sem, ("scaled", "on_ready", "onT_ready", "onT_kept", "wo_ready", "gelu_o", "x_on", "x3_ready"))
        xe_T, xe_T_kept, xe_kept, lg1_ready, lg1_kept = map(sem, ("xe_T", "xe_T_kept", "xe_kept", "lg1_ready", "lg1_kept"))
        xs_zeroed, route_step, ranks_ready, diff_ready, exp_ready, slots_ready, scattered = map(
            sem, ("xs_zeroed", "route_step", "ranks_ready", "diff_ready", "exp_ready", "slots_ready", "scattered"))
        w1_in, w2_in, xs_in, y_out = ([sem(f"{n}{i}") for i in range(2)] for n in ("w1_in", "w2_in", "xs_in", "y_out"))
        xsT_ready, xsT_kept, up_ready, gelued, down_ready, y_kept = map(
            sem, ("xsT_ready", "xsT_kept", "up_ready", "gelued", "down_ready", "y_kept"))
        gathered = [sem(f"gathered{g}") for g in range(NG)]
        half_done, x4_ready = sem("half_done"), sem("x4_ready")
        zero_ready = sem("zero_ready")

        S_BANKS, PT_BANK, O_BANKS, PJ = 0, 4, 5, 7

        x_dram = d["x"].rearrange("(t p) d -> p t d", p=P)
        cn_dram = d["ctx"].rearrange("(t p) d -> p t d", p=P)
        NW = 17 + 4 + 12
        A_BANK, B_BANK, C_BANK, Y_BANK, T_BANK = 0, 2, 4, 6, 7

        block = ctx.enter_context(nc.Block())

        @block.sync
        def _(sp):
            sp.dma_start(X[:, :, :], x_dram).then_inc(x_in, 16)
            for i, name in enumerate(("L0_wq", "L0_wk", "L0_wv", "L0_wo")):
                sp.dma_start(w_att[0][:, i, :], d[name]).then_inc(w_in, 16)
            for i, name in enumerate(("L0_bq", "L0_bk", "L0_bv", "pre_g", "pre_b")):
                sp.dma_start(cols[:, i:i + 1], d[name]).then_inc(w_in, 16)
            sp.dma_start(bo_row[:, :], d["L0_bo"]).then_inc(w_in, 16)
            sp.dma_start(head0[:, :], d["c_head0"]).then_inc(w_in, 16)
            sp.dma_start(head1[:, :], d["c_head1"]).then_inc(w_in, 16)
            sp.dma_start(win_u[:, :], d["c_win_u"]).then_inc(w_in, 16)
            sp.dma_start(win_v[:, :], d["c_win_v"]).then_inc(w_in, 16)
            sp.dma_start(ident[:, :], d["c_ident"]).then_inc(w_in, 16)
            sp.dma_start(gw[:, :], d["gate_w"]).then_inc(w_in, 16)
            sp.dma_start(gb[:, :], d["gate_b"]).then_inc(w_in, 16)
            for i, name in enumerate(("L1_Wq", "L1_Wk", "L1_Wv", "L1_Wo")):
                sp.dma_start(w_att[1][:, i, :], d[name]).then_inc(w_in, 16)
            for t, name in ((w_gate, "w_gate"), (w_up, "w_up"), (reset0, "c_reset0"), (wr, "Wr"), (reset1, "c_reset1"),
                            (reset_t, "c_reset_t"), (steps, "c_steps"), (tile_no, "c_tile"), (before, "c_before")):
                sp.dma_start(t[:, :], d[name]).then_inc(w_in, 16)
            sp.dma_start(w_down[:, :, :], d["w_down"]).then_inc(w_in, 16)
            sp.dma_start(ln_gb[:, :, :], d["ln_gb"]).then_inc(w_in, 16)
            sp.dma_start(Pr[0:3 * E0, 0:2, :].rearrange("p a b -> p (a b)"), d["c_sel3"]).then_inc(w_in, 16)
            sp.dma_start(mask_in[:, :], d["mask"]).then_inc(mask_in_s, 16)
            sp.dma_start(CN[:, :, :], cn_dram).then_inc(cn_in, 16)
            sp.wait_ge(zero_ready, 1)
            sp.dma_start(XS.rearrange("(a p) d -> p a d", p=P),
                         zero[:, :].unsqueeze(1).broadcast_to([P, NSLOT // P, D])).then_inc(xs_zeroed, 16)
            sp.wait_ge(mask_cut, 3)
            for i in range(3):
                sp.dma_start(mask_rows[MROW + i:MROW + i + 1, :].rearrange("o (b k) -> o b k", b=B),
                             mask_part[:, i, :]).then_inc(mask_spread, 16)

            def load_ct(a):
                def body(g, par, prev, cur, nxt):
                    if nxt:
                        need(sp, a.v_ready, g + 1)
                        need(sp, a.k_ready, g + 1)
                        sp.dma_start(ctg[:, :], d["ctxT"][:, span((g + 1) * GTOK, GTOK)]).then_inc(a.ct_in, 16)
                bodies(sp, body, NG)

            load_ct(a0)
            sp.wait_ge(a0.v_ready, NG)
            load_ct(a1)

            sp.wait_ge(scattered, 16 * 2 * NT)
            sp.wait_ge(xs_zeroed, 16)

            def expert_tiles(k, par, prev, cur, nxt):
                if nxt:
                    need(sp, xsT_ready, k)
                    sp.dma_start(xs[:, 1 - par, :, :], XS[span((k + 1) * ST, ST), :].rearrange("(h p) d -> p h d", p=P)).then_inc(xs_in[1 - par], 16)
                if prev:
                    sp.wait_ge(y_kept, k)
                    sp.dma_start(YS[span((k - 1) * ST, ST), :].rearrange("(h p) d -> p h d", p=P), ys[:, 1 - par, :, :]).then_inc(y_out[1 - par], 16)
            for i in range(2):
                sp.sem_inc(y_out[i], 16)
            bodies(sp, expert_tiles, NST)

            for g in range(NG):
                sp.wait_ge(x4_ready, GT * (g + 1))
                sp.dma_start(out.rearrange("(t p) d -> p t d", p=P)[:, g * GT:(g + 1) * GT, :],
                             X[:, g * GT:(g + 1) * GT, :]).then_inc(out_done, 16)
            sp.wait_ge(out_done, 16 * NG)

        @block.gpsimd
        def _(pool):
            nc.gpsimd.memset(ones_row[:, :], 1.0).then_inc(const_ready, 1)
            nc.gpsimd.memset(onesb[:, :], 1.0).then_inc(const_ready, 1)
            nc.gpsimd.memset(zero[:, :], 0.0).then_inc(zero_ready, 1)
            for l in range(2):
                nc.gpsimd.memset(Vz[l][:, :, :, :], 0.0).then_inc(vz_zero, 1)
            pool.wait_ge(w_in, 16 * NW)
            nc.gpsimd.tensor_copy(mask_rows[0:MROW, :].rearrange("r (b k) -> r b k", b=B),
                                  win_v[:, :].unsqueeze(1).broadcast_to([MROW, B, S])).then_inc(mask_fill, 1)

            def normalise(L, a):
                def norm(g, u):
                    n = g * L.units + u
                    pool.wait_ge(a.recip, n + 1)
                    pr = Pr[:, u % 4, :].rearrange("p (s k) -> p s k", k=S)
                    nc.gpsimd.tensor_tensor(pr, pr, rsum[:, u % 2, :].unsqueeze(2).broadcast_to([P, 8, S]),
                                            ALU.mult).then_inc(a.normed, 1)

                def body(g, par, prev, cur, nxt):
                    for u in range(L.units):
                        if cur:
                            norm(g, u)
                        if L.layer == 0 and prev and u == 7:
                            pool.wait_ge(x2T_kept, g)
                            nc.gpsimd.tensor_copy(X2T[:, span((g - 1) * GTOK, GTOK)], xnT[:, :]).then_inc(x2T_spread, 1)
                bodies(pool, body, NG)

            normalise(Att(0), a0)
            normalise(Att(1), a1)

            def layer1_tail(g, par, prev, cur, nxt):
                if cur:
                    pool.wait_ge(on_ready, g + 1)
                    x4 = X[:, span(g * GT, GT), :]
                    nc.gpsimd.tensor_tensor(x4, x4, on[:, par, :, :], ALU.add).then_inc(x_on, 1)
                if nxt:
                    pool.wait_ge(ln_o.done, GT * g + 2 * GT)
                    need(pool, onT_ready, g)
                    gain, offset = (ln_gb[:, i, :].unsqueeze(1).broadcast_to([P, GT, D]) for i in range(2))
                    nc.gpsimd.tensor_tensor(on[:, 1 - par, :, :], xn[:, :, :], gain, ALU.mult).then_inc(scaled, 1)
                    pool.wait_ge(scaled, g + 2)
                    nc.gpsimd.tensor_tensor(on[:, 1 - par, :, :], on[:, 1 - par, :, :], offset, ALU.add).then_inc(on_ready, 1)
                if prev:
                    pool.wait_ge(ln4.done, GT * g)
                    nc.gpsimd.tensor_copy(XE[:, span((g - 1) * GT, GT), :], xm[:, :, :]).then_inc(xe_kept, 1)
            pool.wait_ge(x2_ready, NG)
            bodies(pool, layer1_tail, NG)

            pool.wait_ge(xe_kept, NG)
            pool.wait_ge(xs_zeroed, 16)
            pool.wait_ge(slots_ready, 1)
            for t in range(NT):
                for i in range(2):
                    nc.gpsimd.indirect_dma_start(XS, bass.IndirectOffsetOnAxis(ap=slot[:, i, t:t + 1], axis=0),
                                                 XE[:, t, :], None).then_inc(scattered, 16)

            def expert_weights(k, par, prev, cur, nxt):
                if nxt:
                    e = nc.gpsimd.value_load(expert[0:1, span(k + 1, 1)], min_val=0, max_val=E1 - 1)
                    need(pool, gelued, CH * k)
                    nc.gpsimd.dma_start(w1[:, 1 - par, :], d["w1"][span(e, 1), :, :].rearrange("o p n -> (o p) n")).then_inc(w1_in[1 - par], 16)
                    need(pool, y_kept, k)
                    nc.gpsimd.dma_start(w2[:, 1 - par, :], d["w2"][span(e, 1), :, :].rearrange("o p n -> (o p) n")).then_inc(w2_in[1 - par], 16)
            bodies(pool, expert_weights, NST)

            for i in range(2):
                pool.wait_ge(y_out[i], 16 * ((NST + 1 - i) // 2 + 1))
            for t in range(NT):
                for i in range(2):
                    nc.gpsimd.indirect_dma_start(got[i][:, t, :], None, YS,
                                                 bass.IndirectOffsetOnAxis(ap=slot[:, i, t:t + 1], axis=0)).then_inc(gathered[t // GT], 16)

        @block.vector
        def _(dve):
            dve.wait_ge(w_in, 16 * NW)
            nc.vector.tensor_scalar(bq_h[:, :], head0[:, :], cols[:, BQ:BQ + 1], None, ALU.mult).then_inc(bqh_ready, 1)
            nc.vector.tensor_copy(win_ub[:, :], win_u[:, :]).then_inc(const_ready, 1)
            nc.vector.tensor_copy(identb[:, :], ident[:, :]).then_inc(const_ready, 1)
            nc.vector.tensor_copy(beforeb[:, :], before[:, :]).then_inc(const_ready, 1)
            nc.vector.tensor_copy(sel3[:, :], Pr[0:3 * E0, 0:2, :].rearrange("p a b -> p (a b)")).then_inc(const_ready, 1)
            dve.wait_ge(mask_in_s, 16)
            nc.vector.tensor_scalar(mask_left[:, :], mask_in[:, :], NEG, None, ALU.max).then_inc(mask_clamped, 1)
            dve.wait_ge(mask_clamped, 1)
            nc.vector.tensor_copy(mask_part[:, 0, :], mask_left[:, :]).then_inc(mask_cut, 1)
            for i in range(1, 3):
                dve.wait_ge(mask_cut, i)
                nc.vector.tensor_tensor(mask_left[:, :], mask_left[:, :], mask_part[:, i - 1, :], ALU.subtract).then_inc(mask_clamped, 1)
                dve.wait_ge(mask_clamped, i + 1)
                nc.vector.tensor_copy(mask_part[:, i, :], mask_left[:, :]).then_inc(mask_cut, 1)

            dve.wait_ge(x_in, 16)

            dve.sem_inc(lg_kept, 1)

            def first_norm(g):
                norm_stats(dve, ln1, g, tiles4(X, g))
                need(dve, ln1_T, g)
                norm_apply(dve, ln1, g, tiles4(X, g), local4(xn))

            first_norm(0)
            with dve.Fori(1, NG) as g:
                first_norm(g)

            def attention(L, a):
                def shift(g, u):
                    n = g * L.units + u
                    dve.wait_ge(a.scores, n + 1)
                    need(dve, a.pt_ready, n - 3)
                    s = PS[:, S_BANKS + 2 * (u % 2):S_BANKS + 2 * (u % 2) + 2, 0:256].rearrange("p a (s k) -> p a s k", k=S)
                    pr = Pr[:, u % 4, :].rearrange("p (a s k) -> p a s k", a=2, k=S)
                    m = mx[:, u % 2, :].rearrange("p (a s) -> p a s", a=2)
                    if L.layer == 1:
                        nc.vector.tensor_scalar(pr, s, -10000.0, 10000.0, ALU.max, ALU.min).then_inc(a.clipped, 1)
                        dve.wait_ge(a.clipped, n + 1)
                        s = pr
                    nc.vector.tensor_reduce(m, s, AX.X, ALU.max).then_inc(a.maxed, 1)
                    dve.wait_ge(a.maxed, n + 1)
                    nc.vector.tensor_tensor(pr, s, m.unsqueeze(3).broadcast_to([P, 2, 4, S]), ALU.subtract).then_inc(a.shifted, 1)

                def total(g, u):
                    n = g * L.units + u
                    dve.wait_ge(a.exped, n + 1)
                    nc.vector.tensor_reduce(sums[:, u % 2, :], Pr[:, u % 4, :].rearrange("p (s k) -> p s k", k=S),
                                            AX.X, ALU.add).then_inc(a.summed, 1)
                    dve.wait_ge(a.summed, n + 1)
                    need(dve, a.normed, n - 1)
                    nc.vector.reciprocal(rsum[:, u % 2, :], sums[:, u % 2, :]).then_inc(a.recip, 1)

                def body(g, par, prev, cur, nxt):
                    for u in range(L.units):
                        if u + 1 < L.units:
                            if cur:
                                shift(g, u + 1)
                        elif nxt:
                            shift(g + 1, 0)
                        if cur:
                            total(g, u)
                        if L.layer == 0 and prev and u == 4:
                            dve.wait_ge(proj_ready, g)
                            x4 = X[:, span((g - 1) * GT, GT), :]
                            nc.vector.tensor_tensor(x4, x4, PS[:, PJ, :].rearrange("p (t d) -> p t d", t=GT), ALU.add).then_inc(x1_ready, 1)
                            dve.wait_ge(x1_ready, g)
                            norm_stats(dve, ln2, g - 1, tiles4(X, g - 1))
                        if L.layer == 0 and prev and u == 5:
                            norm_apply(dve, ln2, g - 1, tiles4(X, g - 1), local4(xn))
                        if L.layer == 0 and prev and u == 7:
                            dve.wait_ge(lg_ready, g)
                            nc.vector.tensor_copy(LG[:, span((g - 1) * GT, GT), :],
                                                  PS[:, PJ, 0:GT * E0].rearrange("p (t e) -> p t e", t=GT)).then_inc(lg_kept, 1)
                bodies(dve, body, NG)

            attention(Att(0), a0)

            def chain(s, value, instruction):
                value[0] += 1
                instruction.then_inc(s, 1)
                dve.wait_ge(s, value[0])

            def choose(s, value, v, top, E, K, above, equal, rank, reset):
                for t in range(NT):
                    chain(s, value, nc.vector.max(top[:, t, :], v[:, t, :]))
                least = top[:, :, K - 1].unsqueeze(2).broadcast_to([P, NT, E])
                chain(s, value, nc.vector.tensor_tensor(above, v, least, ALU.is_gt))
                chain(s, value, nc.vector.tensor_tensor(equal, v, least, ALU.is_equal))
                chain(s, value, nc.vector.tensor_reduce(left[:, :], above, AX.X, ALU.add))
                chain(s, value, nc.vector.tensor_scalar(left[:, :], left[:, :], -1.0, float(K), ALU.mult, ALU.add))
                flat = [x.rearrange("p t e -> p (t e)") for x in (rank, equal)]
                chain(s, value, nc.vector.tensor_tensor_scan(flat[0], reset, flat[1], 0.0, ALU.mult, ALU.add))
                chain(s, value, nc.vector.tensor_tensor(rank, rank, left[:, :].unsqueeze(2).broadcast_to([P, NT, E]), ALU.is_le))
                chain(s, value, nc.vector.tensor_tensor(equal, equal, rank, ALU.mult))
                chain(s, value, nc.vector.tensor_tensor(above, above, equal, ALU.add))

            dve.wait_ge(sig_done, 1)
            dve.wait_ge(a0.pt_ready, 8 * NG)
            dve.wait_ge(a0.pv, 8 * NG)
            sig, biased, above, equal = (Pr[:, i, :].rearrange("p (t e) -> p t e", e=E0) for i in range(4))
            rank, w0 = (PT[:, i, :].rearrange("p (t e) -> p t e", e=E0) for i in range(2))
            at = [0]
            chain(gate_step, at, nc.vector.tensor_tensor(biased, sig, gb[:, :].unsqueeze(1).broadcast_to([P, NT, E0]), ALU.add))
            choose(gate_step, at, biased, top8, E0, K0, above, equal, rank, reset0[:, :])
            chain(gate_step, at, nc.vector.tensor_tensor(w0, sig, above, ALU.mult))
            chain(gate_step, at, nc.vector.tensor_reduce(left[:, :], w0, AX.X, ALU.add))
            chain(gate_step, at, nc.vector.reciprocal(left[:, :], left[:, :]))
            chain(gate_step, at, nc.vector.scalar_tensor_tensor(out=w0, in0=w0, scalar=ROUTE_SCALE, in1=left[:, :].unsqueeze(2).broadcast_to([P, NT, E0]),
                                                                op0=ALU.mult, op1=ALU.mult))
            part = [comb3[:, :, i * E0:(i + 1) * E0] for i in range(3)]
            chain(gate_step, at, nc.vector.tensor_copy(part[0], w0))
            chain(gate_step, at, nc.vector.tensor_tensor(w0, w0, part[0], ALU.subtract))
            chain(gate_step, at, nc.vector.tensor_copy(part[1], w0))
            chain(gate_step, at, nc.vector.tensor_tensor(w0, w0, part[1], ALU.subtract))
            nc.vector.tensor_copy(part[2], w0).then_inc(comb_ready, 1)

            def experts0(g, par, prev, cur, nxt):
                for s in range(ITEMS):
                    n = g * ITEMS + s
                    buf = (s + par) % 2
                    rows = P if s < PAIRS else INTER
                    if prev and s == 0:
                        dve.wait_ge(y_ready, g)
                        x4 = X[:, span((g - 1) * GT, GT), :]
                        nc.vector.tensor_tensor(x4, x4, PS[:, Y_BANK, :].rearrange("p (t d) -> p t d", t=GT), ALU.add).then_inc(x2_ready, 1)
                    if cur:
                        dve.wait_ge(silu_done, n + 1)
                        dve.wait_ge(b_ready, n + 1)
                        need(dve, down_done, n - 1)
                        if s < PAIRS:
                            nc.vector.tensor_tensor(gated[:, buf, :], silu[:, buf, :], PS[:, B_BANK + buf, :], ALU.mult).then_inc(gated_done, 1)
                            dve.wait_ge(gated_done, g * PAIRS + s + 1)
                            nc.vector.tensor_tensor(hid[:, buf, :], gated[:, buf, :], PS[:, C_BANK + buf, :], ALU.mult).then_inc(hid_done, 1)
                        else:
                            nc.vector.tensor_tensor(hid[0:rows, buf, :], silu[0:rows, buf, :], PS[0:rows, B_BANK + buf, :], ALU.mult).then_inc(hid_done, 1)
                    if prev and s == 1:
                        dve.wait_ge(x2_ready, g)
                        if not cur:
                            dve.wait_ge(kT_ready, g - 1)
                        norm_stats(dve, ln3, g - 1, tiles4(X, g - 1))
                        norm_apply(dve, ln3, g - 1, tiles4(X, g - 1), local4(xm))
                    if prev and s == 3:
                        dve.wait_ge(ln3.done, GT * g)
                        norm_stats(dve, ln3b, g - 1, local4(xm))
                        if not cur:
                            dve.wait_ge(qT_ready, g - 1)
                        norm_apply(dve, ln3b, g - 1, local4(xm), local4(xn))
                    if prev and s == 5:
                        norm_stats(dve, ln_ctx, g - 1, tiles4(CN, g - 1))
                        norm_apply(dve, ln_ctx, g - 1, tiles4(CN, g - 1), local4(xm))
            dve.wait_ge(cn_in, 16)
            bodies(dve, experts0, NG)

            attention(Att(1), a1)

            def layer1_tail(g, par, prev, cur, nxt):
                if cur:
                    dve.wait_ge(gelu_o, g + 1)
                    dve.wait_ge(x_on, g + 1)
                    x4 = X[:, span(g * GT, GT), :]
                    nc.vector.tensor_tensor(x4, x4, OTs[:, :].rearrange("p (t d) -> p t d", t=GT), ALU.add).then_inc(x3_ready, 1)
                if nxt:
                    norm_stats(dve, ln_o, g + 1, tiles4(OA, g + 1))
                    need(dve, on_ready, g + 1)
                    norm_apply(dve, ln_o, g + 1, tiles4(OA, g + 1), local4(xn))
                if prev:
                    dve.wait_ge(x3_ready, g)
                    norm_stats(dve, ln4, g - 1, tiles4(X, g - 1))
                    if not cur:
                        dve.wait_ge(xe_T, g - 1)
                        dve.wait_ge(xe_kept, g - 1)
                    norm_apply(dve, ln4, g - 1, tiles4(X, g - 1), local4(xm))
                    dve.wait_ge(lg1_ready, g)
                    nc.vector.tensor_copy(LG[:, span((g - 1) * GT, GT), 0:E1],
                                          PS[:, 3, 0:GT * E1].rearrange("p (t e) -> p t e", t=GT)).then_inc(lg1_kept, 1)
            dve.wait_ge(oN_kept, NG + 1)
            bodies(dve, layer1_tail, NG)

            dve.wait_ge(lg1_kept, NG)
            at = [0]
            N1 = NT * E1
            v, above, equal, rank, first, second = (Pr[:, i // 2, (i % 2) * N1:(i % 2 + 1) * N1].rearrange("p (t e) -> p t e", e=E1) for i in range(6))
            place, rest = (Pr[:, 3, i * N1:(i + 1) * N1].rearrange("p (e t) -> p e t", e=E1) for i in range(2))
            run_t = PT[:, 0, 0:N1].rearrange("p (e t) -> p e t", e=E1)
            prod = PT[:, 0, N1:2 * N1].rearrange("p (t e) -> p t e", e=E1)
            many = PT[:, 1, 0:E1 * (TOK // ST)].rearrange("p (e s) -> p e s", e=E1)

            def step(instruction):
                chain(route_step, at, instruction)

            step(nc.vector.tensor_copy(v, LG[:, :, 0:E1]))
            choose(route_step, at, v, top8, E1, 2, above, equal, rank, reset1[:, :])
            best = top8[:, :, 0].unsqueeze(2).broadcast_to([P, NT, E1])
            step(nc.vector.tensor_tensor(equal, v, best, ALU.is_equal))
            step(nc.vector.tensor_tensor_scan(rank.rearrange("p t e -> p (t e)"), reset1[:, :], equal.rearrange("p t e -> p (t e)"), 0.0, ALU.mult, ALU.add))
            step(nc.vector.tensor_scalar(rank, rank, 1.0, None, ALU.is_le))
            step(nc.vector.tensor_tensor(first, equal, rank, ALU.mult))
            step(nc.vector.tensor_tensor(second, above, first, ALU.subtract))
            step(nc.vector.tensor_copy(chosenb[:, :, :].rearrange("p e t -> p t e"), above))
            nc.vector.tensor_tensor(left[:, :], top8[:, :, 1], top8[:, :, 0], ALU.subtract).then_inc(diff_ready, 1)
            dve.wait_ge(ranks_ready, 1)
            ahead = PS[:, 0, 0:N1].rearrange("p (e t) -> p e t", e=E1)
            totals = PS[:, 1, 0:N1]
            step(nc.vector.tensor_copy(rest.rearrange("p e t -> p (e t)"), totals))
            step(nc.vector.tensor_tensor_scan(run_t.rearrange("p e t -> p (e t)"), reset_t[:, :], rest.rearrange("p e t -> p (e t)"), 0.0, ALU.mult, ALU.add))
            step(nc.vector.tensor_tensor(place, run_t, rest, ALU.subtract))
            step(nc.vector.tensor_tensor(place, place, ahead, ALU.add))
            n_tok = run_t[:, :, NT - 1].unsqueeze(2).broadcast_to([P, E1, TOK // ST])
            step(nc.vector.tensor_tensor(many, n_tok, steps[:, :].unsqueeze(1).broadcast_to([P, E1, TOK // ST]), ALU.is_gt))
            step(nc.vector.tensor_reduce(count[:, 0, :], many, AX.X, ALU.add))
            step(nc.vector.memset(count[:, 3, :], 1.0))
            step(nc.vector.tensor_tensor_scan(count[:, 1, :], count[:, 3, :], count[:, 0, :], 0.0, ALU.mult, ALU.add))
            step(nc.vector.tensor_tensor(count[:, 2, :], count[:, 1, :], count[:, 0, :], ALU.subtract))
            step(nc.vector.tensor_scalar(count[:, 2, :], count[:, 2, :], float(ST), None, ALU.mult))
            step(nc.vector.tensor_tensor(place, place, count[:, 2, :].unsqueeze(2).broadcast_to([P, E1, NT]), ALU.add))
            for i, chosen in enumerate((first, second)):
                step(nc.vector.tensor_tensor(prod, chosen, place.rearrange("p e t -> p t e"), ALU.mult))
                step(nc.vector.tensor_reduce(slot_f[:, i, :], prod, AX.X, ALU.add))
            step(nc.vector.tensor_copy(slot[:, :, :], slot_f[:, :, :]))
            own = PT[0:1, 1, 0:NST * E1].rearrange("p (k e) -> p k e", e=E1)
            step(nc.vector.tensor_tensor(own, count[0:1, 1, :].unsqueeze(1).broadcast_to([1, NST, E1]),
                                         tile_no[:, :].unsqueeze(2).broadcast_to([1, NST, E1]), ALU.is_le))
            owner = PT[0:1, 0, 0:NST]
            step(nc.vector.tensor_reduce(owner, own, AX.X, ALU.add))
            step(nc.vector.tensor_scalar(owner, owner, float(E1 - 1), None, ALU.min))
            nc.vector.tensor_copy(expert[:, :], owner).then_inc(slots_ready, 1)
            dve.wait_ge(exp_ready, 1)
            step(nc.vector.tensor_scalar(slot_f[:, 0, :], weight[:, 1, :], 1.0, None, ALU.add))
            step(nc.vector.reciprocal(weight[:, 0, :], slot_f[:, 0, :]))
            step(nc.vector.tensor_tensor(weight[:, 1, :], weight[:, 1, :], weight[:, 0, :], ALU.mult))

            def expert_tiles(k, par, prev, cur, nxt):
                if nxt:
                    dve.wait_ge(xsT_ready, k + 2)
                    need(dve, up_ready, k)
                    nc.vector.tensor_copy(xsT[:, 1 - par, :], PS[:, 4, 0:ST]).then_inc(xsT_kept, 1)
                if prev:
                    dve.wait_ge(down_ready, k)
                    dve.wait_ge(y_out[1 - par], sixteens(k - 1, 1 - par))
                    nc.vector.tensor_tensor(ys[:, 1 - par, :, :], PS[:, 5 + (1 - par), 0:ST].rearrange("p (h d) -> p h d", d=D),
                                            w2[:, 1 - par, HID:HID + D].unsqueeze(1).broadcast_to([P, ST // P, D]), ALU.add).then_inc(y_kept, 1)
            bodies(dve, expert_tiles, NST)

            for t in range(NT):
                if t % GT == 0:
                    dve.wait_ge(gathered[t // GT], 16 * 2 * GT)
                nc.vector.scalar_tensor_tensor(out=X[:, t, :], in0=got[0][:, t, :], scalar=weight[:, 0, t:t + 1], in1=X[:, t, :],
                                               op0=ALU.mult, op1=ALU.add).then_inc(half_done, 1)
                if t >= 1:
                    dve.wait_ge(half_done, t)
                    nc.vector.scalar_tensor_tensor(out=X[:, t - 1, :], in0=got[1][:, t - 1, :], scalar=weight[:, 1, t - 1:t], in1=X[:, t - 1, :],
                                                   op0=ALU.mult, op1=ALU.add).then_inc(x4_ready, 1)
            dve.wait_ge(half_done, NT)
            nc.vector.scalar_tensor_tensor(out=X[:, NT - 1, :], in0=got[1][:, NT - 1, :], scalar=weight[:, 1, NT - 1:NT], in1=X[:, NT - 1, :],
                                           op0=ALU.mult, op1=ALU.add).then_inc(x4_ready, 1)

        @block.scalar
        def _(act):
            def keep_norm(g):
                act.wait_ge(ln1_T, g + 1)
                nc.scalar.activation(XNT[:, span(g * GTOK, GTOK)], PS[:, PT_BANK, :], ACT.Copy).then_inc(ln1_kept, 1)

            keep_norm(0)
            with act.Fori(1, NG) as g:
                keep_norm(g)
            act.wait_ge(w_in, 16 * NW)
            act.wait_ge(bqh_ready, 1)
            act.wait_ge(vz_zero, 2)

            def attention(L, a):
                head = head0 if L.layer == 0 else head1

                def keep_k(g, par):
                    act.wait_ge(a.k_ready, g + 1)
                    if L.layer == 0:
                        nc.scalar.activation(KTb[:, par, :], PS[:, PJ, :], ACT.Identity, bias=cols[:, BK:BK + 1]).then_inc(a.k_kept, 1)
                    else:
                        nc.scalar.activation(KTb[:, par, :], PS[:, PJ, :], ACT.Copy).then_inc(a.k_kept, 1)

                def keep_q(g, par):
                    act.wait_ge(a.q_ready, g + 1)
                    q = PS[:, PJ, :].rearrange("p (b s) -> p b s", s=S)
                    for h in range(L.hl):
                        if L.layer == 0:
                            nc.scalar.activation(Qz[:, par, :, h, :], q, ACT.Identity, bias=bq_h[:, h:h + 1],
                                                 scale=head[:, h:h + 1]).then_inc(a.q_kept, 1)
                        else:
                            nc.scalar.activation(Qz[:, par, :, h, :], q, ACT.Copy, scale=head[:, h:h + 1]).then_inc(a.q_kept, 1)

                def keep_v(g, par):
                    act.wait_ge(a.v_ready, g + 1)
                    for j in range(GT):
                        v = PS[:, PJ, j * P:(j + 1) * P].rearrange("p (a h e) -> p h a e", a=4, e=L.dk)
                        own = Vz[L.layer][:, par, j, :].rearrange("p (h r) -> p h r", h=L.hl)[:, :, 0:P]
                        own = own.rearrange("p h (a m e) -> p h m a e", a=4, e=L.dk)[:, :, 0, :, :]
                        nc.scalar.activation(own, v, ACT.Copy).then_inc(a.v_kept, 1)

                def exp(g, u):
                    n = g * L.units + u
                    act.wait_ge(a.shifted, n + 1)
                    nc.scalar.activation(Pr[:, u % 4, :], Pr[:, u % 4, :], ACT.Exp).then_inc(a.exped, 1)

                def keep_pt(g, u):
                    n = g * L.units + u
                    act.wait_ge(a.pt_ready, n + 1)
                    need(act, a.pv, n - 1)
                    nc.scalar.activation(PT[:, u % 2, :], PS[:, PT_BANK, :], ACT.Copy).then_inc(a.pt_kept, 1)

                def body(g, par, prev, cur, nxt):
                    for u in range(L.units):
                        if u + 1 < L.units:
                            if cur:
                                exp(g, u + 1)
                        elif nxt:
                            exp(g + 1, 0)
                        if u >= 1:
                            if cur:
                                keep_pt(g, u - 1)
                        elif prev:
                            keep_pt(g - 1, L.units - 1)
                        if nxt and u == 0:
                            keep_k(g + 1, 1 - par)
                        if nxt and u == 1:
                            keep_q(g + 1, 1 - par)
                        if nxt and u == 2:
                            keep_v(g + 1, 1 - par)
                        if prev and u == 1:
                            act.wait_ge(a.pv, g * L.units)
                            nc.scalar.activation(OTs[:, :].rearrange("p (j b s) -> p b j s", b=2, s=S),
                                                     PS[:, O_BANKS:O_BANKS + 2, 0:GT * S].rearrange("p b (j s) -> p b j s", s=S),
                                                 ACT.Identity, bias=cols[:, BV:BV + 1] if L.layer == 0 else 0.0).then_inc(a.o_kept, 1)
                        if L.layer == 0 and prev and u == 6:
                            act.wait_ge(x2T_ready, g)
                            if not cur:
                                act.wait_ge(x2T_spread, g - 1)
                            nc.scalar.activation(xnT[:, :], PS[:, PJ, :], ACT.Copy).then_inc(x2T_kept, 1)
                        if L.layer == 1 and prev and u == 3:
                            act.wait_ge(oT_ready, g)
                            nc.scalar.activation(X2T[:, span((g - 1) * GTOK, GTOK)], PS[:, PJ, :], ACT.Copy).then_inc(oN_kept, 1)
                bodies(act, body, NG)

            attention(Att(0), a0)
            act.wait_ge(lg_kept, NG + 1)
            act.wait_ge(a0.pt_ready, 8 * NG)
            nc.scalar.activation(Pr[:, 0, :], LG[:, :, :].rearrange("p t e -> p (t e)"), ACT.Sigmoid).then_inc(sig_done, 1)
            act.wait_ge(combT_ready, 1)
            for i in range(4):
                nc.scalar.activation(combT[:, i * 1024:(i + 1) * 1024], PS[0:3 * E0, i, :].bitcast(BF16), ACT.Copy).then_inc(combT_kept, 1)

            def experts0(g, par, prev, cur, nxt):
                def gate(g, s, buf):
                    n = g * ITEMS + s
                    rows = P if s < PAIRS else INTER
                    act.wait_ge(a_ready, n + 1)
                    nc.scalar.activation(silu[0:rows, buf, :], PS[0:rows, A_BANK + buf, :], ACT.Silu).then_inc(silu_done, 1)

                for s in range(ITEMS):
                    if s + 1 < ITEMS:
                        if cur:
                            gate(g, s + 1, (s + 1 + par) % 2)
                    elif nxt:
                        gate(g + 1, 0, (1 - par) % 2)
                    if prev and s == 5:
                        act.wait_ge(qT_ready, g)
                        nc.scalar.activation(XNT[:, span((g - 1) * GTOK, GTOK)], PS[:, T_BANK, :], ACT.Identity,
                                             bias=cols[:, PB:PB + 1], scale=cols[:, PG:PG + 1]).then_inc(qT_kept, 1)
                    if prev and s == 8:
                        act.wait_ge(kT_ready, g)
                        nc.scalar.activation(KNT[:, span((g - 1) * GTOK, GTOK)], PS[:, T_BANK, :], ACT.Identity,
                                             bias=cols[:, PB:PB + 1], scale=cols[:, PG:PG + 1]).then_inc(kT_kept, 1)
            bodies(act, experts0, NG)
            act.sem_inc(oN_kept, 1)
            attention(Att(1), a1)

            def layer1_tail(g, par, prev, cur, nxt):
                if cur:
                    act.wait_ge(wo_ready, g + 1)
                    need(act, x3_ready, g)
                    nc.scalar.activation(OTs[:, :], PS[:, 1, :], ACT.Gelu).then_inc(gelu_o, 1)
                if nxt:
                    act.wait_ge(onT_ready, g + 2)
                    nc.scalar.activation(onT[:, :], PS[:, 0, :], ACT.Copy).then_inc(onT_kept, 1)
                if prev:
                    act.wait_ge(xe_T, g)
                    nc.scalar.activation(xnT[:, :], PS[:, 2, :], ACT.Copy).then_inc(xe_T_kept, 1)
            bodies(act, layer1_tail, NG)
            act.wait_ge(diff_ready, 1)
            nc.scalar.activation(weight[:, 1, :], left[:, :], ACT.Exp).then_inc(exp_ready, 1)

            def expert_tiles(k, par, prev, cur, nxt):
                if cur:
                    act.wait_ge(up_ready, k + 1)
                    for c in range(CH):
                        nc.scalar.activation(hx[:, par, c, :], PS[:, 2 * par + c // 2, (c % 2) * ST:(c % 2 + 1) * ST], ACT.Gelu,
                                             bias=w1[:, par, HID + c:HID + c + 1]).then_inc(gelued, 1)
            bodies(act, expert_tiles, NST)

        @block.tensor
        def _(pe):
            pe.wait_ge(w_in, 16 * NW)
            pe.wait_ge(const_ready, 6)

            def transpose4(bank, src, done):
                for j in range(GT):
                    last = nc.tensor.transpose(PS[:, bank, j * P:(j + 1) * P], src[:, j, :], ident[:, :])
                last.then_inc(done, 1)

            def first_T(g):
                pe.wait_ge(ln1.done, GT * g + GT)
                need(pe, ln1_kept, g)
                transpose4(PT_BANK, xn, ln1_T)

            first_T(0)
            with pe.Fori(1, NG) as g:
                first_T(g)
            pe.wait_ge(mask_fill, 1)
            pe.wait_ge(mask_spread, 48)
            pe.wait_ge(ln1_kept, NG)

            def attention(L, a):
                w = w_att[L.layer]

                def make_k(g, par):
                    if L.layer == 0:
                        pe.wait_ge(a.ct_in, 16 * g + 16)
                        src = ctg[:, :]
                    else:
                        src = KNT[:, span(g * GTOK, GTOK)]
                    need(pe, lg_kept if L.layer == 0 else oN_kept, g - 1)
                    need(pe, a.v_kept, GT * g)
                    nc.tensor.matmul(PS[:, PJ, :], w[:, 1, :], src, start=True, stop=True).then_inc(a.k_ready, 1)

                def make_q(g, par):
                    pe.wait_ge(a.k_kept, g + 1)
                    nc.tensor.matmul(PS[:, PJ, :], w[:, 0, :], XNT[:, span(g * GTOK, GTOK)], start=True, stop=True).then_inc(a.q_ready, 1)

                def make_v(g, par):
                    pe.wait_ge(a.q_kept, L.hl * g + L.hl)
                    pe.wait_ge(a.ct_in, 16 * g + 16)
                    for j in range(GT):
                        last = nc.tensor.matmul(PS[:, PJ, j * P:(j + 1) * P], ctg[:, j * P:(j + 1) * P], w[:, 2, :], start=True, stop=True)
                    last.then_inc(a.v_ready, 1)

                def scores(g, u, par):
                    n = g * L.units + u
                    if u == 0:
                        pe.wait_ge(a.q_kept, L.hl * g + L.hl)
                        pe.wait_ge(a.k_kept, g + 1)
                    need(pe, a.shifted if L.layer == 0 else a.clipped, n - 1)
                    if L.layer == 0:
                        stand(pe)
                    for a2 in range(2):
                        q = 2 * (u % 2) + a2
                        bank = PS[:, S_BANKS + 2 * (u % 2) + a2, 0:256]
                        if L.layer == 0:
                            m = mask_rows[:, span(g * GTOK + (u // 2) * P, P)]
                            nc.tensor.matmul(bank.rearrange("p (c k) -> p c k", c=2), win_ub[:, :],
                                             m.unsqueeze(1).broadcast_to([MROWS, 2, P]), start=True, stop=False, skip_group_check=True)
                    for c in range(2):
                        for b2 in range(2):
                            for a2 in range(2):
                                q = 2 * (u % 2) + a2
                                j, h = L.slot(u, c)
                                o = (2 * c + b2) * S
                                last = nc.tensor.matmul(
                                    PS[:, S_BANKS + 2 * (u % 2) + a2, o:o + S],
                                    Qz[32 * q:32 * q + 32, par, 2 * j + b2, h:h + 2, :],
                                    KTb[32 * q:32 * q + 32, par, (2 * j + b2) * S:(2 * j + b2 + 1) * S],
                                    start=L.layer == 1, stop=True, skip_group_check=True)
                    last.then_inc(a.scores, 1)

                def turn(g, u):
                    n = g * L.units + u
                    pe.wait_ge(a.normed, n + 1)
                    need(pe, a.pt_kept, n)
                    for i in range(4):
                        last = nc.tensor.transpose(PS[:, PT_BANK, i * P:(i + 1) * P], Pr[:, u % 4, i * P:(i + 1) * P], ident[:, :])
                    last.then_inc(a.pt_ready, 1)

                def weigh(g, u, par):
                    n = g * L.units + u
                    if u == 0:
                        pe.wait_ge(a.v_kept, GT * g + GT)
                        need(pe, a.o_kept, g)
                    pe.wait_ge(vz_zero, 2)
                    pe.wait_ge(a.pt_kept, n + 1)
                    stand(pe)
                    for c in range(2):
                        for b2 in range(2):
                            for a2 in range(2):
                                q = 2 * (u % 2) + a2
                                j, h0 = L.slot(u, c)
                                o = j * S
                                hs = [0, 1] if L.layer == 1 else [2 * c, 2 * c + 1]
                                for h in hs:
                                    t = (2 * a2 + c) * P + (h % 2) * S
                                    first = h == 0
                                    final = h == L.hl - 1
                                    last = nc.tensor.matmul(
                                        PS[32 * q:32 * q + 32, O_BANKS + b2, o:o + S],
                                        Vz[L.layer][64 * b2:64 * b2 + 64, par, j, h * P + 32 * q:h * P + 32 * q + 32],
                                        PT[64 * b2:64 * b2 + 64, u % 2, t:t + S],
                                        start=first, stop=final, skip_group_check=True)
                    last.then_inc(a.pv, 1)

                def body(g, par, prev, cur, nxt):
                    for u in range(L.units):
                        if nxt and u == 0:
                            make_k(g + 1, 1 - par)
                        if nxt and u == 1:
                            make_q(g + 1, 1 - par)
                        if u + 2 < L.units:
                            if cur:
                                scores(g, u + 2, par)
                        elif nxt:
                            scores(g + 1, u + 2 - L.units, 1 - par)
                        if u >= 1:
                            if cur:
                                turn(g, u - 1)
                        elif prev:
                            turn(g - 1, L.units - 1)
                        if u >= 2:
                            if cur:
                                weigh(g, u - 2, par)
                        elif prev:
                            weigh(g - 1, L.units - 2 + u, 1 - par)
                        if nxt and u == 2:
                            make_v(g + 1, 1 - par)
                        if L.layer == 0 and prev and u == 3:
                            pe.wait_ge(a.o_kept, g)
                            if nxt:
                                pe.wait_ge(a.v_kept, GT * (g + 2))
                            else:
                                pe.wait_ge(lg_kept, g)
                            for j in range(GT):
                                nc.tensor.matmul(PS[:, PJ, j * P:(j + 1) * P], ones_row[:, :], bo_row[:, :], start=True, stop=False, skip_group_check=True)
                                last = nc.tensor.matmul(PS[:, PJ, j * P:(j + 1) * P], OTs[:, j * P:(j + 1) * P], w[:, 3, :], start=False, stop=True, skip_group_check=True)
                            last.then_inc(proj_ready, 1)
                        if L.layer == 0 and prev and u == 6:
                            pe.wait_ge(ln2.done, GT * g)
                            pe.wait_ge(x1_ready, g)
                            transpose4(PJ, xn, x2T_ready)
                        if L.layer == 0 and prev and u == 7:
                            pe.wait_ge(x2T_kept, g)
                            for j in range(GT):
                                last = nc.tensor.matmul(PS[:, PJ, j * E0:(j + 1) * E0], xnT[:, j * P:(j + 1) * P], gw[:, :], start=True, stop=True)
                            last.then_inc(lg_ready, 1)
                        if L.layer == 1 and prev and u == 3:
                            pe.wait_ge(a.o_kept, g)
                            if nxt:
                                pe.wait_ge(a.v_kept, GT * (g + 2))
                            else:
                                pe.wait_ge(oN_kept, g)
                            for j in range(GT):
                                last = nc.tensor.transpose(PS[:, PJ, j * P:(j + 1) * P], OTs[:, j * P:(j + 1) * P], ident[:, :])
                            last.then_inc(oT_ready, 1)
                bodies(pe, body, NG)

            attention(Att(0), a0)

            pe.wait_ge(comb_ready, 1)
            pe.wait_ge(lg_kept, NG + 1)
            for t in range(NT):
                last = nc.tensor.transpose(PS[0:3 * E0, t // 8, (t % 8) * 64:(t % 8 + 1) * 64].bitcast(BF16), comb3[:, t, :], identb[:, :])
            last.then_inc(combT_ready, 1)
            pe.wait_ge(combT_kept, 4)
            pe.wait_ge(x2T_spread, NG)

            def experts0(g, par, prev, cur, nxt):
                def up(g, s, buf):
                    n = g * ITEMS + s
                    cols_ = P if s < PAIRS else INTER
                    tokens = X2T[:, span(g * GTOK, GTOK)]
                    need(pe, silu_done, n - 1)
                    need(pe, hid_done, n - 1)
                    if s == PAIRS:
                        stand(pe)
                    nc.tensor.matmul(PS[0:cols_, A_BANK + buf, :], w_gate[:, s * P:s * P + cols_], tokens, start=True, stop=True).then_inc(a_ready, 1)
                    if s < PAIRS:
                        nc.tensor.matmul(PS[:, C_BANK + buf, :], sel3[:, s * P:(s + 1) * P], combT[:, span(g * GTOK, GTOK)], start=True, stop=True)
                    nc.tensor.matmul(PS[0:cols_, B_BANK + buf, :], w_up[:, s * P:s * P + cols_], tokens, start=True, stop=True).then_inc(b_ready, 1)

                def down(g, s, buf):
                    n = g * ITEMS + s
                    rows = P if s < PAIRS else INTER
                    pe.wait_ge(hid_done, n + 1)
                    if s == 0:
                        need(pe, x2_ready, g)
                    for j in range(GT):
                        last = nc.tensor.matmul(PS[:, Y_BANK, j * P:(j + 1) * P], hid[0:rows, buf, j * P:(j + 1) * P], w_down[0:rows, s, :],
                                                start=(s == 0 and j == 0), stop=(s == PAIRS), skip_group_check=True)
                    last.then_inc(down_done, 1)
                    if s == PAIRS:
                        pe.wait_ge(down_done, n + 1)
                        pe.sem_inc(y_ready, 1)

                for s in range(ITEMS):
                    if s + 1 < ITEMS:
                        if cur:
                            up(g, s + 1, (s + 1 + par) % 2)
                    elif nxt:
                        up(g + 1, 0, (1 - par) % 2)
                    if cur:
                        down(g, s, (s + par) % 2)
                    if prev and s == 5:
                        pe.wait_ge(ln3b.done, GT * g)
                        if not cur:
                            pe.wait_ge(kT_kept, g - 1)
                        transpose4(T_BANK, xn, qT_ready)
                    if prev and s == 8:
                        pe.wait_ge(ln_ctx.done, GT * g)
                        pe.wait_ge(qT_kept, g)
                        transpose4(T_BANK, xm, kT_ready)
            bodies(pe, experts0, NG)
            pe.wait_ge(qT_kept, NG)
            pe.wait_ge(kT_kept, NG)
            pe.wait_ge(x2_ready, NG)
            attention(Att(1), a1)
            pe.wait_ge(oN_kept, NG + 1)

            def layer1_tail(g, par, prev, cur, nxt):
                if cur:
                    pe.wait_ge(onT_kept, g + 1)
                    need(pe, gelu_o, g)
                    for j in range(GT):
                        last = nc.tensor.matmul(PS[:, 1, j * P:(j + 1) * P], onT[:, j * P:(j + 1) * P], w_att[1][:, 3, :], start=True, stop=True)
                    last.then_inc(wo_ready, 1)
                if nxt:
                    pe.wait_ge(on_ready, g + 2)
                    for j in range(GT):
                        last = nc.tensor.transpose(PS[:, 0, j * P:(j + 1) * P], on[:, 1 - par, j, :], ident[:, :])
                    last.then_inc(onT_ready, 1)
                if prev:
                    pe.wait_ge(ln4.done, GT * g)
                    transpose4(2, xm, xe_T)
                    pe.wait_ge(xe_T_kept, g)
                    for j in range(GT):
                        last = nc.tensor.matmul(PS[:, 3, j * E1:(j + 1) * E1], xnT[:, j * P:(j + 1) * P], wr[:, :], start=True, stop=True)
                    last.then_inc(lg1_ready, 1)
            bodies(pe, layer1_tail, NG)

            pe.wait_ge(diff_ready, 1)
            pe.wait_ge(lg1_kept, NG)
            flat = chosenb[:, :, :].rearrange("p e t -> p (e t)")
            nc.tensor.matmul(PS[:, 0, 0:NT * E1], beforeb[:, :], flat, start=True, stop=True)
            nc.tensor.matmul(PS[:, 1, 0:NT * E1], onesb[:, :], flat, start=True, stop=True).then_inc(ranks_ready, 1)
            pe.wait_ge(slots_ready, 1)

            def expert_tiles(k, par, prev, cur, nxt):
                if cur:
                    pe.wait_ge(xsT_kept, k + 1)
                    pe.wait_ge(w1_in[par], sixteens(k, par))
                    for c in range(CH):
                        last = nc.tensor.matmul(PS[:, 2 * par + c // 2, (c % 2) * ST:(c % 2 + 1) * ST],
                                                w1[:, par, c * P:(c + 1) * P], xsT[:, par, :], start=True, stop=True)
                    last.then_inc(up_ready, 1)
                if nxt:
                    pe.wait_ge(xs_in[1 - par], sixteens(k + 1, 1 - par))
                    need(pe, xsT_kept, k + 1)
                    for h in range(ST // P):
                        last = nc.tensor.transpose(PS[:, 4, h * P:(h + 1) * P], xs[:, 1 - par, h, :], ident[:, :])
                    last.then_inc(xsT_ready, 1)
                if prev:
                    pe.wait_ge(gelued, CH * k)
                    pe.wait_ge(w2_in[1 - par], sixteens(k - 1, 1 - par))
                    if not cur:
                        pe.wait_ge(y_kept, k - 2)
                    for h in range(ST // P):
                        for c in range(CH):
                            last = nc.tensor.matmul(PS[:, 5 + (1 - par), h * P:(h + 1) * P], hx[:, 1 - par, c, h * P:(h + 1) * P],
                                                    w2[:, 1 - par, c * P:(c + 1) * P], start=(c == 0), stop=(c == CH - 1))
                    last.then_inc(down_ready, 1)
            bodies(pe, expert_tiles, NST)


def kernel(**inputs):
    import numpy as _np
    import concourse.bacc as _bacc
    from concourse import mybir as _mybir
    from concourse.bass_utils import run_bass_kernel_spmd as _run

    def f(name):
        return _np.asarray(inputs[name])

    arrays = {
        "x": f("x").reshape(TOK, D),
        "ctx": f("ctx_1024").reshape(TOK, D),
        "ctxT": f("ctx_1024").reshape(TOK, D).T,
        "mask": f("mask_BxS2_ff0"),
        "L0_wq": f("L0_xattn_wq"), "L0_wk": f("L0_xattn_wk"), "L0_wv": f("L0_xattn_wv"), "L0_wo": f("L0_xattn_wo"),
        "L0_bq": f("L0_xattn_bq")[:, None], "L0_bk": f("L0_xattn_bk")[:, None], "L0_bv": f("L0_xattn_bv")[:, None],
        "L0_bo": f("L0_xattn_bo")[None, :],
        "pre_g": f("L1_xattn_pre_g")[:, None], "pre_b": f("L1_xattn_pre_b")[:, None],
        "gate_w": f("L0_ffn_gate_w").T,
        "gate_b": _np.broadcast_to(f("L0_ffn_gate_b"), (P, E0)),
        "L1_Wq": f("L1_xattn_Wq"), "L1_Wk": f("L1_xattn_Wk"), "L1_Wv": f("L1_xattn_Wv"), "L1_Wo": f("L1_xattn_Wo"),
        "ln_gb": _np.broadcast_to(_np.stack([f("L1_xattn_ln_g"), f("L1_xattn_ln_b")]), (P, 2, D)),
        "w_gate": _np.concatenate([f("L0_ffn_w13")[:, :INTER], f("L0_ffn_w13_s")[None, :INTER]]).transpose(2, 0, 1).reshape(D, -1),
        "w_up": _np.concatenate([f("L0_ffn_w13")[:, INTER:], f("L0_ffn_w13_s")[None, INTER:]]).transpose(2, 0, 1).reshape(D, -1),
        "w_down": _np.concatenate([f("L0_ffn_w2"), f("L0_ffn_w2_s")[None], _np.zeros((1, D, INTER), _np.float32)])
                     .reshape(ITEMS, 2, D, INTER).transpose(1, 3, 0, 2).reshape(P, ITEMS, D),
        "Wr": f("L1_ffn_Wr"),
        "w1": _np.concatenate([f("L1_ffn_W1"), f("L1_ffn_b1").reshape(E1, CH, P).transpose(0, 2, 1)], 2),
        "w2": _np.concatenate([f("L1_ffn_W2").reshape(E1, CH, P, D).transpose(0, 2, 1, 3).reshape(E1, P, CH * D),
                               _np.broadcast_to(f("L1_ffn_b2")[:, None, :], (E1, P, D))], 2),
        **constants(),
    }
    nc = _bacc.Bacc("TRN2", target_bir_lowering=False, num_devices=1)
    aps, given = {}, {}
    for name, a in arrays.items():
        a = _np.ascontiguousarray(a)
        given[f"in_{name}"] = a
        aps[name] = nc.dram_tensor(f"in_{name}", a.shape, _mybir.dt.from_np(a.dtype), kind="ExternalInput").ap()
    out = nc.dram_tensor("out_x", (TOK, D), F32, kind="ExternalOutput").ap()
    program(nc, aps, out)
    r = _run(nc, [given], core_ids=[0])
    return r.results[0]["out_x"].reshape(B, S, D)
```

```python
from contextlib import ExitStack

import concourse.bass as bass
from concourse import mybir
import numpy as np

F32 = mybir.dt.float32
BF16 = mybir.dt.bfloat16
I32 = mybir.dt.int32
U32 = mybir.dt.uint32
ALU = mybir.AluOpType
ACT = mybir.ActivationFunctionType
AX = mybir.AxisListType

P = 128
D = 128
B, S = 64, 64
TOK = B * S
NT = TOK // P
GT = 4
NG = NT // GT
GTOK = GT * P
EPS = 1e-5
NEWTON = 3
ROOT_STEPS = 3 + 3 * NEWTON

H0, H1 = 16, 8
WINDOW, GLOBAL = 32, 16
RANKS = S - WINDOW - 1 - GLOBAL
NEG = -3.3895313892515355e38
MROW = 32
MPARTS = 2 * 3

E0, K0, INTER = 16, 4, 64
ROUTE_SCALE = 2.5
PAIRS = E0 // 2
ITEMS = PAIRS + 1

E1, HID = 8, 512
CH = HID // P
ST = 256
NST = TOK * 2 // ST + E1 - 1
NSLOT = NST * ST
WPACK = HID + HID + CH + D


def constants():
    p = np.arange(P)
    dk0, dk1 = D // H0, D // H1
    own0, own1 = ((p[:, None] // (D // h) == np.arange(h)[None, :]).astype(np.float32) for h in (H0, H1))
    s = np.arange(S)
    u = np.zeros((P, 2, S), np.float32)
    v = np.zeros((MROW, S), np.float32)
    for r in range(RANKS):
        u[r] = (s >= GLOBAL + WINDOW + 1 + r)
        v[r] = NEG * (s == GLOBAL + r)
        u[RANKS + r] = s == GLOBAL + r
        v[RANKS + r] = NEG * (s >= GLOBAL + WINDOW + 1 + r)
    for b2 in range(2):
        u[MROW + 3 * b2:MROW + 3 * b2 + 3, b2] = 1.0
    sel3 = np.zeros((3, E0, PAIRS, 2, INTER), np.float32)
    for e in range(E0):
        sel3[:, e, e // 2, e % 2] = 1.0
    reset0 = np.ones((P, NT, E0), np.float32)
    reset0[:, :, 0] = 0.0
    reset1 = np.ones((P, NT, E1), np.float32)
    reset1[:, :, 0] = 0.0
    reset_t = np.ones((P, E1, NT), np.float32)
    reset_t[:, :, 0] = 0.0
    return {
        "c_ident": np.eye(P, dtype=np.float32),
        "c_own0": own0, "c_own1": own1, 
        "c_side": (p[:, None] // S == np.arange(2)[None, :]).astype(np.float32),
        "c_win_u": u.reshape(P, P),
        "c_win_v": v,
        "c_sel3": sel3.reshape(3 * E0, PAIRS * P),
        "c_before": (p[:, None] < p[None, :]).astype(np.float32),
        "c_reset0": reset0.reshape(P, NT * E0),
        "c_reset1": reset1.reshape(P, NT * E1),
        "c_reset_t": reset_t.reshape(P, E1 * NT),
        "c_steps": np.broadcast_to(ST * np.arange(TOK // ST, dtype=np.float32), (P, TOK // ST)).copy(),
        "c_tile": np.arange(NST, dtype=np.float32)[None, :].copy(),
    }


class Att:

    def __init__(self, layer):
        self.layer = layer
        self.heads = H0 if layer == 0 else H1
        self.dk = D // self.heads
        self.scale = float(np.float32(self.dk ** -0.5 if layer == 0 else D ** -0.5))
        self.parts = self.heads // 8
        self.units = GT * self.parts
        self.key_bufs = 4 // self.parts
        self.values_at = 5 if layer == 0 else 2
        self.lag = 1 if layer == 0 else 3
        self.ahead = 4 if layer == 0 else 3


def need(eng, sem, value):
    if isinstance(value, int) and value <= 0:
        return
    eng.wait_ge(sem, value)


def bodies(eng, body, count, lag=1):
    def peeled(g):
        body(g, g % 2, sum(0 <= g - k < count for k in (2, 3) if k <= lag), *(0 <= g + k < count for k in (-1, 0, 1)))

    pairs = (count - 1 - lag) // 2
    for g in range(-1, lag):
        peeled(g)
    with eng.Fori(0, pairs) as i:
        for k in range(2):
            body(2 * i + lag + k, (lag + k) % 2, lag - 1, True, True, True)
    for g in range(lag + 2 * pairs, count + lag):
        peeled(g)


def here(g):
    return not isinstance(g, int) or 0 <= g < NG


def sixteens(k, parity):
    return 8 * (k + 2 - parity)


def span(start, size):
    return slice(start, start + size) if isinstance(start, int) else bass.ds(start, size)


def program(nc, d, out, stop=9):
    with ExitStack() as ctx:
        def sb(name, shape, dt=F32):
            return ctx.enter_context(nc.sbuf_tensor(name, shape, dt))

        def sem(name):
            return ctx.enter_context(nc.semaphore(name))

        PS = ctx.enter_context(nc.psum_tensor("PS", [P, 8, 512], F32))
        X = sb("X", [P, NT, D])
        CN = sb("CN", [P, NT, D])
        XNT = sb("XNT", [P, TOK])
        X2T = sb("X2T", [P, TOK])
        KNT = sb("KNT", [P, TOK])
        ctg = sb("ctg", [P, GTOK])
        mask_rows = sb("mask_rows", [P, NT * S], BF16)
        combT = sb("combT", [3 * E0, TOK], BF16)
        QT = sb("QT", [P, 2, GTOK])
        KTb = sb("KTb", [P, 2, GTOK])
        keys = sb("keys", [P, 4 * 2 * 8 * S])
        scratch = sb("scratch", [P, 2 * CH * ST + 6 * ST])
        V2 = scratch[:, 0:2 * 8 * D].rearrange("p (a b d) -> p a b d", a=2, b=8)
        Pr = sb("Pr", [P, 4, 512])
        PT = sb("PT", [P, 2, 512])
        OTs = sb("OTs", [P, GTOK])
        mx = sb("mx", [P, 2, 8])
        sums = sb("sums", [P, 2, GT * H0])
        rsum = sb("rsum", [P, 2, GT * H0])
        xn = sb("xn", [P, GT, D])
        xm = sb("xm", [P, GT, D])
        xnT = sb("xnT", [P, GTOK])
        stats = sb("stats", [P, GT, 6])
        mv = sb("mv", [P, 2 * GT, 2])
        rstd = sb("rstd", [P, 2 * GT])
        var_eps = sb("var_eps", [P, 2 * GT])
        root_t = sb("root_t", [P, 2 * GT])
        mv_all = sb("mv_all", [P, NT, 2])
        rstd_all = sb("rstd_all", [P, NT])
        var_all = sb("var_all", [P, NT])
        root_all = sb("root_all", [P, NT])
        LG = sb("LG", [P, NT, E0])
        w_att = [sb(f"w_att{l}", [P, 4, D]) for l in range(2)]
        cols = sb("cols", [P, 8])
        bq_s = sb("bq_s", [P, 1])
        bo_row = sb("bo_row", [1, D])
        ones_row = sb("ones_row", [1, P])
        ident = sb("ident", [P, P])
        identb = sb("identb", [P, P], BF16)
        own = [sb(f"own{l}", [P, h]) for l, h in enumerate((H0, H1))]
        side = sb("side", [P, 2])
        win_u = sb("win_u", [P, P])
        win_ub = sb("win_ub", [P, P], BF16)
        win_v = sb("win_v", [MROW, S])
        mask_in = sb("mask_in", [B, S])
        mask_left = sb("mask_left", [B, S])
        mask_part = sb("mask_part", [B, 3, S], BF16)
        gw = sb("gw", [P, E0])
        gb = sb("gb", [P, E0])
        BQ, BK, BV, PG, PB = range(5)
        w_gate = sb("w_gate", [P, ITEMS * P - INTER])
        w_up = sb("w_up", [P, ITEMS * P - INTER])
        w_down = sb("w_down", [P, ITEMS, D])
        sel3 = sb("sel3", [3 * E0, PAIRS * P], BF16)
        comb3 = sb("comb3", [P, NT, 3 * E0], BF16)
        reset0 = sb("reset0", [P, NT * E0])
        top8 = sb("top8", [P, NT, 8])
        left = sb("left", [P, NT])
        on = sb("on", [P, 2, GT, D])
        onT = sb("onT", [P, GTOK])
        ln_gb = sb("ln_gb", [P, 2, D])
        wr = sb("wr", [P, E1])
        reset1 = sb("reset1", [P, NT * E1])
        reset_t = sb("reset_t", [P, NT * E1])
        steps = sb("steps", [P, TOK // ST])
        tile_no = sb("tile_no", [1, NST])
        before = sb("before", [P, P])
        beforeb = sb("beforeb", [P, P], BF16)
        onesb = sb("onesb", [P, P], BF16)
        zero = sb("zero", [P, D])
        chosenb = sb("chosenb", [P, E1, NT], BF16)
        count = sb("count", [P, 4, E1])
        expert = sb("expert", [1, NST], I32)
        slot = sb("slot", [P, 2, NT], U32)
        slot_f = sb("slot_f", [P, 2, NT])
        weight = sb("weight", [P, 2, NT])
        OA = X2T[:, 0:2 * GTOK].rearrange("p (a t d) -> p a t d", a=2, t=GT)
        XE = CN
        got = [XNT[:, :].rearrange("p (t d) -> p t d", t=NT), X2T[:, :].rearrange("p (t d) -> p t d", t=NT)]
        q_flat = keys
        silu = q_flat[:, 0:2 * GTOK].rearrange("p (a s) -> p a s", a=2)
        hid = q_flat[:, 2 * GTOK:4 * GTOK].rearrange("p (a s) -> p a s", a=2)
        gated = q_flat[:, 4 * GTOK:6 * GTOK].rearrange("p (a s) -> p a s", a=2)
        W1N, W2N = HID + CH, HID + D
        w1 = q_flat[:, 0:2 * W1N].rearrange("p (a n) -> p a n", a=2)
        w2 = q_flat[:, 2 * W1N:2 * (W1N + W2N)].rearrange("p (a n) -> p a n", a=2)
        v_flat = scratch
        hx = v_flat[:, 0:2 * CH * ST].rearrange("p (a c s) -> p a c s", a=2, c=CH)
        o = 2 * CH * ST
        xs = v_flat[:, o:o + 2 * ST].rearrange("p (a h d) -> p a h d", a=2, d=D)
        xsT = v_flat[:, o + 2 * ST:o + 4 * ST].rearrange("p (a s) -> p a s", a=2)
        ys = v_flat[:, o + 4 * ST:o + 6 * ST].rearrange("p (a h d) -> p a h d", a=2, d=D)
        XS = nc.dram_tensor("sorted_tokens", (NSLOT, D), F32, kind="Internal").ap()
        YS = nc.dram_tensor("sorted_results", (NSLOT, D), F32, kind="Internal").ap()

        x_in, cn_in, w_in, mask_in_s, mask_spread = map(sem, ("x_in", "cn_in", "w_in", "mask_in_s", "mask_spread"))
        const_ready, mask_zero, mask_cut, mask_fill = map(sem, ("const_ready", "mask_zero", "mask_cut", "mask_fill"))
        bqs_ready, mask_clamped = map(sem, ("bqs_ready", "mask_clamped"))

        stood = {}

        def stand(eng):
            name = type(eng).__name__
            if name not in stood:
                stood[name] = sem(f"stood_{len(stood)}")
            eng.sem_inc(stood[name], 1)

        class Norm:
            def __init__(self, name, own_done=True):
                self.stats, self.aggr, self.rstd = (sem(f"{name}_{x}") for x in ("stats", "aggr", "rstd"))
                self.done = sem(f"{name}_done") if own_done else None

        def norm_stats(dve, ln, g, src, moments=None):
            moments = mv[:, 0:GT, :] if moments is None else moments
            stand(dve)
            for j in range(GT):
                nc.vector.bn_stats(stats[:, j, :], src[j]).then_inc(ln.stats, 1)
            dve.wait_ge(ln.stats, g * GT + GT)
            stand(dve)
            for j in range(GT):
                nc.vector.bn_aggr(moments[:, j, :], stats[:, j, :]).then_inc(ln.aggr, 1)
            dve.wait_ge(ln.aggr, g * GT + GT)

        def root_guess(dve, ln, g, moments, r, v, twice=False):
            step = g * ROOT_STEPS
            scale, offset = (1 + EPS, EPS * EPS) if twice else (1.0, EPS)
            nc.vector.tensor_scalar(v, moments[:, :, 1], scale, offset, ALU.mult, ALU.add).then_inc(ln.rstd, 1)
            dve.wait_ge(ln.rstd, step + 1)
            nc.vector.tensor_scalar(r.bitcast(I32), v.bitcast(I32), 1, None, ALU.logical_shift_right).then_inc(ln.rstd, 1)
            dve.wait_ge(ln.rstd, step + 2)
            nc.vector.tensor_scalar(r.bitcast(I32), r.bitcast(I32), -1.0, float(0x5f3759df), ALU.mult, ALU.add).then_inc(ln.rstd, 1)
            dve.wait_ge(ln.rstd, step + 3)

        def root_newton(dve, ln, g, i, r, v, t):
            step = g * ROOT_STEPS + 3 + 3 * i
            nc.vector.tensor_tensor(t, r, r, ALU.mult).then_inc(ln.rstd, 1)
            dve.wait_ge(ln.rstd, step + 1)
            nc.vector.scalar_tensor_tensor(out=t, in0=t, scalar=-0.5, in1=v, op0=ALU.mult, op1=ALU.mult).then_inc(ln.rstd, 1)
            dve.wait_ge(ln.rstd, step + 2)
            nc.vector.scalar_tensor_tensor(out=r, in0=t, scalar=1.5, in1=r, op0=ALU.add, op1=ALU.mult).then_inc(ln.rstd, 1)
            dve.wait_ge(ln.rstd, step + 3)

        def norm_apply(dve, ln, g, src, dst, moments=None, r=None):
            moments = mv if moments is None else moments
            r = rstd if r is None else r
            for j in range(GT):
                nc.vector.tensor_scalar(dst[j], src[j], moments[:, j, 0:1], r[:, j:j + 1],
                                        ALU.subtract, ALU.mult).then_inc(ln.done, 1)

        def tiles4(t, g):
            return [t[:, g * GT + j, :] for j in range(GT)]

        def local4(t):
            return [t[:, j, :] for j in range(GT)]

        ln1 = Norm("ln1")
        ln1_T, ln1_kept = sem("ln1_T"), sem("ln1_kept")

        class AttSems:
            def __init__(self, l):
                self.k_ready, self.q_ready, self.v_ready, self.k_kept, self.q_kept = (
                    sem(f"{n}{l}") for n in ("k_ready", "q_ready", "v_ready", "k_kept", "q_kept"))
                self.v_kept, self.ct_in, self.scores, self.maxed, self.clipped = (
                    sem(f"{n}{l}") for n in ("v_kept", "ct_in", "scores", "maxed", "clipped"))
                self.shifted, self.exped, self.summed, self.recip, self.spread = (
                    sem(f"{n}{l}") for n in ("shifted", "exped", "summed", "recip", "spread"))
                self.pt_ready, self.pt_kept, self.pv, self.o_kept = (
                    sem(f"{n}{l}") for n in ("pt_ready", "pt_kept", "pv", "o_kept"))

        att_sems = [AttSems(0), AttSems(1)]
        a0, a1 = att_sems
        proj_ready, x1_ready, x2T_ready, x2T_kept, x2T_spread, lg_ready, lg_kept = map(
            sem, ("proj_ready", "x1_ready", "x2T_ready", "x2T_kept", "x2T_spread", "lg_ready", "lg_kept"))
        ln2 = Norm("ln2")
        oT_ready, oT_kept = sem("oT_ready"), sem("oT_kept")
        out_done = sem("out_done")
        sig_done, gate_step, comb_ready, combT_ready, combT_kept = map(sem, ("sig_done", "gate_step", "comb_ready", "combT_ready", "combT_kept"))
        a_ready, b_ready, silu_done, gated_done, hid_done, down_done, y_ready, x2_ready = map(
            sem, ("a_ready", "b_ready", "silu_done", "gated_done", "hid_done", "down_done", "y_ready", "x2_ready"))
        ln3, ln_ctx = Norm("ln3", False), Norm("ln_ctx")
        ctx_moments = ln_ctx.done
        q_centred, q_normed, k_centred, k_normed = map(sem, ("q_centred", "q_normed", "k_centred", "k_normed"))
        qT_ready, qT_kept, kT_ready, kT_kept = map(sem, ("qT_ready", "qT_kept", "kT_ready", "kT_kept"))
        ln_o, ln4 = Norm("ln_o"), Norm("ln4", False)
        xe_centred, xe_normed = sem("xe_centred"), sem("xe_normed")
        scaled, on_ready, onT_ready, onT_kept, wo_ready, gelu_o, x_on, x3_ready = map(
            sem, ("scaled", "on_ready", "onT_ready", "onT_kept", "wo_ready", "gelu_o", "x_on", "x3_ready"))
        xe_T, xe_T_kept, xe_kept, lg1_ready, lg1_kept = map(sem, ("xe_T", "xe_T_kept", "xe_kept", "lg1_ready", "lg1_kept"))
        xs_zeroed, route_step, ranks_ready, diff_ready, exp_ready, slots_ready, scattered = map(
            sem, ("xs_zeroed", "route_step", "ranks_ready", "diff_ready", "exp_ready", "slots_ready", "scattered"))
        w1_in, w2_in, xs_in, y_out = ([sem(f"{n}{i}") for i in range(2)] for n in ("w1_in", "w2_in", "xs_in", "y_out"))
        xsT_ready, xsT_kept, up_ready, gelued, down_ready, y_kept = map(
            sem, ("xsT_ready", "xsT_kept", "up_ready", "gelued", "down_ready", "y_kept"))
        gathered = [sem(f"gathered{g}") for g in range(NG)]
        half_done, x4_ready = sem("half_done"), sem("x4_ready")
        zero_ready = sem("zero_ready")

        S_BANKS, PT_BANK, LG_BANK, O_BANKS, PJ, PJ2 = 0, 2, 3, 4, 6, 7

        x_dram = d["x"].rearrange("(t p) d -> p t d", p=P)
        cn_dram = d["ctx"].rearrange("(t p) d -> p t d", p=P)
        NW = 18 + 4 + 12
        A_BANK, B_BANK, C_BANK, Y_BANK, T_BANK = 0, 2, 4, 6, 7

        def key_blocks(L, j):
            n = 2 * L.heads * S
            at = j % L.key_bufs * n
            return keys[:, at:at + n].rearrange("p (b h k) -> p b h k", b=2, h=L.heads)

        block = ctx.enter_context(nc.Block())

        @block.sync
        def _(sp):
            sp.dma_start(X[:, :, :], x_dram).then_inc(x_in, 16)
            for i, name in enumerate(("L0_wq", "L0_wk", "L0_wv", "L0_wo")):
                sp.dma_start(w_att[0][:, i, :], d[name]).then_inc(w_in, 16)
            for i, name in enumerate(("L0_bq", "L0_bk", "L0_bv", "pre_g", "pre_b")):
                sp.dma_start(cols[:, i:i + 1], d[name]).then_inc(w_in, 16)
            sp.dma_start(bo_row[:, :], d["L0_bo"]).then_inc(w_in, 16)
            for l in range(2):
                sp.dma_start(own[l][:, :], d[f"c_own{l}"]).then_inc(w_in, 16)
            sp.dma_start(side[:, :], d["c_side"]).then_inc(w_in, 16)
            sp.dma_start(win_u[:, :], d["c_win_u"]).then_inc(w_in, 16)
            sp.dma_start(win_v[:, :], d["c_win_v"]).then_inc(w_in, 16)
            sp.dma_start(ident[:, :], d["c_ident"]).then_inc(w_in, 16)
            sp.dma_start(gw[:, :], d["gate_w"]).then_inc(w_in, 16)
            sp.dma_start(gb[:, :], d["gate_b"]).then_inc(w_in, 16)
            for i, name in enumerate(("L1_Wq", "L1_Wk", "L1_Wv", "L1_Wo")):
                sp.dma_start(w_att[1][:, i, :], d[name]).then_inc(w_in, 16)
            for t, name in ((w_gate, "w_gate"), (w_up, "w_up"), (reset0, "c_reset0"), (wr, "Wr"), (reset1, "c_reset1"),
                            (reset_t, "c_reset_t"), (steps, "c_steps"), (tile_no, "c_tile"), (before, "c_before")):
                sp.dma_start(t[:, :], d[name]).then_inc(w_in, 16)
            sp.dma_start(w_down[:, :, :], d["w_down"]).then_inc(w_in, 16)
            sp.dma_start(ln_gb[:, :, :], d["ln_gb"]).then_inc(w_in, 16)
            sp.dma_start(Pr[0:3 * E0, 0:2, :].rearrange("p a b -> p (a b)"), d["c_sel3"]).then_inc(w_in, 16)
            sp.dma_start(mask_in[:, :], d["mask"]).then_inc(mask_in_s, 16)
            sp.dma_start(CN[:, :, :], cn_dram).then_inc(cn_in, 16)
            sp.wait_ge(zero_ready, 1)
            sp.dma_start(XS.rearrange("(a p) d -> p a d", p=P),
                         zero[:, :].unsqueeze(1).broadcast_to([P, NSLOT // P, D])).then_inc(xs_zeroed, 16)
            sp.wait_ge(mask_cut, 3)
            sp.wait_ge(mask_fill, 1)
            for i in range(3):
                for b2 in range(2):
                    sp.dma_start(mask_rows[MROW + 3 * b2 + i:MROW + 3 * b2 + i + 1, :].rearrange("o (t k) -> o t k", t=NT),
                                 mask_part[b2:B:2, i, :]).then_inc(mask_spread, 16)

            def load_ct(a):
                def body(g, par, older, prev, cur, nxt):
                    if nxt:
                        need(sp, a.v_ready, g + 1)
                        need(sp, a.k_ready, g + 1)
                        sp.dma_start(ctg[:, :], d["ctxT"][:, span((g + 1) * GTOK, GTOK)]).then_inc(a.ct_in, 16)
                bodies(sp, body, NG)

            load_ct(a0)
            sp.wait_ge(a0.v_ready, NG)
            load_ct(a1)

            sp.wait_ge(scattered, 16 * 2 * NT)
            sp.wait_ge(xs_zeroed, 16)

            def load_tokens(k, buf):
                sp.dma_start(xs[:, buf, :, :], XS[span(k * ST, ST), :].rearrange("(h p) d -> p h d", p=P)).then_inc(xs_in[buf], 16)

            load_tokens(0, 0)
            load_tokens(1, 1)

            def expert_tiles(k, par, older, prev, cur, nxt):
                if cur and (not isinstance(k, int) or k + 2 < NST):
                    sp.wait_ge(xsT_ready, k + 1)
                    load_tokens(k + 2, par)
                if prev:
                    sp.wait_ge(y_kept, k)
                    sp.dma_start(YS[span((k - 1) * ST, ST), :].rearrange("(h p) d -> p h d", p=P), ys[:, 1 - par, :, :]).then_inc(y_out[1 - par], 16)
            for i in range(2):
                sp.sem_inc(y_out[i], 16)
            bodies(sp, expert_tiles, NST)

            for g in range(NG):
                sp.wait_ge(x4_ready, GT * (g + 1))
                sp.dma_start(out.rearrange("(t p) d -> p t d", p=P)[:, g * GT:(g + 1) * GT, :],
                             X[:, g * GT:(g + 1) * GT, :]).then_inc(out_done, 16)
            sp.wait_ge(out_done, 16 * NG)

        @block.gpsimd
        def _(pool):
            nc.gpsimd.memset(ones_row[:, :], 1.0).then_inc(const_ready, 1)
            nc.gpsimd.memset(onesb[:, :], 1.0).then_inc(const_ready, 1)
            nc.gpsimd.memset(zero[:, :], 0.0).then_inc(zero_ready, 1)
            nc.gpsimd.memset(mask_rows[:, :], 0.0).then_inc(mask_zero, 1)
            pool.wait_ge(mask_zero, 1)
            pool.wait_ge(w_in, 16 * NW)
            nc.gpsimd.tensor_copy(mask_rows[0:MROW, :].rearrange("r (t k) -> r t k", t=NT),
                                  win_v[:, :].unsqueeze(1).broadcast_to([MROW, NT, S])).then_inc(mask_fill, 1)

            def attention(L, a):
                def spread(g, j, par):
                    if j == 0:
                        pool.wait_ge(a.k_kept, g + 1)
                    need(pool, a.scores, L.parts * (g * GT + j - L.key_bufs + 1))
                    own_keys = KTb[:, par, j * P:(j + 1) * P].rearrange("p (b k) -> p b k", b=2)
                    for b2 in range(2):
                        nc.gpsimd.tensor_tensor(key_blocks(L, j)[:, b2], own_keys[:, b2, :].unsqueeze(1).broadcast_to([P, L.heads, S]),
                                                own[L.layer][:, :].unsqueeze(2).broadcast_to([P, L.heads, S]), ALU.mult).then_inc(a.spread, 1)

                def body(g, par, older, prev, cur, nxt):
                    for u in range(L.units):
                        if u % L.parts == 0:
                            j = (u + L.ahead) // L.parts
                            if j >= GT and nxt:
                                spread(g + 1, j - GT, 1 - par)
                            elif j < GT and cur:
                                spread(g, j, par)
                        if L.layer == 0 and prev and u == 7:
                            pool.wait_ge(x2T_kept, g)
                            nc.gpsimd.tensor_copy(X2T[:, span((g - 1) * GTOK, GTOK)], xnT[:, :]).then_inc(x2T_spread, 1)
                        if L.layer == 1:
                            after_attention1(g, u, par, older, prev)
                bodies(pool, body, NG, L.lag)

            def after_attention1(g, u, par, older, prev):
                if u == 0 and older and here(g - 2):
                    pool.wait_ge(on_ready, g - 1)
                    x4 = X[:, span((g - 2) * GT, GT), :]
                    stand(pool)
                    nc.gpsimd.tensor_tensor(x4, x4, on[:, par, :, :], ALU.add).then_inc(x_on, 1)
                if u == 3 and prev:
                    gain, offset = (ln_gb[:, i, :].unsqueeze(1).broadcast_to([P, GT, D]) for i in range(2))
                    pool.wait_ge(ln_o.done, GT * g)
                    nc.gpsimd.tensor_tensor(on[:, 1 - par, :, :], xn[:, :, :], gain, ALU.mult).then_inc(scaled, 1)
                    pool.wait_ge(scaled, g)
                    nc.gpsimd.tensor_tensor(on[:, 1 - par, :, :], on[:, 1 - par, :, :], offset, ALU.add).then_inc(on_ready, 1)
                if u == 3 and older and here(g - 2):
                    pool.wait_ge(ln_o.rstd, ROOT_STEPS * g)
                    need(pool, xe_T, g - 2)
                    stand(pool)
                    nc.gpsimd.tensor_tensor(xm[:, :, :], X[:, span((g - 2) * GT, GT), :],
                                            mv[:, GT:2 * GT, 0].unsqueeze(2).broadcast_to([P, GT, D]), ALU.subtract).then_inc(xe_centred, 1)
                    pool.wait_ge(xe_centred, g - 1)
                    nc.gpsimd.tensor_tensor(xm[:, :, :], xm[:, :, :], rstd[:, GT:2 * GT].unsqueeze(2).broadcast_to([P, GT, D]),
                                            ALU.mult).then_inc(xe_normed, 1)
                    pool.wait_ge(xe_normed, g - 1)
                    nc.gpsimd.tensor_copy(XE[:, span((g - 2) * GT, GT), :], xm[:, :, :]).then_inc(xe_kept, 1)

            attention(Att(0), a0)

            def experts0(g, par, older, prev, cur, nxt):
                if prev:
                    pool.wait_ge(ln3.rstd, ROOT_STEPS * g)
                    stand(pool)
                    nc.gpsimd.tensor_tensor(xn[:, :, :], X[:, span((g - 1) * GT, GT), :],
                                            mv[:, 0:GT, 0].unsqueeze(2).broadcast_to([P, GT, D]), ALU.subtract).then_inc(q_centred, 1)
                    pool.wait_ge(q_centred, g)
                    nc.gpsimd.tensor_tensor(xn[:, :, :], xn[:, :, :], rstd[:, 0:GT].unsqueeze(2).broadcast_to([P, GT, D]),
                                            ALU.mult).then_inc(q_normed, 1)
                    pool.wait_ge(kT_ready, g)
                    tiles = span((g - 1) * GT, GT)
                    stand(pool)
                    nc.gpsimd.tensor_tensor(xm[:, :, :], CN[:, tiles, :],
                                            mv_all[:, tiles, 0].unsqueeze(2).broadcast_to([P, GT, D]), ALU.subtract).then_inc(k_centred, 1)
                    pool.wait_ge(k_centred, g)
                    stand(pool)
                    nc.gpsimd.tensor_tensor(xm[:, :, :], xm[:, :, :], rstd_all[:, tiles].unsqueeze(2).broadcast_to([P, GT, D]),
                                            ALU.mult).then_inc(k_normed, 1)
            pool.wait_ge(cn_in, 16)
            pool.wait_ge(ln_ctx.rstd, ROOT_STEPS)
            bodies(pool, experts0, NG)

            attention(Att(1), a1)

            pool.wait_ge(xe_kept, NG)
            pool.wait_ge(xs_zeroed, 16)
            pool.wait_ge(slots_ready, 1)
            for t in range(NT):
                for i in range(2):
                    nc.gpsimd.indirect_dma_start(XS, bass.IndirectOffsetOnAxis(ap=slot[:, i, t:t + 1], axis=0),
                                                 XE[:, t, :], None).then_inc(scattered, 16)

            for i in range(2):
                pool.wait_ge(y_out[i], 16 * ((NST + 1 - i) // 2 + 1))
            for t in range(NT):
                for i in range(2):
                    nc.gpsimd.indirect_dma_start(got[i][:, t, :], None, YS,
                                                 bass.IndirectOffsetOnAxis(ap=slot[:, i, t:t + 1], axis=0)).then_inc(gathered[t // GT], 16)

        @block.vector
        def _(dve):
            dve.wait_ge(w_in, 16 * NW)
            nc.vector.tensor_scalar(bq_s[:, :], cols[:, BQ:BQ + 1], Att(0).scale, None, ALU.mult).then_inc(bqs_ready, 1)
            nc.vector.tensor_copy(win_ub[:, :], win_u[:, :]).then_inc(const_ready, 1)
            nc.vector.tensor_copy(identb[:, :], ident[:, :]).then_inc(const_ready, 1)
            nc.vector.tensor_copy(beforeb[:, :], before[:, :]).then_inc(const_ready, 1)
            nc.vector.tensor_copy(sel3[:, :], Pr[0:3 * E0, 0:2, :].rearrange("p a b -> p (a b)")).then_inc(const_ready, 1)
            dve.wait_ge(mask_in_s, 16)
            nc.vector.tensor_scalar(mask_left[:, :], mask_in[:, :], NEG, None, ALU.max).then_inc(mask_clamped, 1)
            dve.wait_ge(mask_clamped, 1)
            nc.vector.tensor_copy(mask_part[:, 0, :], mask_left[:, :]).then_inc(mask_cut, 1)
            for i in range(1, 3):
                dve.wait_ge(mask_cut, i)
                nc.vector.tensor_tensor(mask_left[:, :], mask_left[:, :], mask_part[:, i - 1, :], ALU.subtract).then_inc(mask_clamped, 1)
                dve.wait_ge(mask_clamped, i + 1)
                nc.vector.tensor_copy(mask_part[:, i, :], mask_left[:, :]).then_inc(mask_cut, 1)

            dve.wait_ge(x_in, 16)

            for g in range(NG):
                norm_stats(dve, ln1, g, tiles4(X, g), mv_all[:, g * GT:(g + 1) * GT, :])
            dve.wait_ge(ln1.aggr, GT * NG)
            root_guess(dve, ln1, 0, mv_all[:, :, :], rstd_all[:, :], var_all[:, :])
            for i in range(NEWTON):
                root_newton(dve, ln1, 0, i, rstd_all[:, :], var_all[:, :], root_all[:, :])
            for g in range(NG):
                if g:
                    dve.wait_ge(ln1_T, g)
                norm_apply(dve, ln1, g, tiles4(X, g), local4(xn), mv_all[:, g * GT:(g + 1) * GT, :], rstd_all[:, g * GT:(g + 1) * GT])
            dve.wait_ge(cn_in, 16)

            def attention(L, a):
                def shift(g, u):
                    n = g * L.units + u
                    dve.wait_ge(a.scores, n + 1)
                    need(dve, a.pt_ready, n - 3)
                    s = PS[:, S_BANKS + u % 2, :].rearrange("p (s k) -> p s k", k=S)
                    pr = Pr[:, u % 4, :].rearrange("p (s k) -> p s k", k=S)
                    m = mx[:, u % 2, :]
                    if L.layer == 1:
                        nc.vector.tensor_scalar(pr, s, -10000.0, 10000.0, ALU.max, ALU.min).then_inc(a.clipped, 1)
                        dve.wait_ge(a.clipped, n + 1)
                        s = pr
                    nc.vector.tensor_reduce(m, s, AX.X, ALU.max).then_inc(a.maxed, 1)
                    dve.wait_ge(a.maxed, n + 1)
                    nc.vector.tensor_tensor(pr, s, m.unsqueeze(2).broadcast_to([P, 8, S]), ALU.subtract).then_inc(a.shifted, 1)

                def total(g, u, par):
                    n = g * L.units + u
                    dve.wait_ge(a.exped, n + 1)
                    nc.vector.tensor_reduce(sums[:, par, 8 * u:8 * u + 8], Pr[:, u % 4, :].rearrange("p (s k) -> p s k", k=S),
                                            AX.X, ALU.add).then_inc(a.summed, 1)

                def body(g, par, older, prev, cur, nxt):
                    for u in range(L.units):
                        if u + 1 < L.units:
                            if cur:
                                shift(g, u + 1)
                        elif nxt:
                            shift(g + 1, 0)
                        if cur:
                            total(g, u, par)
                        if prev and u == 0:
                            dve.wait_ge(a.summed, g * L.units)
                            nc.vector.reciprocal(rsum[:, 1 - par, 0:8 * L.units], sums[:, 1 - par, 0:8 * L.units]).then_inc(a.recip, 1)
                        if prev and u == 1:
                            dve.wait_ge(a.recip, g)
                            dve.wait_ge(a.pv, g * L.units)
                            if L.layer == 0:
                                o = xm[:, :, :].rearrange("p t d -> p (t d)")
                            else:
                                o = OA[:, 1 - par, :, :].rearrange("p t d -> p (t d)")
                            nc.vector.tensor_tensor(o.rearrange("p (h e) -> p h e", e=L.dk),
                                                    PS[:, O_BANKS + 1 - par, :].rearrange("p (h e) -> p h e", e=L.dk),
                                                    rsum[:, 1 - par, 0:8 * L.units].unsqueeze(2).broadcast_to([P, 8 * L.units, L.dk]),
                                                    ALU.mult).then_inc(a.o_kept, 1)
                        if L.layer == 0:
                            after_attention0(g, u, prev, cur)
                        else:
                            after_attention1(g, u, par, older, prev)

                def after_attention0(g, u, prev, cur):
                    if cur and u == 3:
                        norm_stats(dve, ln_ctx, g, tiles4(CN, g), mv[:, GT:2 * GT, :])
                        nc.vector.tensor_copy(mv_all[:, span(g * GT, GT), :], mv[:, GT:2 * GT, :]).then_inc(ctx_moments, 1)
                    if not prev:
                        return
                    if u == 4:
                        dve.wait_ge(proj_ready, g)
                        x4 = X[:, span((g - 1) * GT, GT), :]
                        nc.vector.tensor_tensor(x4, x4, PS[:, PJ, :].rearrange("p (t d) -> p t d", t=GT), ALU.add).then_inc(x1_ready, 1)
                        dve.wait_ge(x1_ready, g)
                        norm_stats(dve, ln2, g - 1, tiles4(X, g - 1))
                    if u == 5:
                        dve.wait_ge(ln2.aggr, GT * g)
                        root_guess(dve, ln2, g - 1, mv[:, 0:GT, :], rstd[:, 0:GT], var_eps[:, 0:GT])
                        root_newton(dve, ln2, g - 1, 0, rstd[:, 0:GT], var_eps[:, 0:GT], root_t[:, 0:GT])
                    if u == 6:
                        for i in range(1, NEWTON):
                            root_newton(dve, ln2, g - 1, i, rstd[:, 0:GT], var_eps[:, 0:GT], root_t[:, 0:GT])
                        norm_apply(dve, ln2, g - 1, tiles4(X, g - 1), local4(xn))
                    if u == 7:
                        dve.wait_ge(lg_ready, g)
                        nc.vector.tensor_copy(LG[:, span((g - 1) * GT, GT), :],
                                              PS[:, LG_BANK, 0:GT * E0].rearrange("p (t e) -> p t e", t=GT)).then_inc(lg_kept, 1)

                def after_attention1(g, u, par, older, prev):
                    if u == 1 and prev:
                        dve.wait_ge(a.o_kept, g)
                        norm_stats(dve, ln_o, g - 1, local4(OA[:, 1 - par, :, :]))
                    if u == 2 and older and here(g - 2):
                        dve.wait_ge(gelu_o, g - 1)
                        dve.wait_ge(x_on, g - 1)
                        x4 = X[:, span((g - 2) * GT, GT), :]
                        nc.vector.tensor_tensor(x4, x4, OTs[:, :].rearrange("p (t d) -> p t d", t=GT), ALU.add).then_inc(x3_ready, 1)
                        dve.wait_ge(x3_ready, g - 1)
                        norm_stats(dve, ln4, g - 2, tiles4(X, g - 2), mv[:, GT:2 * GT, :])
                    if u == 3 and (prev or older and here(g - 2)):
                        lo, hi = (0 if prev else GT), (2 * GT if older and here(g - 2) else GT)
                        if prev:
                            dve.wait_ge(ln_o.aggr, GT * g)
                        if hi > GT:
                            dve.wait_ge(ln4.aggr, GT * (g - 1))
                        root_guess(dve, ln_o, g - 1, mv[:, lo:hi, :], rstd[:, lo:hi], var_eps[:, lo:hi])
                        for i in range(NEWTON):
                            root_newton(dve, ln_o, g - 1, i, rstd[:, lo:hi], var_eps[:, lo:hi], root_t[:, lo:hi])
                        if prev:
                            norm_apply(dve, ln_o, g - 1, local4(OA[:, 1 - par, :, :]), local4(xn))
                bodies(dve, body, NG, L.lag)

            attention(Att(0), a0)

            def chain(s, value, instruction):
                value[0] += 1
                instruction.then_inc(s, 1)
                dve.wait_ge(s, value[0])

            def choose(s, value, v, top, E, K, above, equal, rank, reset):
                for t in range(NT):
                    chain(s, value, nc.vector.max(top[:, t, :], v[:, t, :]))
                least = top[:, :, K - 1].unsqueeze(2).broadcast_to([P, NT, E])
                chain(s, value, nc.vector.tensor_tensor(above, v, least, ALU.is_gt))
                chain(s, value, nc.vector.tensor_tensor(equal, v, least, ALU.is_equal))
                chain(s, value, nc.vector.tensor_reduce(left[:, :], above, AX.X, ALU.add))
                chain(s, value, nc.vector.tensor_scalar(left[:, :], left[:, :], -1.0, float(K), ALU.mult, ALU.add))
                flat = [x.rearrange("p t e -> p (t e)") for x in (rank, equal)]
                chain(s, value, nc.vector.tensor_tensor_scan(flat[0], reset, flat[1], 0.0, ALU.mult, ALU.add))
                chain(s, value, nc.vector.tensor_tensor(rank, rank, left[:, :].unsqueeze(2).broadcast_to([P, NT, E]), ALU.is_le))
                chain(s, value, nc.vector.tensor_tensor(equal, equal, rank, ALU.mult))
                chain(s, value, nc.vector.tensor_tensor(above, above, equal, ALU.add))

            dve.wait_ge(sig_done, 1)
            dve.wait_ge(a0.pt_ready, 8 * NG)
            dve.wait_ge(a0.pv, 8 * NG)
            sig, biased, above, equal = (Pr[:, i, :].rearrange("p (t e) -> p t e", e=E0) for i in range(4))
            rank, w0 = (PT[:, i, :].rearrange("p (t e) -> p t e", e=E0) for i in range(2))
            at = [0]
            chain(gate_step, at, nc.vector.tensor_tensor(biased, sig, gb[:, :].unsqueeze(1).broadcast_to([P, NT, E0]), ALU.add))
            choose(gate_step, at, biased, top8, E0, K0, above, equal, rank, reset0[:, :])
            chain(gate_step, at, nc.vector.tensor_tensor(w0, sig, above, ALU.mult))
            chain(gate_step, at, nc.vector.tensor_reduce(left[:, :], w0, AX.X, ALU.add))
            chain(gate_step, at, nc.vector.reciprocal(left[:, :], left[:, :]))
            chain(gate_step, at, nc.vector.scalar_tensor_tensor(out=w0, in0=w0, scalar=ROUTE_SCALE, in1=left[:, :].unsqueeze(2).broadcast_to([P, NT, E0]),
                                                                op0=ALU.mult, op1=ALU.mult))
            part = [comb3[:, :, i * E0:(i + 1) * E0] for i in range(3)]
            chain(gate_step, at, nc.vector.tensor_copy(part[0], w0))
            chain(gate_step, at, nc.vector.tensor_tensor(w0, w0, part[0], ALU.subtract))
            chain(gate_step, at, nc.vector.tensor_copy(part[1], w0))
            chain(gate_step, at, nc.vector.tensor_tensor(w0, w0, part[1], ALU.subtract))
            nc.vector.tensor_copy(part[2], w0).then_inc(comb_ready, 1)

            dve.wait_ge(ctx_moments, NG)
            root_guess(dve, ln_ctx, 0, mv_all[:, :, :], rstd_all[:, :], var_all[:, :])
            for i in range(NEWTON):
                root_newton(dve, ln_ctx, 0, i, rstd_all[:, :], var_all[:, :], root_all[:, :])

            def experts0(g, par, older, prev, cur, nxt):
                for s in range(ITEMS):
                    n = g * ITEMS + s
                    buf = (s + par) % 2
                    rows = P if s < PAIRS else INTER
                    if prev and s == 0:
                        dve.wait_ge(y_ready, g)
                        x4 = X[:, span((g - 1) * GT, GT), :]
                        nc.vector.tensor_tensor(x4, x4, PS[:, Y_BANK, :].rearrange("p (t d) -> p t d", t=GT), ALU.add).then_inc(x2_ready, 1)
                    if cur:
                        dve.wait_ge(silu_done, n + 1)
                        dve.wait_ge(b_ready, n + 1)
                        need(dve, down_done, n - 1)
                        if s < PAIRS:
                            nc.vector.tensor_tensor(gated[:, buf, :], silu[:, buf, :], PS[:, B_BANK + buf, :], ALU.mult).then_inc(gated_done, 1)
                            dve.wait_ge(gated_done, g * PAIRS + s + 1)
                            nc.vector.tensor_tensor(hid[:, buf, :], gated[:, buf, :], PS[:, C_BANK + buf, :], ALU.mult).then_inc(hid_done, 1)
                        else:
                            nc.vector.tensor_tensor(hid[0:rows, buf, :], silu[0:rows, buf, :], PS[0:rows, B_BANK + buf, :], ALU.mult).then_inc(hid_done, 1)
                    if prev and s == 1:
                        dve.wait_ge(x2_ready, g)
                        norm_stats(dve, ln3, g - 1, tiles4(X, g - 1))
                    if prev and s == 2:
                        dve.wait_ge(ln3.aggr, GT * g)
                        root_guess(dve, ln3, g - 1, mv[:, 0:GT, :], rstd[:, 0:GT], var_eps[:, 0:GT], twice=True)
                        root_newton(dve, ln3, g - 1, 0, rstd[:, 0:GT], var_eps[:, 0:GT], root_t[:, 0:GT])
                    if prev and s == 3:
                        for i in range(1, NEWTON):
                            root_newton(dve, ln3, g - 1, i, rstd[:, 0:GT], var_eps[:, 0:GT], root_t[:, 0:GT])
            bodies(dve, experts0, NG)

            attention(Att(1), a1)

            dve.wait_ge(lg1_kept, NG + 1)
            at = [0]
            N1 = NT * E1
            v, above, equal, rank, first, second = (Pr[:, i // 2, (i % 2) * N1:(i % 2 + 1) * N1].rearrange("p (t e) -> p t e", e=E1) for i in range(6))
            place, rest = (Pr[:, 3, i * N1:(i + 1) * N1].rearrange("p (e t) -> p e t", e=E1) for i in range(2))
            run_t = PT[:, 0, 0:N1].rearrange("p (e t) -> p e t", e=E1)
            prod = PT[:, 0, N1:2 * N1].rearrange("p (t e) -> p t e", e=E1)
            many = PT[:, 1, 0:E1 * (TOK // ST)].rearrange("p (e s) -> p e s", e=E1)

            def step(instruction):
                chain(route_step, at, instruction)

            step(nc.vector.tensor_copy(v, LG[:, :, 0:E1]))
            choose(route_step, at, v, top8, E1, 2, above, equal, rank, reset1[:, :])
            best = top8[:, :, 0].unsqueeze(2).broadcast_to([P, NT, E1])
            step(nc.vector.tensor_tensor(equal, v, best, ALU.is_equal))
            step(nc.vector.tensor_tensor_scan(rank.rearrange("p t e -> p (t e)"), reset1[:, :], equal.rearrange("p t e -> p (t e)"), 0.0, ALU.mult, ALU.add))
            step(nc.vector.tensor_scalar(rank, rank, 1.0, None, ALU.is_le))
            step(nc.vector.tensor_tensor(first, equal, rank, ALU.mult))
            step(nc.vector.tensor_tensor(second, above, first, ALU.subtract))
            step(nc.vector.tensor_copy(chosenb[:, :, :].rearrange("p e t -> p t e"), above))
            nc.vector.tensor_tensor(left[:, :], top8[:, :, 1], top8[:, :, 0], ALU.subtract).then_inc(diff_ready, 1)
            dve.wait_ge(ranks_ready, 1)
            ahead = PS[:, 0, 0:N1].rearrange("p (e t) -> p e t", e=E1)
            totals = PS[:, 1, 0:N1]
            step(nc.vector.tensor_copy(rest.rearrange("p e t -> p (e t)"), totals))
            step(nc.vector.tensor_tensor_scan(run_t.rearrange("p e t -> p (e t)"), reset_t[:, :], rest.rearrange("p e t -> p (e t)"), 0.0, ALU.mult, ALU.add))
            step(nc.vector.tensor_tensor(place, run_t, rest, ALU.subtract))
            step(nc.vector.tensor_tensor(place, place, ahead, ALU.add))
            n_tok = run_t[:, :, NT - 1].unsqueeze(2).broadcast_to([P, E1, TOK // ST])
            step(nc.vector.tensor_tensor(many, n_tok, steps[:, :].unsqueeze(1).broadcast_to([P, E1, TOK // ST]), ALU.is_gt))
            step(nc.vector.tensor_reduce(count[:, 0, :], many, AX.X, ALU.add))
            step(nc.vector.memset(count[:, 3, :], 1.0))
            step(nc.vector.tensor_tensor_scan(count[:, 1, :], count[:, 3, :], count[:, 0, :], 0.0, ALU.mult, ALU.add))
            step(nc.vector.tensor_tensor(count[:, 2, :], count[:, 1, :], count[:, 0, :], ALU.subtract))
            step(nc.vector.tensor_scalar(count[:, 2, :], count[:, 2, :], float(ST), None, ALU.mult))
            step(nc.vector.tensor_tensor(place, place, count[:, 2, :].unsqueeze(2).broadcast_to([P, E1, NT]), ALU.add))
            for i, chosen in enumerate((first, second)):
                step(nc.vector.tensor_tensor(prod, chosen, place.rearrange("p e t -> p t e"), ALU.mult))
                step(nc.vector.tensor_reduce(slot_f[:, i, :], prod, AX.X, ALU.add))
            step(nc.vector.tensor_copy(slot[:, :, :], slot_f[:, :, :]))
            own = PT[0:1, 1, 0:NST * E1].rearrange("p (k e) -> p k e", e=E1)
            step(nc.vector.tensor_tensor(own, count[0:1, 1, :].unsqueeze(1).broadcast_to([1, NST, E1]),
                                         tile_no[:, :].unsqueeze(2).broadcast_to([1, NST, E1]), ALU.is_le))
            owner = PT[0:1, 0, 0:NST]
            step(nc.vector.tensor_reduce(owner, own, AX.X, ALU.add))
            step(nc.vector.tensor_scalar(owner, owner, float(E1 - 1), None, ALU.min))
            nc.vector.tensor_copy(expert[:, :], owner).then_inc(slots_ready, 1)
            dve.wait_ge(exp_ready, 1)
            step(nc.vector.tensor_scalar(slot_f[:, 0, :], weight[:, 1, :], 1.0, None, ALU.add))
            step(nc.vector.reciprocal(weight[:, 0, :], slot_f[:, 0, :]))
            step(nc.vector.tensor_tensor(weight[:, 1, :], weight[:, 1, :], weight[:, 0, :], ALU.mult))

            def expert_tiles(k, par, older, prev, cur, nxt):
                if nxt:
                    dve.wait_ge(xsT_ready, k + 2)
                    need(dve, up_ready, k)
                    nc.vector.tensor_copy(xsT[:, 1 - par, :], PS[:, 4, 0:ST]).then_inc(xsT_kept, 1)
                if prev:
                    dve.wait_ge(down_ready, k)
                    dve.wait_ge(y_out[1 - par], sixteens(k - 1, 1 - par))
                    nc.vector.tensor_tensor(ys[:, 1 - par, :, :], PS[:, 5 + (1 - par), 0:ST].rearrange("p (h d) -> p h d", d=D),
                                            w2[:, 1 - par, HID:HID + D].unsqueeze(1).broadcast_to([P, ST // P, D]), ALU.add).then_inc(y_kept, 1)
            bodies(dve, expert_tiles, NST)

            for t in range(NT):
                if t % GT == 0:
                    dve.wait_ge(gathered[t // GT], 16 * 2 * GT)
                nc.vector.scalar_tensor_tensor(out=X[:, t, :], in0=got[0][:, t, :], scalar=weight[:, 0, t:t + 1], in1=X[:, t, :],
                                               op0=ALU.mult, op1=ALU.add).then_inc(half_done, 1)
                if t >= 1:
                    dve.wait_ge(half_done, t)
                    nc.vector.scalar_tensor_tensor(out=X[:, t - 1, :], in0=got[1][:, t - 1, :], scalar=weight[:, 1, t - 1:t], in1=X[:, t - 1, :],
                                                   op0=ALU.mult, op1=ALU.add).then_inc(x4_ready, 1)
            dve.wait_ge(half_done, NT)
            nc.vector.scalar_tensor_tensor(out=X[:, NT - 1, :], in0=got[1][:, NT - 1, :], scalar=weight[:, 1, NT - 1:NT], in1=X[:, NT - 1, :],
                                           op0=ALU.mult, op1=ALU.add).then_inc(x4_ready, 1)

        @block.scalar
        def _(act):
            def keep_norm(g):
                act.wait_ge(ln1_T, g + 1)
                nc.scalar.activation(XNT[:, span(g * GTOK, GTOK)], PS[:, PT_BANK, :], ACT.Copy).then_inc(ln1_kept, 1)

            keep_norm(0)
            with act.Fori(1, NG) as g:
                keep_norm(g)
            act.wait_ge(w_in, 16 * NW)
            act.wait_ge(bqs_ready, 1)

            def attention(L, a):
                def keep_k(g, par):
                    act.wait_ge(a.k_ready, g + 1)
                    if L.layer == 0:
                        nc.scalar.activation(KTb[:, par, :], PS[:, PJ, :], ACT.Identity, bias=cols[:, BK:BK + 1]).then_inc(a.k_kept, 1)
                    else:
                        nc.scalar.activation(KTb[:, par, :], PS[:, PJ, :], ACT.Copy).then_inc(a.k_kept, 1)

                def keep_q(g, par):
                    act.wait_ge(a.q_ready, g + 1)
                    if L.layer == 0:
                        nc.scalar.activation(QT[:, par, :], PS[:, PJ2, :], ACT.Identity, bias=bq_s[:, :], scale=L.scale).then_inc(a.q_kept, 1)
                    else:
                        nc.scalar.activation(QT[:, par, :], PS[:, PJ2, :], ACT.Copy, scale=L.scale).then_inc(a.q_kept, 1)

                def keep_v(g, par):
                    act.wait_ge(a.v_ready, g + 1)
                    need(act, a.pv, L.units * (g - 1))
                    for i in (1, 0):
                        for odd in range(2):
                            nc.scalar.activation(V2[:, par, 4 * i:4 * i + 4, :].rearrange("p b d -> p (b d)")
                                                 .rearrange("p (h o e) -> p o h e", o=2, e=L.dk)[:, odd],
                                                 PS[:, PJ + i, :].rearrange("p (h o e) -> p o h e", o=2, e=L.dk)[:, odd],
                                                 ACT.Copy, scale=side[:, odd:odd + 1]).then_inc(a.v_kept, 1)

                def exp(g, u):
                    n = g * L.units + u
                    act.wait_ge(a.shifted, n + 1)
                    nc.scalar.activation(Pr[:, u % 4, :], Pr[:, u % 4, :], ACT.Exp).then_inc(a.exped, 1)

                def keep_pt(g, u):
                    n = g * L.units + u
                    act.wait_ge(a.pt_ready, n + 1)
                    need(act, a.pv, n - 1)
                    nc.scalar.activation(PT[:, u % 2, :], PS[:, PT_BANK, :], ACT.Copy).then_inc(a.pt_kept, 1)

                def body(g, par, older, prev, cur, nxt):
                    for u in range(L.units):
                        if u + 1 < L.units:
                            if cur:
                                exp(g, u + 1)
                        elif nxt:
                            exp(g + 1, 0)
                        if cur:
                            keep_pt(g, u)
                        if L.layer == 1 and older and here(g - 2):
                            if u == 1:
                                act.wait_ge(onT_ready, g - 1)
                                nc.scalar.activation(onT[:, :], PS[:, LG_BANK, :], ACT.Copy).then_inc(onT_kept, 1)
                            if u == 2:
                                act.wait_ge(wo_ready, g - 1)
                                nc.scalar.activation(OTs[:, :], PS[:, LG_BANK, :], ACT.Gelu).then_inc(gelu_o, 1)
                        if L.layer == 1 and older and here(g - 3) and u == 3:
                            act.wait_ge(xe_T, g - 2)
                            nc.scalar.activation(xnT[:, :], PS[:, LG_BANK, :], ACT.Copy).then_inc(xe_T_kept, 1)
                            act.wait_ge(lg1_ready, g - 2)
                            nc.scalar.activation(LG[:, span((g - 3) * GT, GT), 0:E1],
                                                 PS[:, LG_BANK, 0:GT * E1].rearrange("p (t e) -> p t e", t=GT), ACT.Copy).then_inc(lg1_kept, 1)
                        if nxt and u == 0:
                            keep_k(g + 1, 1 - par)
                        if nxt and u == 0:
                            keep_q(g + 1, 1 - par)
                        if nxt and u == L.values_at + 1:
                            keep_v(g + 1, 1 - par)
                        if L.layer == 0 and prev and u == 2:
                            act.wait_ge(oT_ready, g)
                            nc.scalar.activation(OTs[:, :], PS[:, PJ2, :], ACT.Identity, bias=cols[:, BV:BV + 1]).then_inc(oT_kept, 1)
                        if L.layer == 0 and prev and u == 7:
                            act.wait_ge(x2T_ready, g)
                            if not cur:
                                act.wait_ge(x2T_spread, g - 1)
                            nc.scalar.activation(xnT[:, :], PS[:, PJ2, :], ACT.Copy).then_inc(x2T_kept, 1)
                bodies(act, body, NG, L.lag)

            attention(Att(0), a0)
            act.wait_ge(lg_kept, NG)
            act.wait_ge(a0.pt_ready, 8 * NG)
            nc.scalar.activation(Pr[:, 0, :], LG[:, :, :].rearrange("p t e -> p (t e)"), ACT.Sigmoid).then_inc(sig_done, 1)
            act.wait_ge(combT_ready, 1)
            for i in range(4):
                nc.scalar.activation(combT[:, i * 1024:(i + 1) * 1024], PS[0:3 * E0, i, :].bitcast(BF16), ACT.Copy).then_inc(combT_kept, 1)

            def experts0(g, par, older, prev, cur, nxt):
                def gate(g, s, buf):
                    n = g * ITEMS + s
                    rows = P if s < PAIRS else INTER
                    act.wait_ge(a_ready, n + 1)
                    nc.scalar.activation(silu[0:rows, buf, :], PS[0:rows, A_BANK + buf, :], ACT.Silu).then_inc(silu_done, 1)

                for s in range(ITEMS):
                    if s + 1 < ITEMS:
                        if cur:
                            gate(g, s + 1, (s + 1 + par) % 2)
                    elif nxt:
                        gate(g + 1, 0, (1 - par) % 2)
                    if prev and s == 5:
                        act.wait_ge(qT_ready, g)
                        nc.scalar.activation(XNT[:, span((g - 1) * GTOK, GTOK)], PS[:, T_BANK, :], ACT.Identity,
                                             bias=cols[:, PB:PB + 1], scale=cols[:, PG:PG + 1]).then_inc(qT_kept, 1)
                    if prev and s == 8:
                        act.wait_ge(kT_ready, g + 1)
                        nc.scalar.activation(KNT[:, span((g - 1) * GTOK, GTOK)], PS[:, T_BANK, :], ACT.Identity,
                                             bias=cols[:, PB:PB + 1], scale=cols[:, PG:PG + 1]).then_inc(kT_kept, 1)
            bodies(act, experts0, NG)
            act.sem_inc(lg1_kept, 1)
            attention(Att(1), a1)

            act.wait_ge(diff_ready, 1)
            nc.scalar.activation(weight[:, 1, :], left[:, :], ACT.Exp).then_inc(exp_ready, 1)

            def load_w1(k, buf):
                stand(act)
                e = nc.scalar.value_load(expert[0:1, span(k, 1)], min_val=0, max_val=E1 - 1)
                nc.scalar.dma_start(w1[:, buf, :], d["w1"][span(e, 1), :, :].rearrange("o p n -> (o p) n")).then_inc(w1_in[buf], 16)

            def load_w2(k, buf):
                stand(act)
                e = nc.scalar.value_load(expert[0:1, span(k, 1)], min_val=0, max_val=E1 - 1)
                nc.scalar.dma_start(w2[:, buf, :], d["w2"][span(e, 1), :, :].rearrange("o p n -> (o p) n")).then_inc(w2_in[buf], 16)

            act.wait_ge(slots_ready, 1)
            load_w1(0, 0)
            load_w1(1, 1)
            load_w2(0, 0)

            def expert_tiles(k, par, older, prev, cur, nxt):
                if cur:
                    act.wait_ge(up_ready, k + 1)
                    for c in range(CH):
                        nc.scalar.activation(hx[:, par, c, :], PS[:, 2 * par + c // 2, (c % 2) * ST:(c % 2 + 1) * ST], ACT.Gelu,
                                             bias=w1[:, par, HID + c:HID + c + 1]).then_inc(gelued, 1)
                    if not isinstance(k, int) or k + 2 < NST:
                        act.wait_ge(gelued, CH * (k + 1))
                        load_w1(k + 2, par)
                    if nxt:
                        need(act, y_kept, k)
                        load_w2(k + 1, 1 - par)
            bodies(act, expert_tiles, NST)

        @block.tensor
        def _(pe):
            pe.wait_ge(w_in, 16 * NW)
            pe.wait_ge(const_ready, 6)

            def transpose4(bank, src, done):
                for j in range(GT):
                    last = nc.tensor.transpose(PS[:, bank, j * P:(j + 1) * P], src[:, j, :], ident[:, :])
                last.then_inc(done, 1)

            def first_T(g):
                pe.wait_ge(ln1.done, GT * g + GT)
                need(pe, ln1_kept, g)
                transpose4(PT_BANK, xn, ln1_T)

            first_T(0)
            with pe.Fori(1, NG) as g:
                first_T(g)
            pe.wait_ge(mask_fill, 1)
            pe.wait_ge(mask_spread, 48)
            pe.wait_ge(ln1_kept, NG)

            def attention(L, a):
                w = w_att[L.layer]

                def make_k(g, par):
                    if L.layer == 0:
                        pe.wait_ge(a.ct_in, 16 * g + 16)
                        src = ctg[:, :]
                    else:
                        src = KNT[:, span(g * GTOK, GTOK)]
                    need(pe, a.v_kept, 4 * g)
                    nc.tensor.matmul(PS[:, PJ, :], w[:, 1, :], src, start=True, stop=True).then_inc(a.k_ready, 1)

                def make_q(g, par):
                    need(pe, a.v_kept, 4 * g)
                    nc.tensor.matmul(PS[:, PJ2, :], w[:, 0, :], XNT[:, span(g * GTOK, GTOK)], start=True, stop=True).then_inc(a.q_ready, 1)

                def make_v(g, par):
                    pe.wait_ge(a.k_kept, g + 1)
                    pe.wait_ge(a.q_kept, g + 1)
                    if L.layer == 0:
                        need(pe, x1_ready, g - 1)
                    pe.wait_ge(a.ct_in, 16 * g + 16)
                    for b in range(2 * GT):
                        for r in (0, S):
                            last = nc.tensor.matmul(PS[r:r + S, PJ + b // GT, b % GT * P:(b % GT + 1) * P], ctg[:, b * S:(b + 1) * S],
                                                    w[:, 2, :], start=True, stop=True)
                    last.then_inc(a.v_ready, 1)

                def scores(g, u, par):
                    n = g * L.units + u
                    j, part = u // L.parts, u % L.parts
                    if u == 0:
                        pe.wait_ge(a.q_kept, g + 1)
                    need(pe, a.shifted if L.layer == 0 else a.clipped, n - 1)
                    if part == 0:
                        pe.wait_ge(a.spread, 2 * (g * GT + j + 1))
                    bank = PS[:, S_BANKS + u % 2, :]
                    if L.layer == 0:
                        stand(pe)
                        m = mask_rows[:, span(g * GT * S + j * S, S)]
                        nc.tensor.matmul(bank.rearrange("p (h k) -> p h k", h=8), win_ub[:, :],
                                         m.unsqueeze(1).broadcast_to([P, 8, S]), start=True, stop=False, skip_group_check=True)
                    for b2 in range(2):
                        last = nc.tensor.matmul(PS[64 * b2:64 * b2 + 64, S_BANKS + u % 2, :], QT[:, par, (2 * j + b2) * S:(2 * j + b2 + 1) * S],
                                                key_blocks(L, j)[:, b2, 8 * part:8 * part + 8, :],
                                                start=L.layer == 1, stop=True, skip_group_check=True)
                    last.then_inc(a.scores, 1)

                def turn(g, u):
                    n = g * L.units + u
                    pe.wait_ge(a.exped, n + 1)
                    need(pe, a.pt_kept, n)
                    for i in range(4):
                        last = nc.tensor.transpose(PS[:, PT_BANK, i * P:(i + 1) * P], Pr[:, u % 4, i * P:(i + 1) * P], ident[:, :])
                    last.then_inc(a.pt_ready, 1)

                def weigh(g, u, par):
                    n = g * L.units + u
                    j, part = u // L.parts, u % L.parts
                    if u == 0:
                        pe.wait_ge(a.v_kept, 4 * g + 4)
                        need(pe, a.o_kept, g - 1)
                    pe.wait_ge(a.pt_kept, n + 1)
                    stand(pe)
                    for i in range(4):
                        for r in range(4):
                            o = j * P + (4 * part + i) * 2 * L.dk
                            last = nc.tensor.matmul(PS[32 * r:32 * r + 32, O_BANKS + par, o:o + 2 * L.dk],
                                                    PT[:, u % 2, i * P + 32 * r:i * P + 32 * r + 32],
                                                    V2[:, par, 2 * j + r // 2, o - j * P:o - j * P + 2 * L.dk], start=True, stop=True)
                    last.then_inc(a.pv, 1)

                def body(g, par, older, prev, cur, nxt):
                    for u in range(L.units):
                        if L.layer == 0 and prev and u == 7:
                            pe.wait_ge(ln2.done, GT * g)
                            if nxt:
                                pe.wait_ge(a.v_kept, 4 * (g + 2))
                            transpose4(PJ2, xn, x2T_ready)
                        if u + 2 < L.units:
                            if cur:
                                scores(g, u + 2, par)
                        elif nxt:
                            scores(g + 1, u + 2 - L.units, 1 - par)
                        if cur:
                            turn(g, u)
                        if u >= 1:
                            if cur:
                                weigh(g, u - 1, par)
                        elif prev:
                            weigh(g - 1, L.units - 1, 1 - par)
                        if nxt and u == 0:
                            make_k(g + 1, 1 - par)
                            make_q(g + 1, 1 - par)
                        if nxt and u == L.values_at:
                            make_v(g + 1, 1 - par)
                        if L.layer == 0 and prev and u == 2:
                            pe.wait_ge(a.o_kept, g)
                            if nxt:
                                pe.wait_ge(a.q_kept, g + 2)
                            transpose4(PJ2, xm, oT_ready)
                        if L.layer == 0 and prev and u == 3:
                            pe.wait_ge(oT_kept, g)
                            if nxt:
                                pe.wait_ge(a.k_kept, g + 2)
                            for j in range(GT):
                                nc.tensor.matmul(PS[:, PJ, j * P:(j + 1) * P], ones_row[:, :], bo_row[:, :], start=True, stop=False, skip_group_check=True)
                                last = nc.tensor.matmul(PS[:, PJ, j * P:(j + 1) * P], OTs[:, j * P:(j + 1) * P], w[:, 3, :], start=False, stop=True, skip_group_check=True)
                            last.then_inc(proj_ready, 1)
                        if L.layer == 1 and older and here(g - 2):
                            if u == 0:
                                pe.wait_ge(on_ready, g - 1)
                                pe.wait_ge(lg1_kept, max(g - 2, 1) if isinstance(g, int) else g - 2)
                                transpose4(LG_BANK, on[:, par, :, :], onT_ready)
                            if u == 1:
                                pe.wait_ge(onT_kept, g - 1)
                                for j in range(GT):
                                    last = nc.tensor.matmul(PS[:, LG_BANK, j * P:(j + 1) * P], onT[:, j * P:(j + 1) * P], w[:, 3, :], start=True, stop=True)
                                last.then_inc(wo_ready, 1)
                        if L.layer == 1 and older and here(g - 3):
                            if u == 2:
                                if here(g - 2):
                                    pe.wait_ge(gelu_o, g - 1)
                                else:
                                    pe.wait_ge(lg1_kept, g - 2)
                                pe.wait_ge(xe_normed, g - 2)
                                transpose4(LG_BANK, xm, xe_T)
                            if u == 3:
                                pe.wait_ge(xe_T_kept, g - 2)
                                for j in range(GT):
                                    last = nc.tensor.matmul(PS[:, LG_BANK, j * E1:(j + 1) * E1], xnT[:, j * P:(j + 1) * P], wr[:, :], start=True, stop=True)
                                last.then_inc(lg1_ready, 1)
                        if L.layer == 0 and prev and u == 7:
                            pe.wait_ge(x2T_kept, g)
                            for j in range(GT):
                                last = nc.tensor.matmul(PS[:, LG_BANK, j * E0:(j + 1) * E0], xnT[:, j * P:(j + 1) * P], gw[:, :], start=True, stop=True)
                            last.then_inc(lg_ready, 1)
                bodies(pe, body, NG, L.lag)

            attention(Att(0), a0)

            pe.wait_ge(comb_ready, 1)
            pe.wait_ge(lg_kept, NG)
            for t in range(NT):
                last = nc.tensor.transpose(PS[0:3 * E0, t // 8, (t % 8) * 64:(t % 8 + 1) * 64].bitcast(BF16), comb3[:, t, :], identb[:, :])
            last.then_inc(combT_ready, 1)
            pe.wait_ge(combT_kept, 4)
            pe.wait_ge(x2T_spread, NG)

            def experts0(g, par, older, prev, cur, nxt):
                def up(g, s, buf):
                    n = g * ITEMS + s
                    cols_ = P if s < PAIRS else INTER
                    tokens = X2T[:, span(g * GTOK, GTOK)]
                    need(pe, silu_done, n - 1)
                    need(pe, hid_done, n - 1)
                    if s == PAIRS:
                        stand(pe)
                    nc.tensor.matmul(PS[0:cols_, A_BANK + buf, :], w_gate[:, s * P:s * P + cols_], tokens, start=True, stop=True).then_inc(a_ready, 1)
                    if s < PAIRS:
                        nc.tensor.matmul(PS[:, C_BANK + buf, :], sel3[:, s * P:(s + 1) * P], combT[:, span(g * GTOK, GTOK)], start=True, stop=True)
                    nc.tensor.matmul(PS[0:cols_, B_BANK + buf, :], w_up[:, s * P:s * P + cols_], tokens, start=True, stop=True).then_inc(b_ready, 1)

                def down(g, s, buf):
                    n = g * ITEMS + s
                    rows = P if s < PAIRS else INTER
                    pe.wait_ge(hid_done, n + 1)
                    if s == 0:
                        need(pe, x2_ready, g)
                    for j in range(GT):
                        last = nc.tensor.matmul(PS[:, Y_BANK, j * P:(j + 1) * P], hid[0:rows, buf, j * P:(j + 1) * P], w_down[0:rows, s, :],
                                                start=(s == 0 and j == 0), stop=(s == PAIRS), skip_group_check=True)
                    last.then_inc(down_done, 1)
                    if s == PAIRS:
                        pe.wait_ge(down_done, n + 1)
                        pe.sem_inc(y_ready, 1)

                for s in range(ITEMS):
                    if s + 1 < ITEMS:
                        if cur:
                            up(g, s + 1, (s + 1 + par) % 2)
                    elif nxt:
                        up(g + 1, 0, (1 - par) % 2)
                    if cur:
                        down(g, s, (s + par) % 2)
                    if prev and s == 5:
                        pe.wait_ge(q_normed, g)
                        if not cur:
                            pe.wait_ge(kT_kept, g - 1)
                        transpose4(T_BANK, xn, qT_ready)
                    if prev and s == 8:
                        pe.wait_ge(k_normed, g)
                        pe.wait_ge(qT_kept, g)
                        transpose4(T_BANK, xm, kT_ready)
            pe.sem_inc(kT_ready, 1)
            bodies(pe, experts0, NG)
            pe.wait_ge(qT_kept, NG)
            pe.wait_ge(kT_kept, NG)
            pe.wait_ge(x2_ready, NG)
            attention(Att(1), a1)
            pe.wait_ge(diff_ready, 1)
            pe.wait_ge(lg1_kept, NG + 1)
            flat = chosenb[:, :, :].rearrange("p e t -> p (e t)")
            nc.tensor.matmul(PS[:, 0, 0:NT * E1], beforeb[:, :], flat, start=True, stop=True)
            nc.tensor.matmul(PS[:, 1, 0:NT * E1], onesb[:, :], flat, start=True, stop=True).then_inc(ranks_ready, 1)
            pe.wait_ge(slots_ready, 1)

            def expert_tiles(k, par, older, prev, cur, nxt):
                if cur:
                    pe.wait_ge(xsT_kept, k + 1)
                    pe.wait_ge(w1_in[par], sixteens(k, par))
                    for c in range(CH):
                        last = nc.tensor.matmul(PS[:, 2 * par + c // 2, (c % 2) * ST:(c % 2 + 1) * ST],
                                                w1[:, par, c * P:(c + 1) * P], xsT[:, par, :], start=True, stop=True)
                    last.then_inc(up_ready, 1)
                if nxt:
                    pe.wait_ge(xs_in[1 - par], sixteens(k + 1, 1 - par))
                    need(pe, xsT_kept, k + 1)
                    for h in range(ST // P):
                        last = nc.tensor.transpose(PS[:, 4, h * P:(h + 1) * P], xs[:, 1 - par, h, :], ident[:, :])
                    last.then_inc(xsT_ready, 1)
                if prev:
                    pe.wait_ge(gelued, CH * k)
                    pe.wait_ge(w2_in[1 - par], sixteens(k - 1, 1 - par))
                    if not cur:
                        pe.wait_ge(y_kept, k - 2)
                    for h in range(ST // P):
                        for c in range(CH):
                            last = nc.tensor.matmul(PS[:, 5 + (1 - par), h * P:(h + 1) * P], hx[:, 1 - par, c, h * P:(h + 1) * P],
                                                    w2[:, 1 - par, c * P:(c + 1) * P], start=(c == 0), stop=(c == CH - 1))
                    last.then_inc(down_ready, 1)
            bodies(pe, expert_tiles, NST)


def kernel(**inputs):
    import numpy as _np
    import concourse.bacc as _bacc
    from concourse import mybir as _mybir
    from concourse.bass_utils import run_bass_kernel_spmd as _run

    def f(name):
        return _np.asarray(inputs[name])

    arrays = {
        "x": f("x").reshape(TOK, D),
        "ctx": f("ctx_1024").reshape(TOK, D),
        "ctxT": f("ctx_1024").reshape(TOK, D).T,
        "mask": f("mask_BxS2_ff0"),
        "L0_wq": f("L0_xattn_wq"), "L0_wk": f("L0_xattn_wk"), "L0_wv": f("L0_xattn_wv"), "L0_wo": f("L0_xattn_wo"),
        "L0_bq": f("L0_xattn_bq")[:, None], "L0_bk": f("L0_xattn_bk")[:, None], "L0_bv": f("L0_xattn_bv")[:, None],
        "L0_bo": f("L0_xattn_bo")[None, :],
        "pre_g": f("L1_xattn_pre_g")[:, None], "pre_b": f("L1_xattn_pre_b")[:, None],
        "gate_w": f("L0_ffn_gate_w").T,
        "gate_b": _np.broadcast_to(f("L0_ffn_gate_b"), (P, E0)),
        "L1_Wq": f("L1_xattn_Wq"), "L1_Wk": f("L1_xattn_Wk"), "L1_Wv": f("L1_xattn_Wv"), "L1_Wo": f("L1_xattn_Wo"),
        "ln_gb": _np.broadcast_to(_np.stack([f("L1_xattn_ln_g"), f("L1_xattn_ln_b")]), (P, 2, D)),
        "w_gate": _np.concatenate([f("L0_ffn_w13")[:, :INTER], f("L0_ffn_w13_s")[None, :INTER]]).transpose(2, 0, 1).reshape(D, -1),
        "w_up": _np.concatenate([f("L0_ffn_w13")[:, INTER:], f("L0_ffn_w13_s")[None, INTER:]]).transpose(2, 0, 1).reshape(D, -1),
        "w_down": _np.concatenate([f("L0_ffn_w2"), f("L0_ffn_w2_s")[None], _np.zeros((1, D, INTER), _np.float32)])
                     .reshape(ITEMS, 2, D, INTER).transpose(1, 3, 0, 2).reshape(P, ITEMS, D),
        "Wr": f("L1_ffn_Wr"),
        "w1": _np.concatenate([f("L1_ffn_W1"), f("L1_ffn_b1").reshape(E1, CH, P).transpose(0, 2, 1)], 2),
        "w2": _np.concatenate([f("L1_ffn_W2").reshape(E1, CH, P, D).transpose(0, 2, 1, 3).reshape(E1, P, CH * D),
                               _np.broadcast_to(f("L1_ffn_b2")[:, None, :], (E1, P, D))], 2),
        **constants(),
    }
    nc = _bacc.Bacc("TRN2", target_bir_lowering=False, num_devices=1)
    aps, given = {}, {}
    for name, a in arrays.items():
        a = _np.ascontiguousarray(a)
        given[f"in_{name}"] = a
        aps[name] = nc.dram_tensor(f"in_{name}", a.shape, _mybir.dt.from_np(a.dtype), kind="ExternalInput").ap()
    out = nc.dram_tensor("out_x", (TOK, D), F32, kind="ExternalOutput").ap()
    program(nc, aps, out)
    r = _run(nc, [given], core_ids=[0])
    return r.results[0]["out_x"].reshape(B, S, D)
```

```python
from contextlib import ExitStack

import concourse.bass as bass
from concourse import mybir
import numpy as np

F32 = mybir.dt.float32
BF16 = mybir.dt.bfloat16
I32 = mybir.dt.int32
F32R = mybir.dt.float32r
U32 = mybir.dt.uint32
ALU = mybir.AluOpType
ACT = mybir.ActivationFunctionType
AX = mybir.AxisListType

P = 128
D = 128
B, S = 64, 64
TOK = B * S
NT = TOK // P
GT = 4
NG = NT // GT
GTOK = GT * P
EPS = 1e-5
NEWTON = 3
ROOT_STEPS = 3 + 3 * NEWTON

H0, H1 = 16, 8
WINDOW, GLOBAL = 32, 16
RANKS = S - WINDOW - 1 - GLOBAL
NEG = -3.3895313892515355e38
MROW = 32
MPARTS = 2 * 3

E0, K0, INTER = 16, 4, 64
ROUTE_SCALE = 2.5
PAIRS = E0 // 2
ITEMS = PAIRS + 1
W0 = ITEMS * P - INTER

E1, HID = 8, 512
CH = HID // P
ST = 256
NST = TOK * 2 // ST + E1 - 1
NSLOT = NST * ST
ROW = D + 1
WPACK = HID + HID + CH + D


def constants():
    p = np.arange(P)
    dk0, dk1 = D // H0, D // H1
    own0, own1 = ((p[:, None] // (D // h) == np.arange(h)[None, :]).astype(np.float32) for h in (H0, H1))
    s = np.arange(S)
    u = np.zeros((P, 2, S), np.float32)
    v = np.zeros((MROW, S), np.float32)
    for r in range(RANKS):
        u[r] = (s >= GLOBAL + WINDOW + 1 + r)
        v[r] = NEG * (s == GLOBAL + r)
        u[RANKS + r] = s == GLOBAL + r
        v[RANKS + r] = NEG * (s >= GLOBAL + WINDOW + 1 + r)
    for b2 in range(2):
        u[MROW + 3 * b2:MROW + 3 * b2 + 3, b2] = 1.0
    sel3 = np.zeros((3, E0, PAIRS, 2, INTER), np.float32)
    for e in range(E0):
        sel3[:, e, e // 2, e % 2] = 1.0
    reset0 = np.ones((P, NT, E0), np.float32)
    reset0[:, :, 0] = 0.0
    reset1 = np.ones((P, NT, E1), np.float32)
    reset1[:, :, 0] = 0.0
    reset_t = np.ones((P, E1, NT), np.float32)
    reset_t[:, :, 0] = 0.0
    return {
        "c_ident": np.eye(P, dtype=np.float32),
        "c_own0": own0, "c_own1": own1, 
        "c_side": (p[:, None] // S == np.arange(2)[None, :]).astype(np.float32),
        "c_win_u": u.reshape(P, P),
        "c_win_v": v,
        "c_sel3": sel3.reshape(3 * E0, PAIRS * P),
        "c_before": (p[:, None] < p[None, :]).astype(np.float32),
        "c_reset0": reset0.reshape(P, NT * E0),
        "c_reset1": reset1.reshape(P, NT * E1),
        "c_reset_t": reset_t.reshape(P, E1 * NT),
        "c_steps": np.broadcast_to(ST * np.arange(TOK // ST, dtype=np.float32), (P, TOK // ST)).copy(),
        "c_rows": np.concatenate([2 * (P * np.arange(NT)[None, :] + p[:, None]),
                                  2 * TOK + P * np.arange(ST // P)[None, :] + p[:, None]], 1).astype(np.int32),
        "c_tile": np.arange(NST, dtype=np.float32)[None, :].copy(),
    }


class Att:

    def __init__(self, layer):
        self.layer = layer
        self.heads = H0 if layer == 0 else H1
        self.dk = D // self.heads
        self.scale = float(np.float32(self.dk ** -0.5 if layer == 0 else D ** -0.5))
        self.parts = self.heads // 8
        self.units = GT * self.parts
        self.key_bufs = 4 // self.parts
        self.values_at = 4 if layer == 0 else 2
        self.lag = 1 if layer == 0 else 3
        self.ahead = 4


def need(eng, sem, value):
    if isinstance(value, int) and value <= 0:
        return
    eng.wait_ge(sem, value)


def bodies(eng, body, count, lag=1):
    def peeled(g):
        body(g, g % 2, sum(0 <= g - k < count for k in (2, 3) if k <= lag), *(0 <= g + k < count for k in (-1, 0, 1)))

    pairs = (count - 1 - lag) // 2
    for g in range(-1, lag):
        peeled(g)
    with eng.Fori(0, pairs) as i:
        for k in range(2):
            body(2 * i + lag + k, (lag + k) % 2, lag - 1, True, True, True)
    for g in range(lag + 2 * pairs, count + lag):
        peeled(g)


def here(g):
    return not isinstance(g, int) or 0 <= g < NG


def sixteens(k, parity):
    return 8 * (k + 2 - parity)


def span(start, size):
    return slice(start, start + size) if isinstance(start, int) else bass.ds(start, size)


def program(nc, d, out, stop=9):
    with ExitStack() as ctx:
        def sb(name, shape, dt=F32):
            return ctx.enter_context(nc.sbuf_tensor(name, shape, dt))

        def sem(name):
            return ctx.enter_context(nc.semaphore(name))

        PS = ctx.enter_context(nc.psum_tensor("PS", [P, 8, 512], F32))
        X = sb("X", [P, NT, D])
        CN = sb("CN", [P, NT, ROW])
        XNT = sb("XNT", [P, TOK])
        X2T = sb("X2T", [P, TOK])
        KNT = sb("KNT", [P, TOK])
        ctg = sb("ctg", [P, GTOK])
        mask_rows = sb("mask_rows", [P, NT * S], BF16)
        shared = sb("shared", [P, TOK // 2])
        combT = shared[0:3 * E0, :].bitcast(BF16)
        QT = sb("QT", [P, 2, GTOK])
        KTb = sb("KTb", [P, 2, GTOK])
        keys = sb("keys", [P, 4 * 2 * 8 * S])
        scratch = sb("scratch", [P, 2 * CH * ST + 4 * ST + 4 * ROW])
        V2 = scratch[:, 0:2 * 8 * D].rearrange("p (a b d) -> p a b d", a=2, b=8)
        Pr = sb("Pr", [P, 4, 512])
        PT = sb("PT", [P, 2, 512])
        OTs = sb("OTs", [P, GTOK])
        mx = sb("mx", [P, 2, 8])
        sums = sb("sums", [P, 2, GT * H0])
        rsum = sb("rsum", [P, 2, GT * H0])
        xn = sb("xn", [P, GT, D])
        xm = sb("xm", [P, GT, D])
        xnT = sb("xnT", [P, GTOK])
        stats = sb("stats", [P, GT, 6])
        mv = sb("mv", [P, 2 * GT, 2])
        rstd = sb("rstd", [P, 2 * GT])
        var_eps = sb("var_eps", [P, 2 * GT])
        root_t = sb("root_t", [P, 2 * GT])
        mv_all = sb("mv_all", [P, NT, 2])
        rstd_all = sb("rstd_all", [P, NT])
        var_all = sb("var_all", [P, NT])
        root_all = sb("root_all", [P, NT])
        LG = sb("LG", [P, NT, E0])
        w_att = [sb(f"w_att{l}", [P, 4, D]) for l in range(2)]
        cols = sb("cols", [P, 8])
        bq_s = sb("bq_s", [P, 1])
        bo_row = sb("bo_row", [1, D])
        ones_row = sb("ones_row", [1, P])
        ident = sb("ident", [P, P])
        identb = sb("identb", [P, P], BF16)
        own = [sb(f"own{l}", [P, h]) for l, h in enumerate((H0, H1))]
        side = sb("side", [P, 2])
        win_u = sb("win_u", [P, P])
        win_ub = sb("win_ub", [P, P], BF16)
        win_v = sb("win_v", [MROW, S])
        mask_in = sb("mask_in", [B, S])
        mask_left = sb("mask_left", [B, S])
        mask_part = sb("mask_part", [B, 3, S], BF16)
        gw = sb("gw", [P, E0])
        gb = sb("gb", [P, E0])
        BQ, BK, BV, PG, PB = range(5)
        w_gate, w_up = KNT[:, 0:W0], KNT[:, W0:2 * W0]
        w_down = sb("w_down", [P, ITEMS, D])
        sel3 = sb("sel3", [3 * E0, PAIRS * P], BF16)
        comb3 = sb("comb3", [P, NT, 3 * E0], BF16)
        reset0 = KNT[:, 2 * W0:2 * W0 + NT * E0]
        top8 = sb("top8", [P, NT, 8])
        left = sb("left", [P, NT])
        on = shared[:, 0:2 * GTOK].rearrange("p (a t d) -> p a t d", a=2, t=GT)
        onT = shared[:, 2 * GTOK:3 * GTOK]
        ln_gb = sb("ln_gb", [P, 2, D])
        wr = sb("wr", [P, E1])
        reset1 = sb("reset1", [P, NT * E1])
        reset_t = sb("reset_t", [P, NT * E1])
        steps = sb("steps", [P, TOK // ST])
        tile_no = sb("tile_no", [1, NST])
        before = sb("before", [P, P])
        beforeb = sb("beforeb", [P, P], BF16)
        onesb = sb("onesb", [P, P], BF16)
        empty = sb("empty", [P, ST // P, ROW])
        rows = sb("rows", [P, NT + ST // P], I32)
        rows_of = sb("rows_of", [P, 2, 2, ST // P], I32)
        chosenb = sb("chosenb", [P, E1, NT], BF16)
        count = sb("count", [P, 4, E1])
        expert = sb("expert", [1, NST], I32)
        slot = sb("slot", [P, 2, NT], U32)
        slot_f = sb("slot_f", [P, 2, NT])
        weight = sb("weight", [P, 2, NT])
        OA = X2T[:, 0:2 * GTOK].rearrange("p (a t d) -> p a t d", a=2, t=GT)
        XE = CN
        got = [(XNT, X2T)[g // 4][:, g % 4 * 2 * GTOK:(g % 4 + 1) * 2 * GTOK].rearrange("p (t i d) -> p t i d", t=GT, i=2) for g in range(NG)]
        q_flat = keys
        silu = q_flat[:, 0:2 * GTOK].rearrange("p (a s) -> p a s", a=2)
        hid = q_flat[:, 2 * GTOK:4 * GTOK].rearrange("p (a s) -> p a s", a=2)
        gated = q_flat[:, 4 * GTOK:6 * GTOK].rearrange("p (a s) -> p a s", a=2)
        W1N, W2N = HID + CH, HID + D
        w1 = q_flat[:, 0:2 * W1N].rearrange("p (a n) -> p a n", a=2)
        w2 = q_flat[:, 2 * W1N:2 * (W1N + W2N)].rearrange("p (a n) -> p a n", a=2)
        v_flat = scratch
        hx = v_flat[:, 0:2 * CH * ST].rearrange("p (a c s) -> p a c s", a=2, c=CH)
        o = 2 * CH * ST
        xsT = v_flat[:, o:o + 2 * ST].rearrange("p (a s) -> p a s", a=2)
        ys = v_flat[:, o + 2 * ST:o + 4 * ST].rearrange("p (a h d) -> p a h d", a=2, d=D)
        xs = v_flat[:, o + 4 * ST:o + 4 * ST + 4 * ROW].rearrange("p (a h d) -> p a h d", a=2, d=ROW)
        w_high = [sb(f"w_high{i}", [P, W0], F32R) for i in range(2)]
        w_low = [sb(f"w_low{i}", [P, W0], F32R) for i in range(2)]
        x_parts = sb("x_parts", [P, 2, 2, GTOK], F32R)
        XS = nc.dram_tensor("sorted_tokens", (NSLOT, ROW), F32, kind="Internal").ap()
        YS = nc.dram_tensor("results", (2 * TOK + ST, D), F32, kind="Internal").ap()

        x_in, cn_in, w_in, mask_in_s, mask_spread = map(sem, ("x_in", "cn_in", "w_in", "mask_in_s", "mask_spread"))
        const_ready, mask_zero, mask_cut, mask_fill = map(sem, ("const_ready", "mask_zero", "mask_cut", "mask_fill"))
        bqs_ready, mask_clamped = map(sem, ("bqs_ready", "mask_clamped"))

        stood = sem("stood")

        def stand(eng):
            eng.sem_inc(stood, 1)

        class Norm:
            def __init__(self, name, own_done=True):
                self.stats, self.aggr, self.rstd = (sem(f"{name}_{x}") for x in ("stats", "aggr", "rstd"))
                self.done = sem(f"{name}_done") if own_done else None

        def norm_stats(dve, ln, g, src, moments=None):
            moments = mv[:, 0:GT, :] if moments is None else moments
            stand(dve)
            for j in range(GT):
                nc.vector.bn_stats(stats[:, j, :], src[j]).then_inc(ln.stats, 1)
            dve.wait_ge(ln.stats, g * GT + GT)
            stand(dve)
            for j in range(GT):
                nc.vector.bn_aggr(moments[:, j, :], stats[:, j, :]).then_inc(ln.aggr, 1)
            dve.wait_ge(ln.aggr, g * GT + GT)

        def root_guess(dve, ln, g, moments, r, v, twice=False):
            step = g * ROOT_STEPS
            scale, offset = (1 + EPS, EPS * EPS) if twice else (1.0, EPS)
            nc.vector.tensor_scalar(v, moments[:, :, 1], scale, offset, ALU.mult, ALU.add).then_inc(ln.rstd, 1)
            dve.wait_ge(ln.rstd, step + 1)
            nc.vector.tensor_scalar(r.bitcast(I32), v.bitcast(I32), 1, None, ALU.logical_shift_right).then_inc(ln.rstd, 1)
            dve.wait_ge(ln.rstd, step + 2)
            nc.vector.tensor_scalar(r.bitcast(I32), r.bitcast(I32), -1.0, float(0x5f3759df), ALU.mult, ALU.add).then_inc(ln.rstd, 1)
            dve.wait_ge(ln.rstd, step + 3)

        def root_newton(dve, ln, g, i, r, v, t):
            step = g * ROOT_STEPS + 3 + 3 * i
            nc.vector.tensor_tensor(t, r, r, ALU.mult).then_inc(ln.rstd, 1)
            dve.wait_ge(ln.rstd, step + 1)
            nc.vector.scalar_tensor_tensor(out=t, in0=t, scalar=-0.5, in1=v, op0=ALU.mult, op1=ALU.mult).then_inc(ln.rstd, 1)
            dve.wait_ge(ln.rstd, step + 2)
            nc.vector.scalar_tensor_tensor(out=r, in0=t, scalar=1.5, in1=r, op0=ALU.add, op1=ALU.mult).then_inc(ln.rstd, 1)
            dve.wait_ge(ln.rstd, step + 3)

        def norm_apply(dve, ln, g, src, dst, moments=None, r=None):
            moments = mv if moments is None else moments
            r = rstd if r is None else r
            for j in range(GT):
                nc.vector.tensor_scalar(dst[j], src[j], moments[:, j, 0:1], r[:, j:j + 1],
                                        ALU.subtract, ALU.mult).then_inc(ln.done, 1)

        def tiles4(t, g):
            return [t[:, g * GT + j, 0:D] for j in range(GT)]

        def local4(t):
            return [t[:, j, :] for j in range(GT)]

        ln1 = Norm("ln1")
        ln1_T, ln1_kept = sem("ln1_T"), sem("ln1_kept")

        class AttSems:
            def __init__(self, l):
                self.k_ready, self.q_ready, self.v_ready, self.k_kept, self.q_kept = (
                    sem(f"{n}{l}") for n in ("k_ready", "q_ready", "v_ready", "k_kept", "q_kept"))
                self.v_kept, self.ct_in, self.scores, self.maxed, self.clipped = (
                    sem(f"{n}{l}") for n in ("v_kept", "ct_in", "scores", "maxed", "clipped"))
                self.shifted, self.exped, self.summed, self.recip, self.spread = (
                    sem(f"{n}{l}") for n in ("shifted", "exped", "summed", "recip", "spread"))
                self.pt_ready, self.pt_kept, self.pv, self.o_kept = (
                    sem(f"{n}{l}") for n in ("pt_ready", "pt_kept", "pv", "o_kept"))

        att_sems = [AttSems(0), AttSems(1)]
        a0, a1 = att_sems
        proj_ready, x1_ready, x2T_ready, x2T_kept, x2T_spread, lg_ready, lg_kept = map(
            sem, ("proj_ready", "x1_ready", "x2T_ready", "x2T_kept", "x2T_spread", "lg_ready", "lg_kept"))
        ln2 = Norm("ln2")
        oT_ready, oT_kept = sem("oT_ready"), sem("oT_kept")
        out_done = sem("out_done")
        sig_done, gate_step, comb_ready, combT_ready, combT_kept = map(sem, ("sig_done", "gate_step", "comb_ready", "combT_ready", "combT_kept"))
        a_ready, b_ready, silu_done, gated_done, hid_done, down_done, y_ready, x2_ready = map(
            sem, ("a_ready", "b_ready", "silu_done", "gated_done", "hid_done", "down_done", "y_ready", "x2_ready"))
        ln3, ln_ctx = Norm("ln3", False), Norm("ln_ctx")
        ctx_moments = ln_ctx.done
        q_centred, q_normed, k_centred, k_normed = map(sem, ("q_centred", "q_normed", "k_centred", "k_normed"))
        qT_ready, qT_kept, kT_ready, kT_kept = map(sem, ("qT_ready", "qT_kept", "kT_ready", "kT_kept"))
        ln_o, ln4 = Norm("ln_o"), Norm("ln4", False)
        xe_centred, xe_normed = sem("xe_centred"), sem("xe_normed")
        scaled, on_ready, onT_ready, onT_kept, wo_ready, gelu_o, x_on, x3_ready = map(
            sem, ("scaled", "on_ready", "onT_ready", "onT_kept", "wo_ready", "gelu_o", "x_on", "x3_ready"))
        xe_T, xe_T_kept, xe_kept, lg1_ready, lg1_kept = map(sem, ("xe_T", "xe_T_kept", "xe_kept", "lg1_ready", "lg1_kept"))
        xs_zeroed, route_step, ranks_ready, diff_ready, exp_ready, slots_ready, scattered = map(
            sem, ("xs_zeroed", "route_step", "ranks_ready", "diff_ready", "exp_ready", "slots_ready", "scattered"))
        w1_in, w2_in, xs_in, y_out = ([sem(f"{n}{i}") for i in range(2)] for n in ("w1_in", "w2_in", "xs_in", "y_out"))
        xsT_ready, xsT_kept, up_ready, gelued, down_ready, y_kept = map(
            sem, ("xsT_ready", "xsT_kept", "up_ready", "gelued", "down_ready", "y_kept"))
        results_in = [sem(f"results_in{i}") for i in range(NG // 2)]
        slot_known = sem("slot_known")
        w_split, x_high, x_split = map(sem, ("w_split", "x_high", "x_split"))
        half_done, x4_ready = sem("half_done"), sem("x4_ready")
        empty_ready, rows_in, rows_ready, rows_step = map(sem, ("empty_ready", "rows_in", "rows_ready", "rows_step"))

        S_BANKS, PT_BANK, LG_BANK, O_BANKS, PJ, PJ2 = 0, 2, 3, 4, 6, 7

        x_dram = d["x"].rearrange("(t p) d -> p t d", p=P)
        cn_dram = d["ctx"].rearrange("(t p) d -> p t d", p=P)
        NW = 18 + 4 + 12
        A_BANK, B_BANK, C_BANK, Y_BANK, T_BANK = 0, 2, 4, 6, 7

        def key_blocks(L, j):
            n = 2 * L.heads * S
            at = j % L.key_bufs * n
            return keys[:, at:at + n].rearrange("p (b h k) -> p b h k", b=2, h=L.heads)

        block = ctx.enter_context(nc.Block())

        @block.sync
        def _(sp):
            sp.dma_start(X[:, :, :], x_dram).then_inc(x_in, 16)
            sp.dma_start(rows[:, :], d["c_rows"]).then_inc(rows_in, 16)
            for i, name in enumerate(("L0_wq", "L0_wk", "L0_wv", "L0_wo")):
                sp.dma_start(w_att[0][:, i, :], d[name]).then_inc(w_in, 16)
            for i, name in enumerate(("L0_bq", "L0_bk", "L0_bv", "pre_g", "pre_b")):
                sp.dma_start(cols[:, i:i + 1], d[name]).then_inc(w_in, 16)
            sp.dma_start(bo_row[:, :], d["L0_bo"]).then_inc(w_in, 16)
            for l in range(2):
                sp.dma_start(own[l][:, :], d[f"c_own{l}"]).then_inc(w_in, 16)
            sp.dma_start(side[:, :], d["c_side"]).then_inc(w_in, 16)
            sp.dma_start(win_u[:, :], d["c_win_u"]).then_inc(w_in, 16)
            sp.dma_start(win_v[:, :], d["c_win_v"]).then_inc(w_in, 16)
            sp.dma_start(ident[:, :], d["c_ident"]).then_inc(w_in, 16)
            sp.dma_start(gw[:, :], d["gate_w"]).then_inc(w_in, 16)
            sp.dma_start(gb[:, :], d["gate_b"]).then_inc(w_in, 16)
            for i, name in enumerate(("L1_Wq", "L1_Wk", "L1_Wv", "L1_Wo")):
                sp.dma_start(w_att[1][:, i, :], d[name]).then_inc(w_in, 16)
            for t, name in ((w_gate, "w_gate"), (w_up, "w_up"), (reset0, "c_reset0"), (wr, "Wr"), (reset1, "c_reset1"),
                            (reset_t, "c_reset_t"), (steps, "c_steps"), (tile_no, "c_tile"), (before, "c_before")):
                sp.dma_start(t[:, :], d[name]).then_inc(w_in, 16)
            sp.dma_start(w_down[:, :, :], d["w_down"]).then_inc(w_in, 16)
            sp.dma_start(ln_gb[:, :, :], d["ln_gb"]).then_inc(w_in, 16)
            sp.dma_start(Pr[0:3 * E0, 0:2, :].rearrange("p a b -> p (a b)"), d["c_sel3"]).then_inc(w_in, 16)
            sp.dma_start(mask_in[:, :], d["mask"]).then_inc(mask_in_s, 16)
            def load_ct(a):
                def body(g, par, older, prev, cur, nxt):
                    if nxt:
                        need(sp, a.v_ready, g + 1)
                        need(sp, a.k_ready, g + 1)
                        sp.dma_start(ctg[:, :], d["ctxT"][:, span((g + 1) * GTOK, GTOK)]).then_inc(a.ct_in, 16)
                    if a is a0 and not cur and nxt:
                        sp.dma_start(CN[:, :, 0:D], cn_dram).then_inc(cn_in, 16)
                        sp.wait_ge(empty_ready, 2)
                        for h in range(ST // P):
                            sp.dma_start(XS.rearrange("(k h p) d -> p h k d", p=P, h=ST // P)[:, h],
                                         empty[:, h, :].unsqueeze(1).broadcast_to([P, NST, ROW])).then_inc(xs_zeroed, 16)
                bodies(sp, body, NG)

            load_ct(a0)
            sp.wait_ge(a0.v_ready, NG)
            load_ct(a1)

            sp.wait_ge(scattered, 16 * 2 * NT)
            sp.wait_ge(xs_zeroed, 32)

            def load_tokens(k, buf):
                sp.dma_start(xs[:, buf, :, :], XS[span(k * ST, ST), :].rearrange("(h p) d -> p h d", p=P)).then_inc(xs_in[buf], 16)

            def store(g):
                sp.dma_start(out.rearrange("(t p) d -> p t d", p=P)[:, g * GT:(g + 1) * GT, :],
                             X[:, g * GT:(g + 1) * GT, :]).then_inc(out_done, 16)

            load_tokens(0, 0)
            load_tokens(1, 1)

            def expert_tiles(k, par, older, prev, cur, nxt):
                if cur and (not isinstance(k, int) or k + 2 < NST):
                    sp.wait_ge(xsT_ready, k + 1)
                    sp.wait_ge(xsT_kept, k + 1)
                    load_tokens(k + 2, par)
            bodies(sp, expert_tiles, NST)

            for i in range(2):
                sp.wait_ge(y_out[i], 32 * ((NST + 1 - i) // 2))
            for i in range(NG // 2):
                sp.dma_start((XNT, X2T)[i // 2][:, i % 2 * 4 * GTOK:(i % 2 + 1) * 4 * GTOK].rearrange("p (t i d) -> p t i d", t=2 * GT, i=2),
                             YS[0:2 * TOK, :].rearrange("(t p i) d -> p t i d", p=P, i=2)[:, 2 * i * GT:2 * (i + 1) * GT]).then_inc(results_in[i], 16)
            for g in range(NG):
                sp.wait_ge(x4_ready, GT * (g + 1))
                store(g)
            sp.wait_ge(out_done, 16 * NG)

        @block.gpsimd
        def _(pool):
            nc.gpsimd.memset(ones_row[:, :], 1.0).then_inc(const_ready, 1)
            nc.gpsimd.memset(onesb[:, :], 1.0).then_inc(const_ready, 1)
            nc.gpsimd.memset(empty[:, :, 0:D], 0.0).then_inc(empty_ready, 1)
            pool.wait_ge(rows_in, 16)
            nc.gpsimd.tensor_copy(empty[:, :, D].bitcast(I32), rows[:, NT:NT + ST // P]).then_inc(empty_ready, 1)
            nc.gpsimd.memset(mask_rows[:, :], 0.0).then_inc(mask_zero, 1)
            pool.wait_ge(mask_zero, 1)
            pool.wait_ge(w_in, 16 * NW)
            nc.gpsimd.tensor_copy(mask_rows[0:MROW, :].rearrange("r (t k) -> r t k", t=NT),
                                  win_v[:, :].unsqueeze(1).broadcast_to([MROW, NT, S])).then_inc(mask_fill, 1)

            def attention(L, a):
                def spread(g, j, par):
                    if j == 0:
                        pool.wait_ge(a.k_kept, g + 1)
                    need(pool, a.scores, L.parts * (g * GT + j - L.key_bufs + 1))
                    own_keys = KTb[:, par, j * P:(j + 1) * P].rearrange("p (b k) -> p b k", b=2)
                    for b2 in range(2):
                        nc.gpsimd.tensor_tensor(key_blocks(L, j)[:, b2], own_keys[:, b2, :].unsqueeze(1).broadcast_to([P, L.heads, S]),
                                                own[L.layer][:, :].unsqueeze(2).broadcast_to([P, L.heads, S]), ALU.mult).then_inc(a.spread, 1)

                def body(g, par, older, prev, cur, nxt):
                    for u in range(L.units):
                        if L.layer == 1 and u == 0:
                            after_attention1(g, u, par, older, prev, nxt)
                        if u % L.parts == 0:
                            j = (u + L.ahead) // L.parts
                            if j >= GT and nxt:
                                spread(g + 1, j - GT, 1 - par)
                            elif j < GT and cur:
                                spread(g, j, par)
                        if L.layer == 0 and prev and u == 7:
                            pool.wait_ge(x2T_kept, g)
                            nc.gpsimd.tensor_copy(X2T[:, span((g - 1) * GTOK, GTOK)], xnT[:, :]).then_inc(x2T_spread, 1)
                        if L.layer == 1 and u > 0:
                            after_attention1(g, u, par, older, prev, nxt)
                bodies(pool, body, NG, L.lag)

            def after_attention1(g, u, par, older, prev, nxt):
                if u == 0 and older and here(g - 2):
                    pool.wait_ge(on_ready, g - 1)
                    x4 = X[:, span((g - 2) * GT, GT), :]
                    stand(pool)
                    nc.gpsimd.tensor_tensor(x4, x4, on[:, par, :, :], ALU.add).then_inc(x_on, 1)
                if u == 3 and prev:
                    gain, offset = (ln_gb[:, i, :].unsqueeze(1).broadcast_to([P, GT, D]) for i in range(2))
                    pool.wait_ge(ln_o.done, GT * g)
                    nc.gpsimd.tensor_tensor(on[:, 1 - par, :, :], xn[:, :, :], gain, ALU.mult).then_inc(scaled, 1)
                    pool.wait_ge(scaled, g)
                    nc.gpsimd.tensor_tensor(on[:, 1 - par, :, :], on[:, 1 - par, :, :], offset, ALU.add).then_inc(on_ready, 1)
                if u == 1 and older and here(g - 3):
                    pool.wait_ge(ln_o.rstd, ROOT_STEPS * (g - 1))
                    if not nxt:
                        need(pool, xe_T, g - 3)
                    stand(pool)
                    nc.gpsimd.tensor_tensor(xm[:, :, :], X[:, span((g - 3) * GT, GT), :],
                                            mv[:, GT:2 * GT, 0].unsqueeze(2).broadcast_to([P, GT, D]), ALU.subtract).then_inc(xe_centred, 1)
                    roots = rstd[:, GT:2 * GT].unsqueeze(2).broadcast_to([P, GT, D])
                    pool.wait_ge(xe_centred, g - 2)
                    stand(pool)
                    nc.gpsimd.tensor_tensor(XE[:, span((g - 3) * GT, GT), 0:D], xm[:, :, :], roots, ALU.mult).then_inc(xe_kept, 1)
                    pool.wait_ge(xe_kept, g - 2)
                    nc.gpsimd.tensor_tensor(xm[:, :, :], xm[:, :, :], roots, ALU.mult).then_inc(xe_normed, 1)

            attention(Att(0), a0)

            for i, w in enumerate((w_gate, w_up)):
                nc.gpsimd.tensor_copy(w_high[i][:, :], w[:, :]).then_inc(w_split, 1)
                pool.wait_ge(w_split, 2 * i + 1)
                nc.gpsimd.tensor_tensor(w_low[i][:, :], w[:, :], w_high[i][:, :].bitcast(F32), ALU.subtract).then_inc(w_split, 1)
            def experts0(g, par, older, prev, cur, nxt):
                if nxt:
                    need(pool, b_ready, ITEMS * g)
                    tokens = X2T[:, span((g + 1) * GTOK, GTOK)]
                    high, low = (x_parts[:, 1 - par, i, :] for i in range(2))
                    stand(pool)
                    nc.gpsimd.tensor_copy(high, tokens).then_inc(x_high, 1)
                    pool.wait_ge(x_high, g + 2)
                    stand(pool)
                    nc.gpsimd.tensor_tensor(low, tokens, high.bitcast(F32), ALU.subtract).then_inc(x_split, 1)
                if prev:
                    pool.wait_ge(ln3.rstd, ROOT_STEPS * g)
                    stand(pool)
                    nc.gpsimd.tensor_tensor(xn[:, :, :], X[:, span((g - 1) * GT, GT), :],
                                            mv[:, 0:GT, 0].unsqueeze(2).broadcast_to([P, GT, D]), ALU.subtract).then_inc(q_centred, 1)
                    pool.wait_ge(q_centred, g)
                    nc.gpsimd.tensor_tensor(xn[:, :, :], xn[:, :, :], rstd[:, 0:GT].unsqueeze(2).broadcast_to([P, GT, D]),
                                            ALU.mult).then_inc(q_normed, 1)
                    pool.wait_ge(kT_ready, g)
                    tiles = span((g - 1) * GT, GT)
                    stand(pool)
                    nc.gpsimd.tensor_tensor(xm[:, :, :], CN[:, tiles, 0:D],
                                            mv_all[:, tiles, 0].unsqueeze(2).broadcast_to([P, GT, D]), ALU.subtract).then_inc(k_centred, 1)
                    pool.wait_ge(k_centred, g)
                    stand(pool)
                    nc.gpsimd.tensor_tensor(xm[:, :, :], xm[:, :, :], rstd_all[:, tiles].unsqueeze(2).broadcast_to([P, GT, D]),
                                            ALU.mult).then_inc(k_normed, 1)
            pool.wait_ge(cn_in, 16)
            pool.wait_ge(ln_ctx.rstd, ROOT_STEPS)
            bodies(pool, experts0, NG)

            attention(Att(1), a1)

            pool.wait_ge(xe_kept, NG)
            pool.wait_ge(xs_zeroed, 32)
            for i in range(2):
                nc.gpsimd.tensor_scalar(XE[:, :, D].bitcast(I32), rows[:, 0:NT], i, None, ALU.add).then_inc(rows_ready, 1)
                pool.wait_ge(rows_ready, i + 1)
                pool.wait_ge(slot_known, i + 1)
                for t in range(NT):
                    nc.gpsimd.indirect_dma_start(XS, bass.IndirectOffsetOnAxis(ap=slot[:, i, t:t + 1], axis=0),
                                                 XE[:, t, :], None).then_inc(scattered, 16)
                if i == 0:
                    pool.wait_ge(scattered, 16 * NT)

            def store_results(k, par, older, prev, cur, nxt):
                if prev:
                    if not isinstance(k, int) or k >= 2:
                        pool.wait_ge(y_out[par], 2 * sixteens(k - 2, par))
                    pool.wait_ge(y_kept, k)
                    stand(pool)
                    for h in range(ST // P):
                        nc.gpsimd.indirect_dma_start(YS, bass.IndirectOffsetOnAxis(ap=rows_of[:, 1 - par, 1, h:h + 1].bitcast(U32), axis=0),
                                                     ys[:, 1 - par, h, :], None).then_inc(y_out[1 - par], 16)
            bodies(pool, store_results, NST, 3)

        @block.vector
        def _(dve):
            dve.wait_ge(x_in, 16)

            for g in range(NG):
                norm_stats(dve, ln1, g, tiles4(X, g), mv_all[:, g * GT:(g + 1) * GT, :])
            dve.wait_ge(ln1.aggr, GT * NG)
            root_guess(dve, ln1, 0, mv_all[:, :, :], rstd_all[:, :], var_all[:, :])
            for i in range(NEWTON):
                root_newton(dve, ln1, 0, i, rstd_all[:, :], var_all[:, :], root_all[:, :])
            def first_apply(g):
                if g >= 2:
                    dve.wait_ge(ln1_T, g - 1)
                norm_apply(dve, ln1, g, tiles4(X, g), local4((xn, xm)[g % 2]), mv_all[:, g * GT:(g + 1) * GT, :], rstd_all[:, g * GT:(g + 1) * GT])

            first_apply(0)
            first_apply(1)
            dve.wait_ge(w_in, 16 * NW)
            nc.vector.tensor_scalar(bq_s[:, :], cols[:, BQ:BQ + 1], Att(0).scale, None, ALU.mult).then_inc(bqs_ready, 1)
            nc.vector.tensor_copy(win_ub[:, :], win_u[:, :]).then_inc(const_ready, 1)
            nc.vector.tensor_copy(identb[:, :], ident[:, :]).then_inc(const_ready, 1)
            nc.vector.tensor_copy(beforeb[:, :], before[:, :]).then_inc(const_ready, 1)
            nc.vector.tensor_copy(sel3[:, :], Pr[0:3 * E0, 0:2, :].rearrange("p a b -> p (a b)")).then_inc(const_ready, 1)
            dve.wait_ge(mask_in_s, 16)
            nc.vector.tensor_scalar(mask_left[:, :], mask_in[:, :], NEG, None, ALU.max).then_inc(mask_clamped, 1)
            dve.wait_ge(mask_clamped, 1)
            nc.vector.tensor_copy(mask_part[:, 0, :], mask_left[:, :]).then_inc(mask_cut, 1)
            for i in range(1, 3):
                dve.wait_ge(mask_cut, i)
                nc.vector.tensor_tensor(mask_left[:, :], mask_left[:, :], mask_part[:, i - 1, :], ALU.subtract).then_inc(mask_clamped, 1)
                dve.wait_ge(mask_clamped, i + 1)
                nc.vector.tensor_copy(mask_part[:, i, :], mask_left[:, :]).then_inc(mask_cut, 1)

            for g in range(2, NG):
                first_apply(g)
            dve.wait_ge(ln1_T, NG)
            dve.wait_ge(cn_in, 16)

            def attention(L, a):
                def shift(g, u):
                    n = g * L.units + u
                    dve.wait_ge(a.scores, n + 1)
                    need(dve, a.pt_ready, n - 3)
                    s = PS[:, S_BANKS + u % 2, :].rearrange("p (s k) -> p s k", k=S)
                    pr = Pr[:, u % 4, :].rearrange("p (s k) -> p s k", k=S)
                    m = mx[:, u % 2, :]
                    if L.layer == 1:
                        nc.vector.tensor_scalar(pr, s, -10000.0, 10000.0, ALU.max, ALU.min).then_inc(a.clipped, 1)
                        dve.wait_ge(a.clipped, n + 1)
                        s = pr
                    nc.vector.tensor_reduce(m, s, AX.X, ALU.max).then_inc(a.maxed, 1)
                    dve.wait_ge(a.maxed, n + 1)
                    nc.vector.tensor_tensor(pr, s, m.unsqueeze(2).broadcast_to([P, 8, S]), ALU.subtract).then_inc(a.shifted, 1)

                def total(g, u, par):
                    n = g * L.units + u
                    dve.wait_ge(a.exped, n + 1)
                    nc.vector.tensor_reduce(sums[:, par, 8 * u:8 * u + 8], Pr[:, u % 4, :].rearrange("p (s k) -> p s k", k=S),
                                            AX.X, ALU.add).then_inc(a.summed, 1)

                def body(g, par, older, prev, cur, nxt):
                    for u in range(L.units):
                        if u + 1 < L.units:
                            if cur:
                                shift(g, u + 1)
                        elif nxt:
                            shift(g + 1, 0)
                        if cur:
                            total(g, u, par)
                        if prev and u == 0:
                            dve.wait_ge(a.summed, g * L.units)
                            nc.vector.reciprocal(rsum[:, 1 - par, 0:8 * L.units], sums[:, 1 - par, 0:8 * L.units]).then_inc(a.recip, 1)
                        if prev and u == 1:
                            dve.wait_ge(a.recip, g)
                            dve.wait_ge(a.pv, g * L.units)
                            if L.layer == 0:
                                o = xm[:, :, :].rearrange("p t d -> p (t d)")
                            else:
                                o = OA[:, 1 - par, :, :].rearrange("p t d -> p (t d)")
                            nc.vector.tensor_tensor(o.rearrange("p (h e) -> p h e", e=L.dk),
                                                    PS[:, O_BANKS + 1 - par, :].rearrange("p (h e) -> p h e", e=L.dk),
                                                    rsum[:, 1 - par, 0:8 * L.units].unsqueeze(2).broadcast_to([P, 8 * L.units, L.dk]),
                                                    ALU.mult).then_inc(a.o_kept, 1)
                        if L.layer == 0:
                            after_attention0(g, u, prev, cur)
                        else:
                            after_attention1(g, u, par, older, prev)

                def after_attention0(g, u, prev, cur):
                    if cur and u == 3:
                        norm_stats(dve, ln_ctx, g, tiles4(CN, g), mv[:, GT:2 * GT, :])
                        nc.vector.tensor_copy(mv_all[:, span(g * GT, GT), :], mv[:, GT:2 * GT, :]).then_inc(ctx_moments, 1)
                    if not prev:
                        return
                    if u == 4:
                        dve.wait_ge(proj_ready, g)
                        x4 = X[:, span((g - 1) * GT, GT), :]
                        nc.vector.tensor_tensor(x4, x4, PS[:, PJ, :].rearrange("p (t d) -> p t d", t=GT), ALU.add).then_inc(x1_ready, 1)
                        dve.wait_ge(x1_ready, g)
                        norm_stats(dve, ln2, g - 1, tiles4(X, g - 1))
                    if u == 5:
                        dve.wait_ge(ln2.aggr, GT * g)
                        root_guess(dve, ln2, g - 1, mv[:, 0:GT, :], rstd[:, 0:GT], var_eps[:, 0:GT])
                        root_newton(dve, ln2, g - 1, 0, rstd[:, 0:GT], var_eps[:, 0:GT], root_t[:, 0:GT])
                    if u == 6:
                        for i in range(1, NEWTON):
                            root_newton(dve, ln2, g - 1, i, rstd[:, 0:GT], var_eps[:, 0:GT], root_t[:, 0:GT])
                        norm_apply(dve, ln2, g - 1, tiles4(X, g - 1), local4(xn))
                    if u == 7:
                        dve.wait_ge(lg_ready, g)
                        nc.vector.tensor_copy(LG[:, span((g - 1) * GT, GT), :],
                                              PS[:, LG_BANK, 0:GT * E0].rearrange("p (t e) -> p t e", t=GT)).then_inc(lg_kept, 1)

                def after_attention1(g, u, par, older, prev):
                    if u == 1 and prev:
                        dve.wait_ge(a.o_kept, g)
                        norm_stats(dve, ln_o, g - 1, local4(OA[:, 1 - par, :, :]))
                    if u == 2 and older and here(g - 2):
                        dve.wait_ge(gelu_o, g - 1)
                        dve.wait_ge(x_on, g - 1)
                        x4 = X[:, span((g - 2) * GT, GT), :]
                        nc.vector.tensor_tensor(x4, x4, OTs[:, :].rearrange("p (t d) -> p t d", t=GT), ALU.add).then_inc(x3_ready, 1)
                        dve.wait_ge(x3_ready, g - 1)
                        if here(g - 3):
                            dve.wait_ge(xe_normed, g - 2)
                        norm_stats(dve, ln4, g - 2, tiles4(X, g - 2), mv[:, GT:2 * GT, :])
                    if u == 3 and (prev or older and here(g - 2)):
                        lo, hi = (0 if prev else GT), (2 * GT if older and here(g - 2) else GT)
                        if prev:
                            dve.wait_ge(ln_o.aggr, GT * g)
                        if hi > GT:
                            dve.wait_ge(ln4.aggr, GT * (g - 1))
                        root_guess(dve, ln_o, g - 1, mv[:, lo:hi, :], rstd[:, lo:hi], var_eps[:, lo:hi])
                        for i in range(NEWTON):
                            root_newton(dve, ln_o, g - 1, i, rstd[:, lo:hi], var_eps[:, lo:hi], root_t[:, lo:hi])
                        if prev:
                            norm_apply(dve, ln_o, g - 1, local4(OA[:, 1 - par, :, :]), local4(xn))
                bodies(dve, body, NG, L.lag)

            attention(Att(0), a0)

            def chain(s, value, instruction):
                value[0] += 1
                instruction.then_inc(s, 1)
                dve.wait_ge(s, value[0])

            def choose(s, value, v, top, E, K, above, equal, rank, reset):
                for t in range(NT):
                    nc.vector.max(top[:, t, :], v[:, t, :]).then_inc(s, 1)
                value[0] += NT
                dve.wait_ge(s, value[0])
                least = top[:, :, K - 1].unsqueeze(2).broadcast_to([P, NT, E])
                chain(s, value, nc.vector.tensor_tensor(above, v, least, ALU.is_gt))
                chain(s, value, nc.vector.tensor_tensor(equal, v, least, ALU.is_equal))
                chain(s, value, nc.vector.tensor_reduce(left[:, :], above, AX.X, ALU.add))
                chain(s, value, nc.vector.tensor_scalar(left[:, :], left[:, :], -1.0, float(K), ALU.mult, ALU.add))
                flat = [x.rearrange("p t e -> p (t e)") for x in (rank, equal)]
                chain(s, value, nc.vector.tensor_tensor_scan(flat[0], reset, flat[1], 0.0, ALU.mult, ALU.add))
                chain(s, value, nc.vector.tensor_tensor(rank, rank, left[:, :].unsqueeze(2).broadcast_to([P, NT, E]), ALU.is_le))
                chain(s, value, nc.vector.tensor_tensor(equal, equal, rank, ALU.mult))
                chain(s, value, nc.vector.tensor_tensor(above, above, equal, ALU.add))

            dve.wait_ge(sig_done, 1)
            dve.wait_ge(a0.pt_ready, 8 * NG)
            dve.wait_ge(a0.pv, 8 * NG)
            sig, biased, above, equal = (Pr[:, i, :].rearrange("p (t e) -> p t e", e=E0) for i in range(4))
            rank, w0 = (PT[:, i, :].rearrange("p (t e) -> p t e", e=E0) for i in range(2))
            at = [0]
            chain(gate_step, at, nc.vector.tensor_tensor(biased, sig, gb[:, :].unsqueeze(1).broadcast_to([P, NT, E0]), ALU.add))
            choose(gate_step, at, biased, top8, E0, K0, above, equal, rank, reset0[:, :])
            chain(gate_step, at, nc.vector.tensor_tensor(w0, sig, above, ALU.mult))
            chain(gate_step, at, nc.vector.tensor_reduce(left[:, :], w0, AX.X, ALU.add))
            chain(gate_step, at, nc.vector.reciprocal(left[:, :], left[:, :]))
            chain(gate_step, at, nc.vector.scalar_tensor_tensor(out=w0, in0=w0, scalar=ROUTE_SCALE, in1=left[:, :].unsqueeze(2).broadcast_to([P, NT, E0]),
                                                                op0=ALU.mult, op1=ALU.mult))
            part = [comb3[:, :, i * E0:(i + 1) * E0] for i in range(3)]
            chain(gate_step, at, nc.vector.tensor_copy(part[0], w0))
            chain(gate_step, at, nc.vector.tensor_tensor(w0, w0, part[0], ALU.subtract))
            chain(gate_step, at, nc.vector.tensor_copy(part[1], w0))
            chain(gate_step, at, nc.vector.tensor_tensor(w0, w0, part[1], ALU.subtract))
            nc.vector.tensor_copy(part[2], w0).then_inc(comb_ready, 1)

            dve.wait_ge(ctx_moments, NG)
            root_guess(dve, ln_ctx, 0, mv_all[:, :, :], rstd_all[:, :], var_all[:, :])
            for i in range(NEWTON):
                root_newton(dve, ln_ctx, 0, i, rstd_all[:, :], var_all[:, :], root_all[:, :])

            def experts0(g, par, older, prev, cur, nxt):
                for s in range(ITEMS):
                    n = g * ITEMS + s
                    buf = (s + par) % 2
                    rows = P if s < PAIRS else INTER
                    if prev and s == 0:
                        dve.wait_ge(y_ready, g)
                        x4 = X[:, span((g - 1) * GT, GT), :]
                        nc.vector.tensor_tensor(x4, x4, PS[:, Y_BANK, :].rearrange("p (t d) -> p t d", t=GT), ALU.add).then_inc(x2_ready, 1)
                    if cur:
                        dve.wait_ge(silu_done, n + 1)
                        dve.wait_ge(b_ready, n + 1)
                        need(dve, down_done, n - 1)
                        if s < PAIRS:
                            nc.vector.tensor_tensor(gated[:, buf, :], silu[:, buf, :], PS[:, B_BANK + buf, :], ALU.mult).then_inc(gated_done, 1)
                            dve.wait_ge(gated_done, g * PAIRS + s + 1)
                            nc.vector.tensor_tensor(hid[:, buf, :], gated[:, buf, :], PS[:, C_BANK + buf, :], ALU.mult).then_inc(hid_done, 1)
                        else:
                            nc.vector.tensor_tensor(hid[0:rows, buf, :], silu[0:rows, buf, :], PS[0:rows, B_BANK + buf, :], ALU.mult).then_inc(hid_done, 1)
                    if prev and s == 1:
                        dve.wait_ge(x2_ready, g)
                        norm_stats(dve, ln3, g - 1, tiles4(X, g - 1))
                    if prev and s == 2:
                        dve.wait_ge(ln3.aggr, GT * g)
                        root_guess(dve, ln3, g - 1, mv[:, 0:GT, :], rstd[:, 0:GT], var_eps[:, 0:GT], twice=True)
                        root_newton(dve, ln3, g - 1, 0, rstd[:, 0:GT], var_eps[:, 0:GT], root_t[:, 0:GT])
                    if prev and s == 3:
                        for i in range(1, NEWTON):
                            root_newton(dve, ln3, g - 1, i, rstd[:, 0:GT], var_eps[:, 0:GT], root_t[:, 0:GT])
            bodies(dve, experts0, NG)

            attention(Att(1), a1)

            dve.wait_ge(lg1_kept, NG + 1)
            at = [0]
            N1 = NT * E1
            v, above, equal, rank, first, second = (Pr[:, i // 2, (i % 2) * N1:(i % 2 + 1) * N1].rearrange("p (t e) -> p t e", e=E1) for i in range(6))
            place, rest = (Pr[:, 3, i * N1:(i + 1) * N1].rearrange("p (e t) -> p e t", e=E1) for i in range(2))
            run_t = PT[:, 0, 0:N1].rearrange("p (e t) -> p e t", e=E1)
            prod = PT[:, 0, N1:2 * N1].rearrange("p (t e) -> p t e", e=E1)
            many = PT[:, 1, 0:E1 * (TOK // ST)].rearrange("p (e s) -> p e s", e=E1)

            def step(instruction):
                chain(route_step, at, instruction)

            step(nc.vector.tensor_copy(v, LG[:, :, 0:E1]))
            choose(route_step, at, v, top8, E1, 2, above, equal, rank, reset1[:, :])
            best = top8[:, :, 0].unsqueeze(2).broadcast_to([P, NT, E1])
            step(nc.vector.tensor_tensor(equal, v, best, ALU.is_equal))
            step(nc.vector.tensor_tensor_scan(rank.rearrange("p t e -> p (t e)"), reset1[:, :], equal.rearrange("p t e -> p (t e)"), 0.0, ALU.mult, ALU.add))
            step(nc.vector.tensor_scalar(rank, rank, 1.0, None, ALU.is_le))
            step(nc.vector.tensor_tensor(first, equal, rank, ALU.mult))
            step(nc.vector.tensor_tensor(second, above, first, ALU.subtract))
            step(nc.vector.tensor_copy(chosenb[:, :, :].rearrange("p e t -> p t e"), above))
            nc.vector.tensor_tensor(left[:, :], top8[:, :, 1], top8[:, :, 0], ALU.subtract).then_inc(diff_ready, 1)
            dve.wait_ge(ranks_ready, 1)
            ahead = PS[:, 0, 0:N1].rearrange("p (e t) -> p e t", e=E1)
            totals = PS[:, 1, 0:N1]
            step(nc.vector.tensor_copy(rest.rearrange("p e t -> p (e t)"), totals))
            step(nc.vector.tensor_tensor_scan(run_t.rearrange("p e t -> p (e t)"), reset_t[:, :], rest.rearrange("p e t -> p (e t)"), 0.0, ALU.mult, ALU.add))
            step(nc.vector.tensor_tensor(place, run_t, rest, ALU.subtract))
            step(nc.vector.tensor_tensor(place, place, ahead, ALU.add))
            n_tok = run_t[:, :, NT - 1].unsqueeze(2).broadcast_to([P, E1, TOK // ST])
            step(nc.vector.tensor_tensor(many, n_tok, steps[:, :].unsqueeze(1).broadcast_to([P, E1, TOK // ST]), ALU.is_gt))
            step(nc.vector.tensor_reduce(count[:, 0, :], many, AX.X, ALU.add))
            step(nc.vector.memset(count[:, 3, :], 1.0))
            step(nc.vector.tensor_tensor_scan(count[:, 1, :], count[:, 3, :], count[:, 0, :], 0.0, ALU.mult, ALU.add))
            step(nc.vector.tensor_tensor(count[:, 2, :], count[:, 1, :], count[:, 0, :], ALU.subtract))
            step(nc.vector.tensor_scalar(count[:, 2, :], count[:, 2, :], float(ST), None, ALU.mult))
            step(nc.vector.tensor_tensor(place, place, count[:, 2, :].unsqueeze(2).broadcast_to([P, E1, NT]), ALU.add))
            for i, chosen in enumerate((first, second)):
                step(nc.vector.tensor_tensor(prod, chosen, place.rearrange("p e t -> p t e"), ALU.mult))
                step(nc.vector.tensor_reduce(slot_f[:, i, :], prod, AX.X, ALU.add))
                nc.vector.tensor_copy(slot[:, i, :], slot_f[:, i, :]).then_inc(slot_known, 1)
            own = PT[0:1, 1, 0:NST * E1].rearrange("p (k e) -> p k e", e=E1)
            step(nc.vector.tensor_tensor(own, count[0:1, 1, :].unsqueeze(1).broadcast_to([1, NST, E1]),
                                         tile_no[:, :].unsqueeze(2).broadcast_to([1, NST, E1]), ALU.is_le))
            owner = PT[0:1, 0, 0:NST]
            step(nc.vector.tensor_reduce(owner, own, AX.X, ALU.add))
            step(nc.vector.tensor_scalar(owner, owner, float(E1 - 1), None, ALU.min))
            nc.vector.tensor_copy(expert[:, :], owner).then_inc(slots_ready, 1)
            dve.wait_ge(exp_ready, 1)
            step(nc.vector.tensor_scalar(slot_f[:, 0, :], weight[:, 1, :], 1.0, None, ALU.add))
            step(nc.vector.reciprocal(weight[:, 0, :], slot_f[:, 0, :]))
            step(nc.vector.tensor_tensor(weight[:, 1, :], weight[:, 1, :], weight[:, 0, :], ALU.mult))

            def expert_tiles(k, par, older, prev, cur, nxt):
                if prev:
                    if not isinstance(k, int) or k >= 3:
                        dve.wait_ge(y_out[1 - par], 2 * sixteens(k - 3, 1 - par))
                    nc.vector.tensor_copy(rows_of[:, 1 - par, 1, :], rows_of[:, 1 - par, 0, :]).then_inc(rows_step, 1)
                if nxt:
                    dve.wait_ge(xsT_ready, k + 2)
                    if prev:
                        dve.wait_ge(rows_step, 2 * k + 1)
                    nc.vector.tensor_copy(rows_of[:, 1 - par, 0, :], xs[:, 1 - par, :, D].bitcast(I32)).then_inc(rows_step, 1)
                    need(dve, up_ready, k)
                    nc.vector.tensor_copy(xsT[:, 1 - par, :], PS[:, 4, 0:ST]).then_inc(xsT_kept, 1)
                if prev:
                    dve.wait_ge(down_ready, k)
                    nc.vector.tensor_tensor(ys[:, 1 - par, :, :], PS[:, 5 + (1 - par), 0:ST].rearrange("p (h d) -> p h d", d=D),
                                            w2[:, 1 - par, HID:HID + D].unsqueeze(1).broadcast_to([P, ST // P, D]), ALU.add).then_inc(y_kept, 1)
            bodies(dve, expert_tiles, NST, 3)

            for t in range(NT):
                if t % (2 * GT) == 0:
                    dve.wait_ge(results_in[t // (2 * GT)], 16)
                nc.vector.scalar_tensor_tensor(out=X[:, t, :], in0=got[t // GT][:, t % GT, 0, :], scalar=weight[:, 0, t:t + 1], in1=X[:, t, :],
                                               op0=ALU.mult, op1=ALU.add).then_inc(half_done, 1)
                if t >= 1:
                    dve.wait_ge(half_done, t)
                    nc.vector.scalar_tensor_tensor(out=X[:, t - 1, :], in0=got[(t - 1) // GT][:, (t - 1) % GT, 1, :], scalar=weight[:, 1, t - 1:t], in1=X[:, t - 1, :],
                                                   op0=ALU.mult, op1=ALU.add).then_inc(x4_ready, 1)
            dve.wait_ge(half_done, NT)
            nc.vector.scalar_tensor_tensor(out=X[:, NT - 1, :], in0=got[NG - 1][:, GT - 1, 1, :], scalar=weight[:, 1, NT - 1:NT], in1=X[:, NT - 1, :],
                                           op0=ALU.mult, op1=ALU.add).then_inc(x4_ready, 1)

        @block.scalar
        def _(act):
            act.wait_ge(mask_cut, 3)
            act.wait_ge(mask_fill, 1)
            for i in range(3):
                for b2 in range(2):
                    act.dma_start(mask_rows[MROW + 3 * b2 + i:MROW + 3 * b2 + i + 1, :].rearrange("o (t k) -> o t k", t=NT),
                                 mask_part[b2:B:2, i, :]).then_inc(mask_spread, 16)
            for g in range(NG):
                act.wait_ge(ln1_T, g + 1)
                nc.scalar.activation(XNT[:, g * GTOK:(g + 1) * GTOK], PS[:, g, :], ACT.Copy).then_inc(ln1_kept, 1)
            act.wait_ge(w_in, 16 * NW)
            act.wait_ge(bqs_ready, 1)

            def attention(L, a):
                def keep_k(g, par):
                    act.wait_ge(a.k_ready, g + 1)
                    if L.layer == 0:
                        nc.scalar.activation(KTb[:, par, :], PS[:, PJ, :], ACT.Identity, bias=cols[:, BK:BK + 1]).then_inc(a.k_kept, 1)
                    else:
                        nc.scalar.activation(KTb[:, par, :], PS[:, PJ, :], ACT.Copy).then_inc(a.k_kept, 1)

                def keep_q(g, par):
                    act.wait_ge(a.q_ready, g + 1)
                    if L.layer == 0:
                        nc.scalar.activation(QT[:, par, :], PS[:, PJ2, :], ACT.Identity, bias=bq_s[:, :], scale=L.scale).then_inc(a.q_kept, 1)
                    else:
                        nc.scalar.activation(QT[:, par, :], PS[:, PJ2, :], ACT.Copy, scale=L.scale).then_inc(a.q_kept, 1)

                def keep_v(g, par):
                    act.wait_ge(a.v_ready, g + 1)
                    need(act, a.pv, L.units * (g - 1))
                    for i in (1, 0):
                        for odd in range(2):
                            nc.scalar.activation(V2[:, par, 4 * i:4 * i + 4, :].rearrange("p b d -> p (b d)")
                                                 .rearrange("p (h o e) -> p o h e", o=2, e=L.dk)[:, odd],
                                                 PS[:, PJ + i, :].rearrange("p (h o e) -> p o h e", o=2, e=L.dk)[:, odd],
                                                 ACT.Copy, scale=side[:, odd:odd + 1]).then_inc(a.v_kept, 1)

                def exp(g, u):
                    n = g * L.units + u
                    act.wait_ge(a.shifted, n + 1)
                    nc.scalar.activation(Pr[:, u % 4, :], Pr[:, u % 4, :], ACT.Exp).then_inc(a.exped, 1)

                def keep_pt(g, u):
                    n = g * L.units + u
                    act.wait_ge(a.pt_ready, n + 1)
                    need(act, a.pv, n - 1)
                    nc.scalar.activation(PT[:, u % 2, :], PS[:, PT_BANK, :], ACT.Copy).then_inc(a.pt_kept, 1)

                def body(g, par, older, prev, cur, nxt):
                    for u in range(L.units):
                        if u + 1 < L.units:
                            if cur:
                                exp(g, u + 1)
                        elif nxt:
                            exp(g + 1, 0)
                        if cur:
                            keep_pt(g, u)
                        if L.layer == 1 and older and here(g - 2):
                            if u == 1:
                                act.wait_ge(onT_ready, g - 1)
                                nc.scalar.activation(onT[:, :], PS[:, LG_BANK, :], ACT.Copy).then_inc(onT_kept, 1)
                            if u == 2:
                                act.wait_ge(wo_ready, g - 1)
                                nc.scalar.activation(OTs[:, :], PS[:, LG_BANK, :], ACT.Gelu).then_inc(gelu_o, 1)
                        if L.layer == 1 and older and here(g - 3) and u == 3:
                            act.wait_ge(xe_T, g - 2)
                            nc.scalar.activation(xnT[:, :], PS[:, LG_BANK, :], ACT.Copy).then_inc(xe_T_kept, 1)
                            act.wait_ge(lg1_ready, g - 2)
                            nc.scalar.activation(LG[:, span((g - 3) * GT, GT), 0:E1],
                                                 PS[:, LG_BANK, 0:GT * E1].rearrange("p (t e) -> p t e", t=GT), ACT.Copy).then_inc(lg1_kept, 1)
                        if nxt and u == 0:
                            keep_k(g + 1, 1 - par)
                        if nxt and u == 0:
                            keep_q(g + 1, 1 - par)
                        if nxt and u == L.values_at + 1:
                            keep_v(g + 1, 1 - par)
                        if L.layer == 0 and prev and u == 2:
                            act.wait_ge(oT_ready, g)
                            nc.scalar.activation(OTs[:, :], PS[:, PJ2, :], ACT.Identity, bias=cols[:, BV:BV + 1]).then_inc(oT_kept, 1)
                        if L.layer == 0 and prev and u == 7:
                            act.wait_ge(x2T_ready, g)
                            if not cur:
                                act.wait_ge(x2T_spread, g - 1)
                            nc.scalar.activation(xnT[:, :], PS[:, PJ2, :], ACT.Copy).then_inc(x2T_kept, 1)
                bodies(act, body, NG, L.lag)

            attention(Att(0), a0)
            act.wait_ge(lg_kept, NG)
            act.wait_ge(a0.pt_ready, 8 * NG)
            nc.scalar.activation(Pr[:, 0, :], LG[:, :, :].rearrange("p t e -> p (t e)"), ACT.Sigmoid).then_inc(sig_done, 1)
            for i in range(4):
                act.wait_ge(combT_ready, i + 1)
                nc.scalar.activation(combT[:, i * 1024:(i + 1) * 1024], PS[0:3 * E0, 4 + i, :].bitcast(BF16), ACT.Copy).then_inc(combT_kept, 1)

            def experts0(g, par, older, prev, cur, nxt):
                def gate(g, s, buf):
                    n = g * ITEMS + s
                    rows = P if s < PAIRS else INTER
                    act.wait_ge(a_ready, n + 1)
                    nc.scalar.activation(silu[0:rows, buf, :], PS[0:rows, A_BANK + buf, :], ACT.Silu).then_inc(silu_done, 1)

                for s in range(ITEMS):
                    if s + 1 < ITEMS:
                        if cur:
                            gate(g, s + 1, (s + 1 + par) % 2)
                    elif nxt:
                        gate(g + 1, 0, (1 - par) % 2)
                    if prev and s == 5:
                        act.wait_ge(qT_ready, g)
                        nc.scalar.activation(XNT[:, span((g - 1) * GTOK, GTOK)], PS[:, T_BANK, :], ACT.Identity,
                                             bias=cols[:, PB:PB + 1], scale=cols[:, PG:PG + 1]).then_inc(qT_kept, 1)
                    if prev and s == 8:
                        act.wait_ge(kT_ready, g + 1)
                        nc.scalar.activation(KNT[:, span((g - 1) * GTOK, GTOK)], PS[:, T_BANK, :], ACT.Identity,
                                             bias=cols[:, PB:PB + 1], scale=cols[:, PG:PG + 1]).then_inc(kT_kept, 1)
            bodies(act, experts0, NG)
            act.sem_inc(lg1_kept, 1)
            attention(Att(1), a1)

            act.wait_ge(diff_ready, 1)
            nc.scalar.activation(weight[:, 1, :], left[:, :], ACT.Exp).then_inc(exp_ready, 1)

            def load_w1(k, buf):
                stand(act)
                e = nc.scalar.value_load(expert[0:1, span(k, 1)], min_val=0, max_val=E1 - 1)
                nc.scalar.dma_start(w1[:, buf, :], d["w1"][span(e, 1), :, :].rearrange("o p n -> (o p) n")).then_inc(w1_in[buf], 16)

            def load_w2(k, buf):
                stand(act)
                e = nc.scalar.value_load(expert[0:1, span(k, 1)], min_val=0, max_val=E1 - 1)
                nc.scalar.dma_start(w2[:, buf, :], d["w2"][span(e, 1), :, :].rearrange("o p n -> (o p) n")).then_inc(w2_in[buf], 16)

            act.wait_ge(slots_ready, 1)
            load_w1(0, 0)
            load_w1(1, 1)
            load_w2(0, 0)

            def expert_tiles(k, par, older, prev, cur, nxt):
                if cur:
                    act.wait_ge(up_ready, k + 1)
                    for c in range(CH):
                        nc.scalar.activation(hx[:, par, c, :], PS[:, 2 * par + c // 2, (c % 2) * ST:(c % 2 + 1) * ST], ACT.Gelu,
                                             bias=w1[:, par, HID + c:HID + c + 1]).then_inc(gelued, 1)
                    if not isinstance(k, int) or k + 2 < NST:
                        act.wait_ge(gelued, CH * (k + 1))
                        load_w1(k + 2, par)
                    if nxt:
                        need(act, y_kept, k)
                        load_w2(k + 1, 1 - par)
            bodies(act, expert_tiles, NST)

        @block.tensor
        def _(pe):
            pe.wait_ge(w_in, 16 * NW)

            def transpose4(bank, src, done):
                for j in range(GT):
                    last = nc.tensor.transpose(PS[:, bank, j * P:(j + 1) * P], src[:, j, :], ident[:, :])
                last.then_inc(done, 1)

            for g in range(NG):
                pe.wait_ge(ln1.done, GT * g + GT)
                transpose4(g, (xn, xm)[g % 2], ln1_T)
            pe.wait_ge(const_ready, 6)
            pe.wait_ge(ln1_kept, NG)

            def attention(L, a):
                w = w_att[L.layer]

                def make_k(g, par):
                    if L.layer == 0:
                        pe.wait_ge(a.ct_in, 16 * g + 16)
                        src = ctg[:, :]
                    else:
                        src = KNT[:, span(g * GTOK, GTOK)]
                    need(pe, a.v_kept, 4 * g)
                    nc.tensor.matmul(PS[:, PJ, :], w[:, 1, :], src, start=True, stop=True).then_inc(a.k_ready, 1)

                def make_q(g, par):
                    need(pe, a.v_kept, 4 * g)
                    nc.tensor.matmul(PS[:, PJ2, :], w[:, 0, :], XNT[:, span(g * GTOK, GTOK)], start=True, stop=True).then_inc(a.q_ready, 1)

                def make_v(g, par):
                    pe.wait_ge(a.k_kept, g + 1)
                    pe.wait_ge(a.q_kept, g + 1)
                    if L.layer == 0:
                        need(pe, x1_ready, g - 1)
                    pe.wait_ge(a.ct_in, 16 * g + 16)
                    for b in range(2 * GT):
                        for r in (0, S):
                            last = nc.tensor.matmul(PS[r:r + S, PJ + b // GT, b % GT * P:(b % GT + 1) * P], ctg[:, b * S:(b + 1) * S],
                                                    w[:, 2, :], start=True, stop=True)
                    last.then_inc(a.v_ready, 1)

                def scores(g, u, par):
                    n = g * L.units + u
                    j, part = u // L.parts, u % L.parts
                    if u == 0:
                        pe.wait_ge(a.q_kept, g + 1)
                    need(pe, a.shifted if L.layer == 0 else a.clipped, n - 1)
                    if part == 0:
                        pe.wait_ge(a.spread, 2 * (g * GT + j + 1))
                    bank = PS[:, S_BANKS + u % 2, :]
                    if L.layer == 0:
                        if isinstance(g, int) and g == 0 and u == 0:
                            pe.wait_ge(mask_fill, 1)
                            pe.wait_ge(mask_spread, 16 * MPARTS)
                        stand(pe)
                        m = mask_rows[:, span(g * GT * S + j * S, S)]
                        nc.tensor.matmul(bank.rearrange("p (h k) -> p h k", h=8), win_ub[:, :],
                                         m.unsqueeze(1).broadcast_to([P, 8, S]), start=True, stop=False, skip_group_check=True)
                    for b2 in range(2):
                        last = nc.tensor.matmul(PS[64 * b2:64 * b2 + 64, S_BANKS + u % 2, :], QT[:, par, (2 * j + b2) * S:(2 * j + b2 + 1) * S],
                                                key_blocks(L, j)[:, b2, 8 * part:8 * part + 8, :],
                                                start=L.layer == 1, stop=True, skip_group_check=True)
                    last.then_inc(a.scores, 1)

                def turn(g, u):
                    n = g * L.units + u
                    pe.wait_ge(a.exped, n + 1)
                    need(pe, a.pt_kept, n)
                    for i in range(4):
                        last = nc.tensor.transpose(PS[:, PT_BANK, i * P:(i + 1) * P], Pr[:, u % 4, i * P:(i + 1) * P], ident[:, :])
                    last.then_inc(a.pt_ready, 1)

                def weigh(g, u, par):
                    n = g * L.units + u
                    j, part = u // L.parts, u % L.parts
                    if u == 0:
                        pe.wait_ge(a.v_kept, 4 * g + 4)
                        if L.layer == 1 or isinstance(g, int):
                            need(pe, a.o_kept, g - 1)
                    pe.wait_ge(a.pt_kept, n + 1)
                    stand(pe)
                    for i in range(4):
                        for r in range(4):
                            o = j * P + (4 * part + i) * 2 * L.dk
                            last = nc.tensor.matmul(PS[32 * r:32 * r + 32, O_BANKS + par, o:o + 2 * L.dk],
                                                    PT[:, u % 2, i * P + 32 * r:i * P + 32 * r + 32],
                                                    V2[:, par, 2 * j + r // 2, o - j * P:o - j * P + 2 * L.dk], start=True, stop=True)
                    last.then_inc(a.pv, 1)

                def body(g, par, older, prev, cur, nxt):
                    for u in range(L.units):
                        if u + 2 < L.units:
                            if cur:
                                scores(g, u + 2, par)
                        elif nxt:
                            scores(g + 1, u + 2 - L.units, 1 - par)
                        if L.layer == 0 and prev and u == 7:
                            pe.wait_ge(ln2.done, GT * g)
                            if nxt:
                                pe.wait_ge(a.v_kept, 4 * (g + 2))
                            transpose4(PJ2, xn, x2T_ready)
                        if cur:
                            turn(g, u)
                        if u >= 1:
                            if cur:
                                weigh(g, u - 1, par)
                        elif prev:
                            weigh(g - 1, L.units - 1, 1 - par)
                        if nxt and u == L.values_at:
                            make_v(g + 1, 1 - par)
                        if L.layer == 0 and prev and u == 2:
                            pe.wait_ge(a.o_kept, g)
                            if nxt:
                                pe.wait_ge(a.q_kept, g + 2)
                            transpose4(PJ2, xm, oT_ready)
                        if L.layer == 0 and prev and u == 3:
                            pe.wait_ge(oT_kept, g)
                            if nxt:
                                pe.wait_ge(a.k_kept, g + 2)
                            for j in range(GT):
                                nc.tensor.matmul(PS[:, PJ, j * P:(j + 1) * P], ones_row[:, :], bo_row[:, :], start=True, stop=False, skip_group_check=True)
                                last = nc.tensor.matmul(PS[:, PJ, j * P:(j + 1) * P], OTs[:, j * P:(j + 1) * P], w[:, 3, :], start=False, stop=True, skip_group_check=True)
                            last.then_inc(proj_ready, 1)
                        if L.layer == 1 and older and here(g - 2):
                            if u == 0:
                                pe.wait_ge(on_ready, g - 1)
                                pe.wait_ge(lg1_kept, max(g - 2, 1) if isinstance(g, int) else g - 2)
                                transpose4(LG_BANK, on[:, par, :, :], onT_ready)
                            if u == 1:
                                pe.wait_ge(onT_kept, g - 1)
                                for j in range(GT):
                                    last = nc.tensor.matmul(PS[:, LG_BANK, j * P:(j + 1) * P], onT[:, j * P:(j + 1) * P], w[:, 3, :], start=True, stop=True)
                                last.then_inc(wo_ready, 1)
                        if L.layer == 1 and older and here(g - 3):
                            if u == 2:
                                if here(g - 2):
                                    pe.wait_ge(gelu_o, g - 1)
                                else:
                                    pe.wait_ge(lg1_kept, g - 2)
                                pe.wait_ge(xe_normed, g - 2)
                                transpose4(LG_BANK, xm, xe_T)
                            if u == 3:
                                pe.wait_ge(xe_T_kept, g - 2)
                                for j in range(GT):
                                    last = nc.tensor.matmul(PS[:, LG_BANK, j * E1:(j + 1) * E1], xnT[:, j * P:(j + 1) * P], wr[:, :], start=True, stop=True)
                                last.then_inc(lg1_ready, 1)
                        if L.layer == 0 and prev and u == 7:
                            pe.wait_ge(x2T_kept, g)
                            for j in range(GT):
                                last = nc.tensor.matmul(PS[:, LG_BANK, j * E0:(j + 1) * E0], xnT[:, j * P:(j + 1) * P], gw[:, :], start=True, stop=True)
                            last.then_inc(lg_ready, 1)
                        if nxt and u == 0:
                            make_k(g + 1, 1 - par)
                            make_q(g + 1, 1 - par)
                bodies(pe, body, NG, L.lag)

            attention(Att(0), a0)

            pe.wait_ge(comb_ready, 1)
            pe.wait_ge(lg_kept, NG)
            for t in range(NT):
                last = nc.tensor.transpose(PS[0:3 * E0, 4 + t // 8, (t % 8) * 64:(t % 8 + 1) * 64].bitcast(BF16), comb3[:, t, :], identb[:, :])
                if t % 8 == 7:
                    last.then_inc(combT_ready, 1)
            pe.wait_ge(w_split, 4)

            def experts0(g, par, older, prev, cur, nxt):
                def wide(bank, i, s, cols_, buf_x):
                    high, low = (w[i][:, s * P:s * P + cols_] for w in (w_high, w_low))
                    xh, xl = (x_parts[:, buf_x, k, :] for k in range(2))
                    nc.tensor.matmul(bank, low, xh, start=True, stop=False)
                    nc.tensor.matmul(bank, high, xl, start=False, stop=False)
                    return nc.tensor.matmul(bank, high, xh, start=False, stop=True)

                def up(g, s, buf, buf_x):
                    n = g * ITEMS + s
                    cols_ = P if s < PAIRS else INTER
                    if s == 0:
                        pe.wait_ge(x_split, g + 1)
                    need(pe, silu_done, n - 1)
                    need(pe, hid_done, n - 1)
                    wide(PS[0:cols_, A_BANK + buf, :], 0, s, cols_, buf_x).then_inc(a_ready, 1)
                    if s == 0 and isinstance(g, int) and g == 0:
                        pe.wait_ge(combT_kept, 4)
                    if s < PAIRS:
                        nc.tensor.matmul(PS[:, C_BANK + buf, :], sel3[:, s * P:(s + 1) * P], combT[:, span(g * GTOK, GTOK)], start=True, stop=True)
                    wide(PS[0:cols_, B_BANK + buf, :], 1, s, cols_, buf_x).then_inc(b_ready, 1)

                def down(g, s, buf):
                    n = g * ITEMS + s
                    rows = P if s < PAIRS else INTER
                    pe.wait_ge(hid_done, n + 1)
                    if s == 0:
                        need(pe, x2_ready, g)
                    for j in range(GT):
                        last = nc.tensor.matmul(PS[:, Y_BANK, j * P:(j + 1) * P], hid[0:rows, buf, j * P:(j + 1) * P], w_down[0:rows, s, :],
                                                start=(s == 0 and j == 0), stop=(s == PAIRS), skip_group_check=True)
                    last.then_inc(down_done, 1)
                    if s == PAIRS:
                        pe.wait_ge(down_done, n + 1)
                        pe.sem_inc(y_ready, 1)

                for s in range(ITEMS):
                    if s + 1 < ITEMS:
                        if cur:
                            up(g, s + 1, (s + 1 + par) % 2, par)
                    elif nxt:
                        up(g + 1, 0, 1 - par, 1 - par)
                    if cur:
                        down(g, s, (s + par) % 2)
                    if prev and s == 5:
                        pe.wait_ge(q_normed, g)
                        if not cur:
                            pe.wait_ge(kT_kept, g - 1)
                        transpose4(T_BANK, xn, qT_ready)
                    if prev and s == 8:
                        pe.wait_ge(k_normed, g)
                        pe.wait_ge(qT_kept, g)
                        transpose4(T_BANK, xm, kT_ready)
            pe.sem_inc(kT_ready, 1)
            bodies(pe, experts0, NG)
            pe.wait_ge(qT_kept, NG)
            pe.wait_ge(kT_kept, NG)
            pe.wait_ge(x2_ready, NG)
            attention(Att(1), a1)
            pe.wait_ge(diff_ready, 1)
            pe.wait_ge(lg1_kept, NG + 1)
            flat = chosenb[:, :, :].rearrange("p e t -> p (e t)")
            nc.tensor.matmul(PS[:, 0, 0:NT * E1], beforeb[:, :], flat, start=True, stop=True)
            nc.tensor.matmul(PS[:, 1, 0:NT * E1], onesb[:, :], flat, start=True, stop=True).then_inc(ranks_ready, 1)
            pe.wait_ge(slots_ready, 1)

            def expert_tiles(k, par, older, prev, cur, nxt):
                if cur:
                    pe.wait_ge(xsT_kept, k + 1)
                    pe.wait_ge(w1_in[par], sixteens(k, par))
                    for c in range(CH):
                        last = nc.tensor.matmul(PS[:, 2 * par + c // 2, (c % 2) * ST:(c % 2 + 1) * ST],
                                                w1[:, par, c * P:(c + 1) * P], xsT[:, par, :], start=True, stop=True)
                    last.then_inc(up_ready, 1)
                if nxt:
                    pe.wait_ge(xs_in[1 - par], sixteens(k + 1, 1 - par))
                    need(pe, xsT_kept, k + 1)
                    for h in range(ST // P):
                        last = nc.tensor.transpose(PS[:, 4, h * P:(h + 1) * P], xs[:, 1 - par, h, 0:D], ident[:, :])
                    last.then_inc(xsT_ready, 1)
                if prev:
                    pe.wait_ge(gelued, CH * k)
                    pe.wait_ge(w2_in[1 - par], sixteens(k - 1, 1 - par))
                    if not cur:
                        pe.wait_ge(y_kept, k - 2)
                    for h in range(ST // P):
                        for c in range(CH):
                            last = nc.tensor.matmul(PS[:, 5 + (1 - par), h * P:(h + 1) * P], hx[:, 1 - par, c, h * P:(h + 1) * P],
                                                    w2[:, 1 - par, c * P:(c + 1) * P], start=(c == 0), stop=(c == CH - 1))
                    last.then_inc(down_ready, 1)
            bodies(pe, expert_tiles, NST)


def kernel(**inputs):
    import numpy as _np
    import concourse.bacc as _bacc
    from concourse import mybir as _mybir
    from concourse.bass_utils import run_bass_kernel_spmd as _run

    def f(name):
        return _np.asarray(inputs[name])

    arrays = {
        "x": f("x").reshape(TOK, D),
        "ctx": f("ctx_1024").reshape(TOK, D),
        "ctxT": f("ctx_1024").reshape(TOK, D).T,
        "mask": f("mask_BxS2_ff0"),
        "L0_wq": f("L0_xattn_wq"), "L0_wk": f("L0_xattn_wk"), "L0_wv": f("L0_xattn_wv"), "L0_wo": f("L0_xattn_wo"),
        "L0_bq": f("L0_xattn_bq")[:, None], "L0_bk": f("L0_xattn_bk")[:, None], "L0_bv": f("L0_xattn_bv")[:, None],
        "L0_bo": f("L0_xattn_bo")[None, :],
        "pre_g": f("L1_xattn_pre_g")[:, None], "pre_b": f("L1_xattn_pre_b")[:, None],
        "gate_w": f("L0_ffn_gate_w").T,
        "gate_b": _np.broadcast_to(f("L0_ffn_gate_b"), (P, E0)),
        "L1_Wq": f("L1_xattn_Wq"), "L1_Wk": f("L1_xattn_Wk"), "L1_Wv": f("L1_xattn_Wv"), "L1_Wo": f("L1_xattn_Wo"),
        "ln_gb": _np.broadcast_to(_np.stack([f("L1_xattn_ln_g"), f("L1_xattn_ln_b")]), (P, 2, D)),
        "w_gate": _np.concatenate([f("L0_ffn_w13")[:, :INTER], f("L0_ffn_w13_s")[None, :INTER]]).transpose(2, 0, 1).reshape(D, -1),
        "w_up": _np.concatenate([f("L0_ffn_w13")[:, INTER:], f("L0_ffn_w13_s")[None, INTER:]]).transpose(2, 0, 1).reshape(D, -1),
        "w_down": _np.concatenate([f("L0_ffn_w2"), f("L0_ffn_w2_s")[None], _np.zeros((1, D, INTER), _np.float32)])
                     .reshape(ITEMS, 2, D, INTER).transpose(1, 3, 0, 2).reshape(P, ITEMS, D),
        "Wr": f("L1_ffn_Wr"),
        "w1": _np.concatenate([f("L1_ffn_W1"), f("L1_ffn_b1").reshape(E1, CH, P).transpose(0, 2, 1)], 2),
        "w2": _np.concatenate([f("L1_ffn_W2").reshape(E1, CH, P, D).transpose(0, 2, 1, 3).reshape(E1, P, CH * D),
                               _np.broadcast_to(f("L1_ffn_b2")[:, None, :], (E1, P, D))], 2),
        **constants(),
    }
    nc = _bacc.Bacc("TRN2", target_bir_lowering=False, num_devices=1)
    aps, given = {}, {}
    for name, a in arrays.items():
        a = _np.ascontiguousarray(a)
        given[f"in_{name}"] = a
        aps[name] = nc.dram_tensor(f"in_{name}", a.shape, _mybir.dt.from_np(a.dtype), kind="ExternalInput").ap()
    out = nc.dram_tensor("out_x", (TOK, D), F32, kind="ExternalOutput").ap()
    program(nc, aps, out)
    r = _run(nc, [given], core_ids=[0])
    return r.results[0]["out_x"].reshape(B, S, D)
```
